# Optimizing a Trainium2 kernel written in Bass

```python
import numpy as np
import jax
import jax.numpy as jnp

def _softmax(x, axis=-1):
    return jax.nn.softmax(x, axis=axis)

def _gelu(x):
    return jax.nn.gelu(x, approximate=True)

def _silu(x):
    return jax.nn.silu(x)

def _sigmoid(x):
    return jax.nn.sigmoid(x)

def _layernorm(x, axis=-1, eps=1e-05):
    m = jnp.mean(x, axis=axis, keepdims=True)
    v = jnp.var(x, axis=axis, keepdims=True)
    return (x - m) / jnp.sqrt(v + eps)

def _scatter_add(tgt, idx, src, axis=0):
    return tgt.at[idx].add(src)

def _segment_sum(src, seg, n):
    return jax.ops.segment_sum(src, seg, n)
kernel_name = 'mk_macaron_d1_jaxref_r8_8dfdd7'

def setup_inputs(seed: int=0):
    np.random.seed(seed)
    _w = jnp.asarray

    def _L0_attn_setup():
        import jax, jax.numpy as jnp
        import numpy as np
        D_MODEL = 256
        N_HEADS = 16
        N_KV_HEADS = 4
        HEAD_DIM = D_MODEL // N_HEADS
        ROPE_BASE = 10000.0

        def _rope_tables(T, head_dim):
            half = head_dim // 2
            theta = 1.0 / ROPE_BASE ** (jnp.arange(half, dtype=jnp.float32) / half)
            m = jnp.arange(T, dtype=jnp.float32)
            freqs = jnp.outer(m, theta)
            return (jnp.cos(freqs), jnp.sin(freqs))

        def _apply_rope(x, cos, sin):
            half = x.shape[-1] // 2
            x1, x2 = (x[..., :half], x[..., half:])
            cos = cos[None, None, :, :]
            sin = sin[None, None, :, :]
            return jnp.concatenate([x1 * cos - x2 * sin, x1 * sin + x2 * cos], axis=-1)
        key = jax.random.key(seed)
        ks = jax.random.split(key, 5)
        B, T = (4, 256)
        x = jax.random.normal(ks[0], (B, T, D_MODEL), dtype=jnp.float32)
        Wq = jax.random.normal(ks[1], (D_MODEL, N_HEADS * HEAD_DIM), dtype=jnp.float32) * 0.02
        Wk = jax.random.normal(ks[2], (D_MODEL, N_KV_HEADS * HEAD_DIM), dtype=jnp.float32) * 0.02
        Wv = jax.random.normal(ks[3], (D_MODEL, N_KV_HEADS * HEAD_DIM), dtype=jnp.float32) * 0.02
        Wo = jax.random.normal(ks[4], (N_HEADS * HEAD_DIM, D_MODEL), dtype=jnp.float32) * (0.02 / np.sqrt(2.0))
        return {'x': x, 'Wq': Wq, 'Wk': Wk, 'Wv': Wv, 'Wo': Wo}
    _L0_attn_in = _L0_attn_setup()

    def _L0_ffn_setup():
        import jax, jax.numpy as jnp
        import numpy as np
        import math
        D_MODEL = 256
        D_FF = 1024
        NUM_EXPERTS = 8
        TOP_K = 2
        CAPACITY_FACTOR = 1.25
        BATCH, SEQ = (4, 256)

        def _moe_forward(x, Wg, w1, w2):
            B, T, d = x.shape
            S = B * T
            E, K = (NUM_EXPERTS, TOP_K)
            C = math.ceil(CAPACITY_FACTOR * S * K / E)
            xr = x.reshape(S, d)
            probs = jax.nn.softmax(xr @ Wg, axis=-1)
            gate_vals, expert_idx = jax.lax.top_k(probs, K)
            flat_e = expert_idx.reshape(-1)
            oh = jax.nn.one_hot(flat_e, E, dtype=jnp.int32)
            pos = jnp.sum((jnp.cumsum(oh, axis=0) - 1) * oh, axis=1)
            kept = pos < C
            i = jnp.arange(S * K)
            slot = i % K * S + i // K
            sentinel = S * K
            pos_w = jnp.where(kept, pos, C)
            dispatch_mask = jnp.full((E, C), sentinel, dtype=jnp.int32)
            dispatch_mask = dispatch_mask.at[flat_e, pos_w].set(slot.astype(jnp.int32), mode='drop')
            combine_weights = (gate_vals * kept.reshape(S, K)).T
            dispatched = xr[dispatch_mask.reshape(-1) % S].reshape(E, C, d)
            h = jax.nn.relu(jnp.einsum('ecd,edf->ecf', dispatched, w1))
            expert_out = jnp.einsum('ecf,efd->ecd', h, w2)
            rerouted = jnp.zeros((S * K + 1, d), dtype=expert_out.dtype)
            rerouted = rerouted.at[dispatch_mask.reshape(-1)].set(expert_out.reshape(-1, d))
            rerouted = rerouted[:-1].reshape(K, S, d)
            out = jnp.einsum('ks,ksm->sm', combine_weights, rerouted)
            return out.reshape(B, T, d)
        key = jax.random.key(seed)
        k1, k2, k3, k4 = jax.random.split(key, 4)
        x = jax.random.normal(k1, (BATCH, SEQ, D_MODEL), dtype=jnp.float32)
        Wg = jax.random.normal(k2, (D_MODEL, NUM_EXPERTS), dtype=jnp.float32) * 0.02
        w1 = jax.random.normal(k3, (NUM_EXPERTS, D_MODEL, D_FF), dtype=jnp.float32) * 0.02
        w2 = jax.random.normal(k4, (NUM_EXPERTS, D_FF, D_MODEL), dtype=jnp.float32) * 0.02
        return {'x': x, 'Wg': Wg, 'w1': w1, 'w2': w2}
    _L0_ffn_in = _L0_ffn_setup()
    _d = {'L0_attn_x': _L0_attn_in['x'], 'L0_attn_Wq': _L0_attn_in['Wq'], 'L0_attn_Wk': _L0_attn_in['Wk'], 'L0_attn_Wv': _L0_attn_in['Wv'], 'L0_attn_Wo': _L0_attn_in['Wo'], 'L0_ffn_Wg': _L0_ffn_in['Wg'], 'L0_ffn_w1': _L0_ffn_in['w1'], 'L0_ffn_w2': _L0_ffn_in['w2']}
    _x0 = _d['L0_attn_x']
    _d['L0_attn_x'] = jax.random.normal(jax.random.fold_in(jax.random.key(seed), 1), (2, 1024, 256), dtype=_x0.dtype)
    del _x0
    return _d

def reference(L0_attn_x, L0_attn_Wq, L0_attn_Wk, L0_attn_Wv, L0_attn_Wo, L0_ffn_Wg, L0_ffn_w1, L0_ffn_w2):

    def _L0_attn_ref(x, Wq, Wk, Wv, Wo):
        import jax, jax.numpy as jnp
        import numpy as np
        D_MODEL = 256
        N_HEADS = 16
        N_KV_HEADS = 4
        HEAD_DIM = D_MODEL // N_HEADS
        ROPE_BASE = 10000.0

        def _rope_tables(T, head_dim):
            half = head_dim // 2
            theta = 1.0 / ROPE_BASE ** (jnp.arange(half, dtype=jnp.float32) / half)
            m = jnp.arange(T, dtype=jnp.float32)
            freqs = jnp.outer(m, theta)
            return (jnp.cos(freqs), jnp.sin(freqs))

        def _apply_rope(x, cos, sin):
            half = x.shape[-1] // 2
            x1, x2 = (x[..., :half], x[..., half:])
            cos = cos[None, None, :, :]
            sin = sin[None, None, :, :]
            return jnp.concatenate([x1 * cos - x2 * sin, x1 * sin + x2 * cos], axis=-1)
        B, T, C = x.shape
        groups = N_HEADS // N_KV_HEADS
        q = (x @ Wq).reshape(B, T, N_HEADS, HEAD_DIM).transpose(0, 2, 1, 3)
        k = (x @ Wk).reshape(B, T, N_KV_HEADS, HEAD_DIM).transpose(0, 2, 1, 3)
        v = (x @ Wv).reshape(B, T, N_KV_HEADS, HEAD_DIM).transpose(0, 2, 1, 3)
        cos, sin = _rope_tables(T, HEAD_DIM)
        q = _apply_rope(q, cos, sin)
        k = _apply_rope(k, cos, sin)
        k = jnp.repeat(k, groups, axis=1)
        v = jnp.repeat(v, groups, axis=1)
        scale = 1.0 / np.sqrt(HEAD_DIM)
        scores = jnp.einsum('bhqd,bhkd->bhqk', q, k) * scale
        pos = jnp.arange(T)
        dist = jnp.minimum(pos[None, :] - pos[:, None], 0).astype(jnp.float32)
        slopes = 2.0 ** (-8.0 * jnp.arange(1, N_HEADS + 1, dtype=jnp.float32) / N_HEADS)
        alibi = slopes[:, None, None] * dist[None, :, :]
        scores = scores + alibi[None]
        causal = pos[None, :] > pos[:, None]
        scores = jnp.where(causal[None, None], -jnp.inf, scores)
        weights = jax.nn.softmax(scores, axis=-1)
        out = jnp.einsum('bhqk,bhkd->bhqd', weights, v)
        out = out.transpose(0, 2, 1, 3).reshape(B, T, N_HEADS * HEAD_DIM)
        return out @ Wo

    def _L0_ffn_ref(x, Wg, w1, w2):
        import jax, jax.numpy as jnp
        import numpy as np
        import math
        D_MODEL = 256
        D_FF = 1024
        NUM_EXPERTS = 8
        TOP_K = 2
        CAPACITY_FACTOR = 1.25
        BATCH, SEQ = (4, 256)

        def _moe_forward(x, Wg, w1, w2):
            B, T, d = x.shape
            S = B * T
            E, K = (NUM_EXPERTS, TOP_K)
            C = math.ceil(CAPACITY_FACTOR * S * K / E)
            xr = x.reshape(S, d)
            probs = jax.nn.softmax(xr @ Wg, axis=-1)
            gate_vals, expert_idx = jax.lax.top_k(probs, K)
            flat_e = expert_idx.reshape(-1)
            oh = jax.nn.one_hot(flat_e, E, dtype=jnp.int32)
            pos = jnp.sum((jnp.cumsum(oh, axis=0) - 1) * oh, axis=1)
            kept = pos < C
            i = jnp.arange(S * K)
            slot = i % K * S + i // K
            sentinel = S * K
            pos_w = jnp.where(kept, pos, C)
            dispatch_mask = jnp.full((E, C), sentinel, dtype=jnp.int32)
            dispatch_mask = dispatch_mask.at[flat_e, pos_w].set(slot.astype(jnp.int32), mode='drop')
            combine_weights = (gate_vals * kept.reshape(S, K)).T
            dispatched = xr[dispatch_mask.reshape(-1) % S].reshape(E, C, d)
            h = jax.nn.relu(jnp.einsum('ecd,edf->ecf', dispatched, w1))
            expert_out = jnp.einsum('ecf,efd->ecd', h, w2)
            rerouted = jnp.zeros((S * K + 1, d), dtype=expert_out.dtype)
            rerouted = rerouted.at[dispatch_mask.reshape(-1)].set(expert_out.reshape(-1, d))
            rerouted = rerouted[:-1].reshape(K, S, d)
            out = jnp.einsum('ks,ksm->sm', combine_weights, rerouted)
            return out.reshape(B, T, d)
        return _moe_forward(x, Wg, w1, w2)
    x = L0_attn_x
    x = x + 0.5 * _L0_ffn_ref(_layernorm(x, axis=-1), L0_ffn_Wg, L0_ffn_w1, L0_ffn_w2)
    x = x + _L0_attn_ref(_layernorm(x, axis=-1), L0_attn_Wq, L0_attn_Wk, L0_attn_Wv, L0_attn_Wo)
    x = x + 0.5 * _L0_ffn_ref(_layernorm(x, axis=-1), L0_ffn_Wg, L0_ffn_w1, L0_ffn_w2)
    return x

_drawn_inputs = setup_inputs


def setup_inputs(seed=0):
    import zlib

    import numpy as np

    out = dict(_drawn_inputs(seed))
    spreads = {}
    factors = {'L0_attn_Wq': 8.0, 'L0_attn_Wk': 8.0, 'L0_attn_Wv': 2.774, 'L0_attn_Wo': 2.782}
    for name, (base, spread) in spreads.items():
        noise = np.random.default_rng([zlib.crc32(name.encode()), seed]).standard_normal(out[name].shape)
        drawn = base * np.exp(spread * noise) if base else spread * noise
        out[name] = jnp.asarray(drawn.astype(out[name].dtype))
    for name, factor in factors.items():
        out[name] = (out[name] * factor).astype(out[name].dtype)
    return out
```

```python
from contextlib import ExitStack

import numpy as np

import concourse.bass as bass
from concourse import mybir

F32 = mybir.dt.float32
F32R = mybir.dt.float32r
BF16 = mybir.dt.bfloat16
U32 = mybir.dt.uint32
ALU = mybir.AluOpType
ACT = mybir.ActivationFunctionType
AX = mybir.AxisListType

P = 128
BATCH, SEQ, D = 2, 1024, 256
TOKENS = BATCH * SEQ
TILES = TOKENS // P
KD = D // P
EXPERTS, TOPK, DFF = 8, 2, 1024
CAP = -(-5 * TOKENS * TOPK // (4 * EXPERTS))
SLOTS = EXPERTS * CAP
ROWTILES = CAP // P
KF = DFF // P
HALFCAP = CAP // 2
EPS = 1e-5
BANK = 512
HEADS, KV_HEADS, HD = 16, 4, 16
HALF = HD // 2
GROUP = HEADS // KV_HEADS
NEG = -1e30


def normalise(dve, step, X, stats, mv, veps, sd, rstd, nwt, xn, s_var, s_sd, s_xn):
    for t in range(TILES):
        step(dve.bn_stats(stats[:, t, :], X[:, t, :]), t == TILES - 1)
    for t in range(TILES):
        step(dve.bn_aggr(mv[:, t, :], stats[:, t, :]), t == TILES - 1)
    dve.tensor_scalar(veps[:, :], mv[:, :, 1], EPS, None, ALU.add).then_inc(s_var, 1)
    dve.wait_ge(s_var, 1)
    step(dve.tensor_scalar(nwt[:, :], veps[:, :], -0.5, None, ALU.mult), False)
    dve.wait_ge(s_sd, 1)
    step(dve.reciprocal(rstd[:, :], sd[:, :]))
    step(dve.tensor_tensor(sd[:, :], rstd[:, :], rstd[:, :], ALU.mult))
    step(dve.tensor_tensor(sd[:, :], sd[:, :], nwt[:, :], ALU.mult))
    step(dve.scalar_tensor_tensor(rstd[:, :], sd[:, :], 1.5, rstd[:, :], ALU.add, ALU.mult))
    for t in range(TILES):
        dve.tensor_scalar(xn[:, t, :], X[:, t, :], mv[:, t, 0:1], rstd[:, t:t + 1],
                          ALU.subtract, ALU.mult).then_inc(s_xn, 1)


def ffn(nc, X, x_dram, Wg, w1, w2, Xd, Y, consts, out_dram, tag):
    first = x_dram is not None
    with ExitStack() as ctx:
        def sb(name, shape, dt):
            return ctx.enter_context(nc.sbuf_tensor(f"{name}_{tag}", shape, dt))

        def ps(name, shape, dt=F32):
            return ctx.enter_context(nc.psum_tensor(f"{name}_{tag}", shape, dt))

        def sem(name):
            return ctx.enter_context(nc.semaphore(f"{name}_{tag}"))

        identf = sb("identf", [P, P], F32)
        before = sb("before", [P, P], BF16)
        onesb = sb("onesb", [P, P], BF16)
        iota = sb("iota", [P, TILES, EXPERTS], F32)
        restart = sb("restart", [P, EXPERTS * TILES], F32)
        wg = sb("wg", [P, KD, EXPERTS], F32)
        xn = sb("xn", [P, TILES, D], F32)
        stats = sb("stats", [P, TILES, 6], F32)
        mv = sb("mv", [P, TILES, 2], F32)
        veps = sb("veps", [P, TILES], F32)
        sd = sb("sd", [P, TILES], F32)
        rstd = sb("rstd", [P, TILES], F32)
        nwt = sb("nwt", [P, TILES], F32)
        xt = sb("xt", [P, 2, D], F32)
        logits = sb("logits", [P, TILES, EXPERTS], F32)
        top = sb("top", [P, TILES, 8], F32)
        topi = sb("topi", [P, TILES, 8], U32)
        shifted = sb("shifted", [P, TILES, EXPERTS], F32)
        exps = sb("exps", [P, TILES, EXPERTS], F32)
        gap = sb("gap", [P, TILES], F32)
        egap = sb("egap", [P, TILES], F32)
        zsum = sb("zsum", [P, TILES], F32)
        gates = sb("gates", [P, TOPK, TILES], F32)
        expert = sb("expert", [P, TOPK, TILES], F32)
        onehot = sb("onehot", [P, TOPK, TILES, EXPERTS], F32)
        count = sb("count", [P, EXPERTS, TILES], F32)
        countb = sb("countb", [P, EXPERTS * TILES], BF16)
        upto = sb("upto", [P, EXPERTS * TILES], F32)
        priorb = sb("priorb", [P, EXPERTS * TILES], BF16)
        picked = sb("picked", [P, TOPK, TILES, EXPERTS], F32)
        pos = sb("pos", [P, TOPK, TILES], F32)
        keep = sb("keep", [P, TOPK, TILES], F32)
        slotf = sb("slotf", [P, TOPK, TILES], F32)
        slot = sb("slot", [P, TOPK, TILES], U32)
        w1raw = sb("w1raw", [P, KD, DFF], F32)
        w2raw = sb("w2raw", [P, KF, D], F32)
        w1hi = sb("w1hi", [P, KD, DFF], F32R)
        w1lo = sb("w1lo", [P, KD, DFF], F32R)
        w2hi = sb("w2hi", [P, KF, D], F32R)
        w2lo = sb("w2lo", [P, KF, D], F32R)
        xe = sb("xe", [P, ROWTILES, D], F32)
        xthi = sb("xthi", [P, KD, CAP], F32R)
        xtlo = sb("xtlo", [P, KD, CAP], F32R)
        hhi = sb("hhi", [P, KF, CAP], F32R)
        hlo = sb("hlo", [P, KF, CAP], F32R)
        ysb = sb("ysb", [P, ROWTILES, D], F32)
        GR = 4
        picks = sb("picks", [P, GR, TOPK, D], F32)
        half = sb("half", [P, 2, D], F32)

        up = [ps(f"up{i}", [P, 2, BANK]) for i in range(2)]
        turn = ps("turn", [P, 2 * BANK])
        down = [ps(f"down{i}", [P, BANK]) for i in range(2)]

        s_const = sem("s_const")
        s_x = sem("s_x")
        s_zero = sem("s_zero")
        s_zeroed = sem("s_zeroed")
        s_vec = sem("s_vec")
        s_var = sem("s_var")
        s_sd = sem("s_sd")
        s_xn = sem("s_xn")
        s_rt = sem("s_rt")
        s_xt = sem("s_xt")
        s_gate = sem("s_gate")
        s_shift = sem("s_shift")
        s_exp = sem("s_exp")
        s_count = sem("s_count")
        s_pos = sem("s_pos")
        s_slot = sem("s_slot")
        s_scat = sem("s_scat")
        w1_in = sem("w1_in")
        w2_in = sem("w2_in")
        xe_in = sem("xe_in")
        w1hi_ok = sem("w1hi_ok")
        w1lo_ok = sem("w1lo_ok")
        w2hi_ok = sem("w2hi_ok")
        w2lo_ok = sem("w2lo_ok")
        turned = sem("turned")
        xthi_ok = sem("xthi_ok")
        xtlo_ok = sem("xtlo_ok")
        up_ok = sem("up_ok")
        hhi_ok = sem("hhi_ok")
        hlo_ok = sem("hlo_ok")
        down_ok = sem("down_ok")
        y_ok = sem("y_ok")
        y_out = sem("y_out")
        ysb_free = sem("ysb_free")
        s_pick = [sem(f"s_pick{i}") for i in range(GR)]
        s_half = sem("s_half")
        s_sum = sem("s_sum")
        s_out = sem("s_out")

        w1_v = w1.rearrange("e (k p) f -> e p k f", p=P)
        w2_v = w2.rearrange("e (k p) d -> e p k d", p=P)
        xd_v = Xd[0:SLOTS, :].rearrange("(e r p) d -> e p r d", e=EXPERTS, p=P)
        y_v = Y[0:SLOTS, :].rearrange("(e r p) d -> e p r d", e=EXPERTS, p=P)
        NCONST = 6

        block = ctx.enter_context(nc.Block())

        @block.sync
        def _(sp):
            if first:
                sp.dma_start(X[:, :, :], x_dram.rearrange("(t p) d -> p t d", p=P)).then_inc(s_x, 16)
            for dst, src in ((identf[:, :], consts["identf"]), (before[:, :], consts["before"]),
                             (onesb[:, :], consts["onesb"]), (iota[:, :, :], consts["iota"]),
                             (restart[:, :], consts["restart"]),
                             (wg[:, :, :], Wg.rearrange("(k p) e -> p k e", p=P))):
                sp.dma_start(dst, src).then_inc(s_const, 16)
            sp.dma_start(w1raw[:, :, :], w1_v[0]).then_inc(w1_in, 16)
            sp.dma_start(w2raw[:, :, :], w2_v[0]).then_inc(w2_in, 16)
            if first:
                sp.wait_ge(s_zero, 1)
                zeros = hhi[:, 0:4, :].bitcast(F32).rearrange("p k c -> p (k c)")
                flat = Xd[0:SLOTS, :].rearrange("(p r) d -> p (r d)", p=P)
                for c in range(4):
                    sp.dma_start(flat[:, 2560 * c:2560 * (c + 1)], zeros).then_inc(s_zeroed, 16)
                sp.dma_start(Y[SLOTS:SLOTS + 1, :], zeros[0:1, 0:D]).then_inc(s_zeroed, 16)
            sp.wait_ge(s_scat, 16 * TOPK * TILES)
            sp.dma_start(xe[:, :, :], xd_v[0]).then_inc(xe_in, 16)
            with sp.Fori(1, EXPERTS) as e:
                sp.wait_ge(w1hi_ok, e)
                sp.wait_ge(w1lo_ok, e)
                sp.dma_start(w1raw[:, :, :], w1_v[e]).then_inc(w1_in, 16)
                sp.wait_ge(turned, KD * e)
                sp.dma_start(xe[:, :, :], xd_v[e]).then_inc(xe_in, 16)
                sp.wait_ge(w2hi_ok, e)
                sp.wait_ge(w2lo_ok, e)
                sp.dma_start(w2raw[:, :, :], w2_v[e]).then_inc(w2_in, 16)
            if out_dram is not None:
                out_v = out_dram.rearrange("(t p) d -> p t d", p=P)
                for t in range(TILES):
                    sp.wait_ge(s_sum, t + 1)
                    sp.dma_start(out_v[:, t, :], X[:, t, :]).then_inc(s_out, 16)
                sp.wait_ge(s_out, 16 * TILES)

        @block.gpsimd
        def _(pool):
            pool.sem_inc(ysb_free, 1)
            pool.wait_ge(s_slot, 1)
            if first:
                pool.wait_ge(s_zeroed, 16 * 5)
            for t in range(TILES):
                for k in range(TOPK):
                    pool.indirect_dma_start(
                        out=Xd[:, :], out_offset=bass.IndirectOffsetOnAxis(ap=slot[:, k, t:t + 1], axis=0),
                        in_=xn[:, t, :], in_offset=None, bounds_check=SLOTS - 1,
                        oob_is_err=False).then_inc(s_scat, 16)
            with pool.Fori(0, EXPERTS) as e:
                pool.wait_ge(y_ok, ROWTILES * e + ROWTILES)
                pool.dma_start(y_v[e], ysb[:, :, :]).then_inc(y_out, 16)
                pool.wait_ge(y_out, 16 * e + 16)
                pool.sem_inc(ysb_free, 1)
            for t in range(TILES):
                if t >= GR:
                    pool.wait_ge(s_sum, t - GR + 1)
                for k in range(TOPK):
                    pool.indirect_dma_start(
                        out=picks[:, t % GR, k, :], out_offset=None, in_=Y[:, :],
                        in_offset=bass.IndirectOffsetOnAxis(ap=slot[:, k, t:t + 1], axis=0),
                        bounds_check=SLOTS, oob_is_err=False).then_inc(s_pick[t % GR], 16)

        @block.tensor
        def _(pe):
            def turn_tile(t):
                pe.wait_ge(s_xn, t + 1)
                if t >= 2:
                    pe.wait_ge(s_xt, t - 1)
                for k in range(KD):
                    mm = pe.transpose(turn[:, (t % 2) * BANK + k * P:(t % 2) * BANK + (k + 1) * P],
                                      xn[:, t, k * P:(k + 1) * P], identf[:, :])
                mm.then_inc(s_rt, 1)

            def gate_tile(t):
                pe.wait_ge(s_xt, t + 1)
                for k in range(KD):
                    mm = pe.matmul(down[0][:, t * EXPERTS:(t + 1) * EXPERTS], xt[:, t % 2, k * P:(k + 1) * P],
                                   wg[:, k, :], start=(k == 0), stop=(k == KD - 1))
                mm.then_inc(s_gate, 1)

            pe.wait_ge(s_const, 16 * NCONST)
            turn_tile(0)
            for t in range(TILES):
                if t + 1 < TILES:
                    turn_tile(t + 1)
                gate_tile(t)
            pe.wait_ge(s_count, 2)
            pe.matmul(down[1][:, 0:P], before[:, :], countb[:, :], start=True, stop=False)
            pe.matmul(down[1][:, 0:P], onesb[:, :], priorb[:, :], start=False, stop=True).then_inc(s_pos, 1)

            def turn_rows(e, k):
                if k == 0:
                    pe.wait_ge(xe_in, 16 * e + 16)
                pe.wait_ge(xtlo_ok, KD * e + k)
                for r in range(ROWTILES):
                    mm = pe.transpose(turn[:, r * P:(r + 1) * P], xe[:, r, k * P:(k + 1) * P], identf[:, :])
                mm.then_inc(turned, 1)

            def up_product(e):
                pe.wait_ge(w1lo_ok, e + 1)
                for f in range(KF):
                    if f == 0:
                        pe.wait_ge(xtlo_ok, KD * e + KD)
                    if f >= 2:
                        pe.wait_ge(hlo_ok, KF * e + f - 1)
                    for c in range(2):
                        o = up[f % 2][:, c, 0:HALFCAP]
                        n = 0
                        for k in range(KD):
                            for w, x in ((w1hi, xthi), (w1hi, xtlo), (w1lo, xthi)):
                                mm = pe.matmul(o, w[:, k, f * P:(f + 1) * P],
                                               x[:, k, c * HALFCAP:(c + 1) * HALFCAP],
                                               start=(n == 0), stop=(n == 3 * KD - 1))
                                n += 1
                    mm.then_inc(up_ok, 1)

            def down_tile(e, r):
                if r == 0:
                    pe.wait_ge(w2lo_ok, e + 1)
                    pe.wait_ge(hlo_ok, KF * e + KF)
                if r >= 2:
                    pe.wait_ge(y_ok, ROWTILES * e + r - 1)
                o = down[r % 2][:, 0:D]
                n = 0
                for f in range(KF):
                    for h, w in ((hhi, w2hi), (hhi, w2lo), (hlo, w2hi)):
                        mm = pe.matmul(o, h[:, f, r * P:(r + 1) * P], w[:, f, :],
                                       start=(n == 0), stop=(n == 3 * KF - 1))
                        n += 1
                mm.then_inc(down_ok, 1)

            def down_product(e, between=None):
                for r in range(ROWTILES):
                    down_tile(e, r)
                    if r == 0 and between is not None:
                        between()

            turn_rows(0, 0)
            turn_rows(0, 1)
            up_product(0)
            with pe.Fori(1, EXPERTS) as e:
                turn_rows(e, 0)
                down_product(e - 1, lambda: turn_rows(e, 1))
                up_product(e)
            down_product(EXPERTS - 1)

        @block.scalar
        def _(act):
            act.wait_ge(s_var, 1)
            act.activation(sd[:, :], veps[:, :], ACT.Sqrt).then_inc(s_sd, 1)
            for t in range(TILES):
                act.wait_ge(s_rt, t + 1)
                if t >= 2:
                    act.wait_ge(s_gate, t - 1)
                act.copy(xt[:, t % 2, :], turn[:, (t % 2) * BANK:(t % 2) * BANK + D]).then_inc(s_xt, 1)
            act.wait_ge(s_shift, 2)
            act.activation(exps[:, :, :], shifted[:, :, :], ACT.Exp).then_inc(s_exp, 1)
            act.activation(egap[:, :], gap[:, :], ACT.Exp).then_inc(s_exp, 1)

            def split_w1(e):
                act.wait_ge(w1_in, 16 * e + 16)
                act.wait_ge(up_ok, KF * e)
                act.copy(w1hi[:, :, :], w1raw[:, :, :]).then_inc(w1hi_ok, 1)

            def split_w2(e):
                act.wait_ge(w2_in, 16 * e + 16)
                act.wait_ge(down_ok, ROWTILES * e)
                act.copy(w2hi[:, :, :], w2raw[:, :, :]).then_inc(w2hi_ok, 1)

            def split_rows(e, k):
                act.wait_ge(turned, KD * e + k + 1)
                if k == 0:
                    act.wait_ge(up_ok, KF * e)
                act.copy(xthi[:, k, :], turn[:, 0:CAP]).then_inc(xthi_ok, 1)

            def relu(e, fs):
                for f in fs:
                    act.wait_ge(up_ok, KF * e + f + 1)
                    if f == 0:
                        act.wait_ge(down_ok, ROWTILES * e)
                    act.activation(hhi[:, f, :].rearrange("p (c n) -> p c n", c=2),
                                   up[f % 2][:, :, 0:HALFCAP], ACT.Relu).then_inc(hhi_ok, 1)

            def copy_down(e):
                for r in range(ROWTILES):
                    act.wait_ge(down_ok, ROWTILES * e + r + 1)
                    if r == 0:
                        act.wait_ge(ysb_free, e + 1)
                    act.copy(ysb[:, r, :], down[r % 2][:, 0:D]).then_inc(y_ok, 1)

            if first:
                act.wait_ge(s_zeroed, 16 * 5)
            split_w1(0)
            split_rows(0, 0)
            split_rows(0, 1)
            relu(0, range(3))
            split_w2(0)
            relu(0, range(3, KF))
            with act.Fori(1, EXPERTS) as e:
                split_rows(e, 0)
                split_rows(e, 1)
                split_w1(e)
                copy_down(e - 1)
                relu(e, range(3))
                split_w2(e)
                relu(e, range(3, KF))
            copy_down(EXPERTS - 1)

        @block.vector
        def _(dve):
            steps = [0]

            def step(ins, wait=True):
                steps[0] += 1
                ins.then_inc(s_vec, 1)
                if wait:
                    dve.wait_ge(s_vec, steps[0])

            if first:
                dve.memset(hhi[:, 0:4, :].bitcast(F32), 0.0).then_inc(s_zero, 1)
                dve.wait_ge(s_x, 16)
            normalise(dve, step, X, stats, mv, veps, sd, rstd, nwt, xn, s_var, s_sd, s_xn)
            dve.wait_ge(s_gate, TILES)
            step(dve.tensor_copy(logits[:, :, :], down[0][:, 0:TILES * EXPERTS].rearrange(
                "p (t e) -> p t e", e=EXPERTS)))
            for t in range(TILES):
                step(dve.max(top[:, t, :], logits[:, t, :]), t == TILES - 1)
            dve.tensor_tensor(shifted[:, :, :], logits[:, :, :],
                              top[:, :, 0:1].to_broadcast([P, TILES, EXPERTS]), ALU.subtract).then_inc(s_shift, 1)
            dve.tensor_tensor(gap[:, :], top[:, :, 1], top[:, :, 0], ALU.subtract).then_inc(s_shift, 1)
            for t in range(TILES):
                step(dve.max_index(topi[:, t, :], top[:, t, :], logits[:, t, :]), t == TILES - 1)
            step(dve.tensor_copy(expert[:, :, :], topi[:, :, 0:TOPK].rearrange("p t k -> p k t")))
            for k in range(TOPK):
                step(dve.tensor_tensor(onehot[:, k, :, :], iota[:, :, :],
                                       expert[:, k, :].rearrange("p (t o) -> p t o", o=1).to_broadcast(
                                           [P, TILES, EXPERTS]), ALU.is_equal), k == TOPK - 1)
            step(dve.tensor_tensor(count[:, :, :].rearrange("p e t -> p t e"), onehot[:, 0, :, :],
                                   onehot[:, 1, :, :], ALU.add))
            cflat = count[:, :, :].rearrange("p e t -> p (e t)")
            dve.tensor_copy(countb[:, :], cflat).then_inc(s_count, 1)
            step(dve.tensor_tensor_scan(upto[:, :], restart[:, :], cflat, 0.0, ALU.mult, ALU.add))
            dve.tensor_tensor(priorb[:, :], upto[:, :], cflat, ALU.subtract).then_inc(s_count, 1)
            dve.wait_ge(s_exp, 2)
            step(dve.tensor_reduce(zsum[:, :], exps[:, :, :], AX.X, ALU.add))
            step(dve.reciprocal(zsum[:, :], zsum[:, :]))
            step(dve.tensor_scalar(gates[:, 0, :], zsum[:, :], 0.5, None, ALU.mult))
            step(dve.tensor_tensor(gates[:, 1, :], gates[:, 0, :], egap[:, :], ALU.mult))
            dve.wait_ge(s_pos, 1)
            for k in range(TOPK):
                step(dve.tensor_tensor(picked[:, k, :, :], onehot[:, k, :, :],
                                       down[1][:, 0:P].rearrange("p (e t) -> p t e", e=EXPERTS),
                                       ALU.mult), k == TOPK - 1)
            step(dve.tensor_reduce(pos[:, :, :], picked[:, :, :, :], AX.X, ALU.add))
            step(dve.tensor_scalar(keep[:, :, :], pos[:, :, :], float(CAP), None, ALU.is_lt))
            step(dve.scalar_tensor_tensor(slotf[:, :, :], expert[:, :, :], float(CAP), pos[:, :, :],
                                          ALU.mult, ALU.add))
            step(dve.scalar_tensor_tensor(slotf[:, :, :], slotf[:, :, :], float(-SLOTS), keep[:, :, :],
                                          ALU.add, ALU.mult))
            step(dve.tensor_tensor(gates[:, :, :], gates[:, :, :], keep[:, :, :], ALU.mult))
            dve.tensor_scalar(slot[:, :, :], slotf[:, :, :], float(SLOTS), None, ALU.add).then_inc(s_slot, 1)

            def rest(e, raw, hi, lo, hi_ok, lo_ok):
                dve.wait_ge(hi_ok, e + 1)
                dve.tensor_tensor(lo[:, :, :], raw[:, :, :], hi[:, :, :].bitcast(F32),
                                  ALU.subtract).then_inc(lo_ok, 1)

            def rest_rows(e, k):
                dve.wait_ge(xthi_ok, KD * e + k + 1)
                dve.tensor_tensor(xtlo[:, k, :], turn[:, 0:CAP], xthi[:, k, :].bitcast(F32),
                                  ALU.subtract).then_inc(xtlo_ok, 1)

            def rest_relu(e, fs):
                for f in fs:
                    dve.wait_ge(hhi_ok, KF * e + f + 1)
                    dve.scalar_tensor_tensor(
                        hlo[:, f, :].rearrange("p (c n) -> p c n", c=2), up[f % 2][:, :, 0:HALFCAP], 0.0,
                        hhi[:, f, :].bitcast(F32).rearrange("p (c n) -> p c n", c=2),
                        ALU.max, ALU.subtract).then_inc(hlo_ok, 1)

            rest(0, w1raw, w1hi, w1lo, w1hi_ok, w1lo_ok)
            rest_rows(0, 0)
            rest_rows(0, 1)
            rest_relu(0, range(3))
            rest(0, w2raw, w2hi, w2lo, w2hi_ok, w2lo_ok)
            rest_relu(0, range(3, KF))
            with dve.Fori(1, EXPERTS) as e:
                rest_rows(e, 0)
                rest_rows(e, 1)
                rest(e, w1raw, w1hi, w1lo, w1hi_ok, w1lo_ok)
                rest_relu(e, range(3))
                rest(e, w2raw, w2hi, w2lo, w2hi_ok, w2lo_ok)
                rest_relu(e, range(3, KF))
            for t in range(TILES):
                dve.wait_ge(s_pick[t % GR], 16 * TOPK * (t // GR + 1))
                dve.scalar_tensor_tensor(half[:, t % 2, :], picks[:, t % GR, 0, :], gates[:, 0, t:t + 1],
                                         X[:, t, :], ALU.mult, ALU.add).then_inc(s_half, 1)
                dve.wait_ge(s_half, t + 1)
                dve.scalar_tensor_tensor(X[:, t, :], picks[:, t % GR, 1, :], gates[:, 1, t:t + 1],
                                         half[:, t % 2, :], ALU.mult, ALU.add).then_inc(s_sum, 1)
            dve.wait_ge(s_sum, TILES)


CHUNK = 512
CHUNKS = TOKENS // CHUNK
CT = CHUNK // P
GROUPS = BATCH * KV_HEADS
QT_TILES = SEQ // P
Q_PARTS = (0, 0, 1, 1, 0, 2)
K_PARTS = (0, 1, 0, 1, 2, 0)
PRODUCTS = len(Q_PARTS)
PROWS = 2 * PRODUCTS * HALF
SHIFT_ROWS, ALIBI_ROWS = 2, 6
KROWS = PROWS + SHIFT_ROWS + ALIBI_ROWS


def project(nc, X, Wq, Wk, Wv, consts, q_dram, k_dram, v_all):
    with ExitStack() as ctx:
        def sb(name, shape, dt):
            return ctx.enter_context(nc.sbuf_tensor(name, shape, dt))

        def ps(name, shape, dt=F32):
            return ctx.enter_context(nc.psum_tensor(name, shape, dt))

        def sem(name):
            return ctx.enter_context(nc.semaphore(name))

        NQ, NK = HEADS * HD, KV_HEADS * HD
        QH, KH = NQ // 2, NK // 2
        NW = NQ + 2 * NK
        identf = sb("p_identf", [P, P], F32)
        tables = sb("p_tables", [P, 4, SEQ], F32)
        wraw = sb("p_wraw", [P, KD, NW], F32)
        whi = sb("p_whi", [P, KD, NW], F32R)
        wlo = sb("p_wlo", [P, KD, NW], F32R)
        xn = sb("p_xn", [P, TILES, D], F32)
        stats = sb("p_stats", [P, TILES, 6], F32)
        mv = sb("p_mv", [P, TILES, 2], F32)
        veps = sb("p_veps", [P, TILES], F32)
        sd = sb("p_sd", [P, TILES], F32)
        rstd = sb("p_rstd", [P, TILES], F32)
        nwt = sb("p_nwt", [P, TILES], F32)
        xthi = sb("p_xthi", [P, KD, CHUNK], F32R)
        xtlo = sb("p_xtlo", [P, KD, CHUNK], F32R)
        terms = [sb(f"p_terms{i}", [P, 4, CHUNK], F32) for i in range(2)]
        rot = [sb(f"p_rot{i}", [P, 2, CHUNK], F32) for i in range(2)]
        rest = [sb(f"p_rest{i}", [P, 2, CHUNK], F32) for i in range(2)]
        parts = [sb(f"p_parts{i}", [P, 3, 2, CHUNK], BF16) for i in range(2)]

        turn = [ps(f"p_turn{i}", [P, BANK]) for i in range(KD)]
        halves = [[ps(f"p_half{i}{h}", [P, BANK]) for h in range(2)] for i in range(2)]
        vps = ps("p_v", [P, BANK])

        s_const = sem("p_const")
        s_w = sem("p_w")
        s_vec = sem("p_vec")
        s_var = sem("p_var")
        s_sd = sem("p_sd")
        s_xn = sem("p_xn")
        s_whi = sem("p_whi")
        s_wlo = sem("p_wlo")
        s_turn = sem("p_turned")
        s_hi = sem("p_xthi")
        s_lo = sem("p_xtlo")
        s_qk = sem("p_qk")
        s_v = sem("p_v")
        s_terms = sem("p_terms")
        s_rot = sem("p_rot")
        s_p0 = sem("p_part0")
        s_r1 = sem("p_rest1")
        s_p1 = sem("p_part1")
        s_p2 = sem("p_part2")
        s_vout = sem("p_vout")
        s_vone = sem("p_vone")
        s_store = [sem(f"p_store{i}") for i in range(2)]

        rows = (P, KH)
        nheads = (HEADS, KV_HEADS)
        scratch = (q_dram, k_dram)
        which = (Q_PARTS, K_PARTS)
        block = ctx.enter_context(nc.Block())

        @block.sync
        def _(sp):
            sp.dma_start(identf[:, :], consts["identf"]).then_inc(s_const, 16)
            off = 0
            for w in (Wq, Wk, Wv):
                n = w.shape[1]
                sp.dma_start(wraw[:, :, off:off + n], w.rearrange("(k p) n -> p k n", p=P)).then_inc(s_w, 16)
                off += n
            sp.dma_start(tables[:, :, :], consts["rotary"]).then_inc(s_const, 16)
            for c in range(CHUNKS):
                b, t0 = c * CHUNK // SEQ, c * CHUNK % SEQ
                for i in range(2):
                    n = nheads[i]
                    sp.wait_ge(s_p0, 2 * c + i + 1)
                    sp.wait_ge(s_p1, 2 * c + i + 1)
                    sp.wait_ge(s_p2, 2 * c + i + 1)
                    for h in range(2):
                        for r, part in enumerate(which[i]):
                            row = (h * PRODUCTS + r) * HALF
                            dst = scratch[i][row:row + HALF, b * n:(b + 1) * n, t0:t0 + CHUNK].rearrange(
                                "j h t -> h j t")
                            sp.dma_start(dst, parts[i][0:rows[i], part, h, :]).then_inc(s_store[i], 16)
            for i in range(2):
                sp.wait_ge(s_store[i], 16 * 2 * PRODUCTS * CHUNKS)

        @block.gpsimd
        def _(pool):
            pool.memset(v_all[:, :, :, HD:HD + 1], 1.0).then_inc(s_vone, 1)
            pool.memset(v_all[:, :, :, HD + 1:2 * HD], 0.0).then_inc(s_vone, 1)
            for c in range(CHUNKS):
                for i in range(2):
                    m = rows[i]
                    pool.wait_ge(s_terms, 4 * (2 * c + i + 1))
                    pool.wait_ge(s_p0, 2 * c + i - 1) if c else None
                    pool.wait_ge(s_r1, 2 * c + i - 1) if c else None
                    pool.tensor_tensor(rot[i][0:m, 0, :], terms[i][0:m, 0, :], terms[i][0:m, 1, :],
                                       ALU.subtract).then_inc(s_rot, 1)
                    pool.tensor_tensor(rot[i][0:m, 1, :], terms[i][0:m, 2, :], terms[i][0:m, 3, :],
                                       ALU.add).then_inc(s_rot, 1)
            pool.wait_ge(s_vone, 2)

        @block.tensor
        def _(pe):
            pe.wait_ge(s_const, 32)

            def turn_chunk(c):
                pe.wait_ge(s_xn, CT * (c + 1))
                for k in range(KD):
                    if c:
                        pe.wait_ge(s_lo, KD * (c - 1) + k + 1)
                    for r in range(CT):
                        mm = pe.transpose(turn[k][:, r * P:(r + 1) * P],
                                          xn[:, c * CT + r, k * P:(k + 1) * P], identf[:, :])
                    mm.then_inc(s_turn, 1)

            def passes(k, a, b):
                return ((whi[:, k, a:b], xthi, xtlo), (wlo[:, k, a:b], xthi, None))

            turn_chunk(0)
            for c in range(CHUNKS):
                if c == 0:
                    pe.wait_ge(s_wlo, 1)
                pe.wait_ge(s_lo, KD * (c + 1))
                for i in range(2):
                    if c:
                        pe.wait_ge(s_terms, 4 * (2 * (c - 1) + i + 1))
                    for h in range(2):
                        m = rows[i]
                        a = i * NQ + h * m
                        n = 0
                        for k in range(KD):
                            for w, x in ((whi, xthi), (whi, xtlo), (wlo, xthi)):
                                mm = pe.matmul(halves[i][h][0:m, :], w[:, k, a:a + m], x[:, k, :],
                                               start=(n == 0), stop=(n == 3 * KD - 1))
                                n += 1
                    mm.then_inc(s_qk, 1)
                if c:
                    pe.wait_ge(s_vout, c)
                for r in range(CT):
                    n = 0
                    for k in range(KD):
                        for w, x in ((whi, xthi), (wlo, xthi), (whi, xtlo)):
                            mm = pe.matmul(vps[:, r * NK:(r + 1) * NK], x[:, k, r * P:(r + 1) * P],
                                           w[:, k, NQ + NK:NW], start=(n == 0), stop=(n == 3 * KD - 1))
                            n += 1
                mm.then_inc(s_v, 1)
                if c + 1 < CHUNKS:
                    turn_chunk(c + 1)

        @block.scalar
        def _(act):
            act.wait_ge(s_w, 48)
            act.copy(whi[:, :, :], wraw[:, :, :]).then_inc(s_whi, 1)
            act.wait_ge(s_var, 1)
            act.activation(sd[:, :], veps[:, :], ACT.Sqrt).then_inc(s_sd, 1)
            for c in range(CHUNKS):
                for k in range(KD):
                    act.wait_ge(s_turn, KD * c + k + 1)
                    if c:
                        act.wait_ge(s_v, c)
                    act.copy(xthi[:, k, :], turn[k][:, :]).then_inc(s_hi, 1)
                act.wait_ge(s_v, c + 1)
                b, t0 = c * CT // QT_TILES, c * CT % QT_TILES
                for r in range(CT):
                    cp = act.copy(v_all[:, b * KV_HEADS:(b + 1) * KV_HEADS, t0 + r, 0:HD],
                                  vps[:, r * NK:(r + 1) * NK].rearrange("p (g d) -> p g d", g=KV_HEADS))
                cp.then_inc(s_vout, 1)
                for i in range(2):
                    m = rows[i]
                    act.wait_ge(s_rot, 2 * (2 * c + i + 1))
                    if c:
                        act.wait_ge(s_store[i], 16 * 2 * PRODUCTS * c)
                    act.copy(parts[i][0:m, 0, :, :], rot[i][0:m, :, :]).then_inc(s_p0, 1)
                    act.wait_ge(s_r1, 2 * c + i + 1)
                    act.copy(parts[i][0:m, 1, :, :], rest[i][0:m, :, :]).then_inc(s_p1, 1)

        @block.vector
        def _(dve):
            steps = [0]

            def step(ins, wait=True):
                steps[0] += 1
                ins.then_inc(s_vec, 1)
                if wait:
                    dve.wait_ge(s_vec, steps[0])

            normalise(dve, step, X, stats, mv, veps, sd, rstd, nwt, xn, s_var, s_sd, s_xn)
            dve.wait_ge(s_whi, 1)
            dve.tensor_tensor(wlo[:, :, :], wraw[:, :, :], whi[:, :, :].bitcast(F32),
                              ALU.subtract).then_inc(s_wlo, 1)
            dve.wait_ge(s_const, 32)
            for c in range(CHUNKS):
                t0 = c * CHUNK % SEQ
                for k in range(KD):
                    dve.wait_ge(s_hi, KD * c + k + 1)
                    dve.tensor_tensor(xtlo[:, k, :], turn[k][:, :], xthi[:, k, :].bitcast(F32),
                                      ALU.subtract).then_inc(s_lo, 1)
                for i in range(2):
                    m = rows[i]
                    dve.wait_ge(s_qk, 2 * c + i + 1)
                    if c:
                        dve.wait_ge(s_rot, 2 * (2 * (c - 1) + i + 1))
                    cos = tables[0:m, 2 * i, t0:t0 + CHUNK]
                    sin = tables[0:m, 2 * i + 1, t0:t0 + CHUNK]
                    for n, (h, table) in enumerate(((0, cos), (1, sin), (0, sin), (1, cos))):
                        dve.tensor_tensor(terms[i][0:m, n, :], halves[i][h][0:m, :], table,
                                          ALU.mult).then_inc(s_terms, 1)
                for i in range(2):
                    m = rows[i]
                    dve.wait_ge(s_p0, 2 * c + i + 1)
                    dve.tensor_tensor(rest[i][0:m, :, :], rot[i][0:m, :, :], parts[i][0:m, 0, :, :],
                                      ALU.subtract).then_inc(s_r1, 1)
                    dve.wait_ge(s_p1, 2 * c + i + 1)
                    dve.tensor_tensor(parts[i][0:m, 2, :, :], rest[i][0:m, :, :], parts[i][0:m, 1, :, :],
                                      ALU.subtract).then_inc(s_p2, 1)


MAX_PIECES = [(i, c * BANK, min(BANK, (i + 1) * P - c * BANK))
              for i in range(QT_TILES) for c in range(2) if (i + 1) * P > c * BANK]
EXP_PIECES = [(j, max(j * P, c * BANK), BANK * (c + 1) - max(j * P, c * BANK))
              for j in range(QT_TILES) for c in range(2) if BANK * (c + 1) > j * P]
PIECES = len(MAX_PIECES)


def attend(nc, consts, q_dram, k_dram, v_all, attended):
    LAG, NS, NP = 2, 3, 4
    with ExitStack() as ctx:
        def sb(name, shape, dt):
            return ctx.enter_context(nc.sbuf_tensor(name, shape, dt))

        def ps(name, shape, dt=F32):
            return ctx.enter_context(nc.psum_tensor(name, shape, dt))

        def sem(name):
            return ctx.enter_context(nc.semaphore(name))

        identf = sb("a_identf", [P, P], F32)
        identb = sb("a_identb", [P, P], BF16)
        future = sb("a_future", [P, P], BF16)
        qt = sb("a_qt", [KROWS, BATCH * HEADS, SEQ], BF16)
        kt = sb("a_kt", [KROWS, GROUPS, SEQ], BF16)
        vg = sb("a_vg", [P, QT_TILES, 2 * HD], F32)
        probs = [sb(f"a_probs{i}", [P, BANK], F32) for i in range(NP)]
        piecemax = sb("a_piecemax", [P, GROUP, PIECES], F32)
        shift = sb("a_shift", [P, GROUP, QT_TILES], F32)
        shiftb = sb("a_shiftb", [P, P // (GROUP * QT_TILES), GROUP, QT_TILES], BF16)
        shiftT = sb("a_shiftT", [SHIFT_ROWS * GROUP * QT_TILES, P], BF16)
        osb = sb("a_osb", [P, SEQ], F32)
        rsum = sb("a_rsum", [P, QT_TILES, GROUP], F32)

        mscore = [ps(f"a_mscore{i}", [P, BANK]) for i in range(2)]
        score = [ps(f"a_score{i}", [P, BANK]) for i in range(NS)]
        oT = ps("a_oT", [P, 2 * BANK])
        misc = ps("a_misc", [P, BANK])

        s_const = sem("a_const")
        q_in = sem("a_q_in")
        mscored = sem("a_mscored")
        reduced = sem("a_reduced")
        s_blank = sem("a_blank")
        s_fin = sem("a_fin")
        shifts_ok = sem("a_shifts_ok")
        shiftT_ok = sem("a_shiftT_ok")
        shift_in = sem("a_shift_in")
        scored = sem("a_scored")
        expd = sem("a_expd")
        pv = sem("a_pv")
        vg_ok = sem("a_vg_ok")
        misc_shift = sem("a_misc_shift")
        misc_o = sem("a_misc_o")
        osb_ok = sem("a_osb_ok")
        s_rsum = sem("a_rsum")
        out_ok = sem("a_out_ok")

        PG = PIECES * GROUP
        NCONST = 5

        def wait(eng, s, value):
            if not isinstance(value, int) or value > 0:
                eng.wait_ge(s, value)

        block = ctx.enter_context(nc.Block())

        @block.sync
        def _(sp):
            sp.dma_start(identf[:, :], consts["identf"]).then_inc(s_const, 16)
            sp.dma_start(identb[:, :], consts["identb"]).then_inc(s_const, 16)
            sp.dma_start(future[:, :], consts["future"]).then_inc(s_const, 16)
            sp.dma_start(kt[PROWS:KROWS, :, :], consts["key_rows"]).then_inc(s_const, 16)
            sp.dma_start(qt[PROWS:KROWS, :, :], consts["query_rows"]).then_inc(s_const, 16)
            for b in range(BATCH):
                sp.dma_start(kt[0:PROWS, b * KV_HEADS:(b + 1) * KV_HEADS, :],
                             k_dram[:, b * KV_HEADS:(b + 1) * KV_HEADS, :]).then_inc(q_in, 16)
                sp.dma_start(qt[0:PROWS, b * HEADS:(b + 1) * HEADS, :],
                             q_dram[:, b * HEADS:(b + 1) * HEADS, :]).then_inc(q_in, 16)
                sp.wait_ge(q_in, 32 * (b + 1))
            with sp.Fori(0, GROUPS) as n:
                sp.wait_ge(shiftT_ok, n + 1)
                R = GROUP * QT_TILES
                for s in range(SHIFT_ROWS):
                    sp.dma_start(qt[PROWS + s:PROWS + s + 1, bass.ds(n * GROUP, GROUP), :].rearrange(
                        "o h (i q) -> o (h i) q", q=P), shiftT[s * R:(s + 1) * R, :]).then_inc(shift_in, 16)
            sp.wait_ge(shift_in, 16 * SHIFT_ROWS * GROUPS)

        @block.gpsimd
        def _(pool):
            def group(n):
                wait(pool, pv, PG * n)
                pool.tensor_copy(vg[:, :, :].rearrange("p j d -> p (j d)"),
                                 v_all[:, n, :, :].rearrange("p j d -> p (j d)")).then_inc(vg_ok, 1)

            group(0)
            with pool.Fori(1, GROUPS) as n:
                group(n)

        @block.tensor
        def _(pe):
            def max_piece(n, hh, t):
                i, k0, w = MAX_PIECES[t]
                last = k0 + w == (i + 1) * P
                wait(pe, reduced, PG * n + PIECES * hh + t - 1)
                o = mscore[t % 2][:, 0:w]
                mm = pe.matmul(o, qt[:, n * GROUP + hh, i * P:(i + 1) * P], kt[:, n, k0:k0 + w],
                               start=True, stop=True)
                if last:
                    mm = pe.matmul(mscore[t % 2][:, w - P:w], identb[:, :], future[:, :], start=False,
                                   stop=True, skip_group_check=True)
                mm.then_inc(mscored, 1)

            def exp_piece(n, hh, t):
                j, q0, w = EXP_PIECES[t]
                if hh == 0 and t == 0:
                    pe.wait_ge(shift_in, 16 * SHIFT_ROWS * (n + 1))
                wait(pe, expd, PG * n + PIECES * hh + t - NS + 1)
                mm = pe.matmul(score[t % NS][:, 0:w], kt[:, n, j * P:(j + 1) * P],
                               qt[:, n * GROUP + hh, q0:q0 + w], start=True, stop=True)
                if q0 == j * P:
                    mm = pe.matmul(score[t % NS][:, 0:P], future[:, :], identb[:, :], start=False,
                                   stop=True, skip_group_check=True)
                mm.then_inc(scored, 1)

            def v_piece(n, hh, t):
                j, q0, w = EXP_PIECES[t]
                if hh == 0 and t == 0:
                    pe.wait_ge(vg_ok, n + 1)
                    wait(pe, osb_ok, n)
                pe.wait_ge(expd, PG * n + PIECES * hh + t + 1)
                c = q0 // BANK
                pe.matmul(oT[2 * HD * hh:2 * HD * (hh + 1), q0:q0 + w], vg[:, j, :], probs[t % NP][:, 0:w],
                          start=(j == 0), stop=(j == (BANK * (c + 1)) // P - 1),
                          skip_group_check=True).then_inc(pv, 1)

            def turn_shifts(n):
                pe.wait_ge(shifts_ok, n + 1)
                wait(pe, out_ok, 2 * (n - 1))
                pe.transpose(misc[:, 0:P // 2].bitcast(BF16),
                             shiftb[:, :, :, :].rearrange("p s h i -> p (s h i)"),
                             identb[:, :]).then_inc(misc_shift, 1)

            def turn_out(n, c):
                pe.wait_ge(osb_ok, n + 1)
                if c == 0:
                    pe.wait_ge(shiftT_ok, n + 2 if not isinstance(n, int) or n + 1 < GROUPS else n + 1)
                else:
                    pe.wait_ge(out_ok, 2 * n + 1)
                for r in range(BANK // P):
                    mm = pe.transpose(misc[:, r * P:(r + 1) * P],
                                      osb[:, c * BANK + r * P:c * BANK + (r + 1) * P], identf[:, :])
                mm.then_inc(misc_o, 1)

            def group(n, more, before):
                for hh in range(GROUP):
                    for t in range(PIECES + LAG):
                        if t < PIECES:
                            exp_piece(n, hh, t)
                            if more:
                                max_piece(n + 1, hh, t)
                        if before and hh == 0 and t == 5:
                            turn_out(n - 1, 0)
                        if before and hh == 0 and t == 8:
                            turn_out(n - 1, 1)
                        if t >= LAG:
                            v_piece(n, hh, t - LAG)
                if more:
                    turn_shifts(n + 1)

            pe.wait_ge(s_const, 16 * NCONST)
            pe.wait_ge(q_in, 32 * BATCH)
            for hh in range(GROUP):
                for t in range(PIECES):
                    max_piece(0, hh, t)
            turn_shifts(0)
            group(0, True, False)
            with pe.Fori(1, GROUPS - 1) as n:
                group(n, True, True)
            group(GROUPS - 1, False, True)
            turn_out(GROUPS - 1, 0)
            turn_out(GROUPS - 1, 1)

        @block.scalar
        def _(act):
            def group(n):
                for hh in range(GROUP):
                    for t in range(PIECES):
                        w = EXP_PIECES[t][2]
                        act.wait_ge(scored, PG * n + PIECES * hh + t + 1)
                        wait(act, pv, PG * n + PIECES * hh + t - NP + 1)
                        act.activation(probs[t % NP][:, 0:w], score[t % NS][:, 0:w], ACT.Exp).then_inc(expd, 1)

            group(0)
            with act.Fori(1, GROUPS) as n:
                group(n)

        @block.vector
        def _(dve):
            def reduce_piece(n, hh, t):
                dve.wait_ge(mscored, PG * n + PIECES * hh + t + 1)
                if hh == 0 and t == 0:
                    wait(dve, s_fin, 4 * n)
                dve.tensor_reduce(piecemax[:, hh, t:t + 1], mscore[t % 2][:, 0:MAX_PIECES[t][2]], AX.X,
                                  ALU.max, negate=True).then_inc(reduced, 1)

            def finish_shifts(n):
                H = QT_TILES // 2
                dve.wait_ge(reduced, PG * (n + 1))
                two = piecemax[:, :, H:PIECES].rearrange("p h (i c) -> p h i c", c=2)
                dve.tensor_copy(shift[:, :, 0:H], piecemax[:, :, 0:H]).then_inc(s_fin, 1)
                dve.tensor_tensor(shift[:, :, H:QT_TILES], two[:, :, :, 0], two[:, :, :, 1],
                                  ALU.min).then_inc(s_fin, 1)
                dve.wait_ge(s_fin, 4 * n + 2)
                wait(dve, misc_shift, n)
                dve.tensor_copy(shiftb[:, 0, :, :], shift[:, :, :]).then_inc(s_fin, 1)
                dve.wait_ge(s_fin, 4 * n + 3)
                dve.tensor_tensor(shiftb[:, 1, :, :], shift[:, :, :], shiftb[:, 0, :, :],
                                  ALU.subtract).then_inc(s_fin, 1)
                dve.wait_ge(s_fin, 4 * n + 4)
                dve.sem_inc(shifts_ok, 1)

            def copy_shifts(n):
                dve.wait_ge(misc_shift, n + 1)
                wait(dve, shift_in, 16 * SHIFT_ROWS * n)
                dve.tensor_copy(shiftT[:, :], misc[:, 0:P // 2].bitcast(BF16)[
                    0:SHIFT_ROWS * GROUP * QT_TILES, 0:P]).then_inc(shiftT_ok, 1)

            def copy_sums(n):
                dve.wait_ge(pv, PG * (n + 1))
                wait(dve, misc_o, 2 * n)
                dve.tensor_copy(osb[:, :], oT[:, :]).then_inc(osb_ok, 1)

            def write_out(n, c):
                dve.wait_ge(misc_o, 2 * n + c + 1)
                H = BANK // P
                m = misc[:, :].rearrange("p (i h d) -> p i h d", i=H, h=GROUP)
                rs = rsum[:, c * H:(c + 1) * H, :]
                dve.reciprocal(rs, m[:, :, :, HD]).then_inc(s_rsum, 1)
                dve.wait_ge(s_rsum, 2 * n + c + 1)
                for r in range(H):
                    d = attended[:, c * H + r, bass.ds(n * GROUP * HD, GROUP * HD)]
                    last = dve.tensor_tensor(d.rearrange("p (h d) -> p h d", h=GROUP), m[:, r, :, 0:HD],
                                             rsum[:, c * H + r, :].rearrange("p (h o) -> p h o", o=1)
                                             .to_broadcast([P, GROUP, HD]), ALU.mult)
                last.then_inc(out_ok, 1)

            def group(n, more, before):
                for hh in range(GROUP):
                    for t in range(PIECES):
                        if before and hh == 0 and t == 6:
                            write_out(n - 1, 0)
                        if before and hh == 0 and t == 9:
                            write_out(n - 1, 1)
                        if more:
                            reduce_piece(n + 1, hh, t)
                if more:
                    finish_shifts(n + 1)
                    copy_shifts(n + 1)
                copy_sums(n)

            dve.memset(shiftb[:, SHIFT_ROWS:, :, :], 0.0).then_inc(s_blank, 1)
            dve.wait_ge(s_blank, 1)
            for hh in range(GROUP):
                for t in range(PIECES):
                    reduce_piece(0, hh, t)
            finish_shifts(0)
            copy_shifts(0)
            group(0, True, False)
            with dve.Fori(1, GROUPS - 1) as n:
                group(n, True, True)
            group(GROUPS - 1, False, True)
            write_out(GROUPS - 1, 0)
            write_out(GROUPS - 1, 1)
            dve.wait_ge(out_ok, 2 * GROUPS)


def project_out(nc, X, Wo, attended, consts, out_dram=None):
    with ExitStack() as ctx:
        def sb(name, shape, dt):
            return ctx.enter_context(nc.sbuf_tensor(name, shape, dt))

        def ps(name, shape, dt=F32):
            return ctx.enter_context(nc.psum_tensor(name, shape, dt))

        def sem(name):
            return ctx.enter_context(nc.semaphore(name))

        identf = sb("o_identf", [P, P], F32)
        wraw = sb("o_wraw", [P, KD, D], F32)
        whi = sb("o_whi", [P, KD, D], F32R)
        wlo = sb("o_wlo", [P, KD, D], F32R)
        ahi = sb("o_ahi", [P, 2, KD, P], F32R)
        alo = sb("o_alo", [P, 2, KD, P], F32R)
        turn = [ps(f"o_turn{i}", [P, BANK]) for i in range(2)]
        acc = [ps(f"o_acc{i}", [P, BANK]) for i in range(2)]
        s_w = sem("o_w")
        s_whi = sem("o_whi")
        s_wlo = sem("o_wlo")
        s_turn = sem("o_turned")
        s_hi = sem("o_hi")
        s_lo = sem("o_lo")
        s_mm = sem("o_mm")
        s_add = sem("o_add")
        s_out = sem("o_out")
        block = ctx.enter_context(nc.Block())

        @block.sync
        def _(sp):
            sp.dma_start(identf[:, :], consts["identf"]).then_inc(s_w, 16)
            sp.dma_start(wraw[:, :, :], Wo.rearrange("(k p) n -> p k n", p=P)).then_inc(s_w, 16)
            if out_dram is not None:
                sp.wait_ge(s_add, TILES)
                sp.dma_start(out_dram.rearrange("(t p) d -> p t d", p=P), X[:, :, :]).then_inc(s_out, 16)
                sp.wait_ge(s_out, 16)

        @block.tensor
        def _(pe):
            def turn_tile(t):
                b, i = t // QT_TILES, t % QT_TILES
                if t >= 2:
                    pe.wait_ge(s_lo, t - 1)
                for k in range(KD):
                    src = attended[:, i, b * D + k * P:b * D + (k + 1) * P]
                    mm = pe.transpose(turn[t % 2][:, k * P:(k + 1) * P], src, identf[:, :])
                mm.then_inc(s_turn, 1)

            pe.wait_ge(s_w, 32)
            turn_tile(0)
            pe.wait_ge(s_wlo, 1)
            for t in range(TILES):
                if t + 1 < TILES:
                    turn_tile(t + 1)
                pe.wait_ge(s_lo, t + 1)
                if t >= 2:
                    pe.wait_ge(s_add, t - 1)
                n = 0
                for k in range(KD):
                    for a, w in ((ahi, whi), (ahi, wlo), (alo, whi)):
                        mm = pe.matmul(acc[t % 2][:, 0:D], a[:, t % 2, k, :], w[:, k, :],
                                       start=(n == 0), stop=(n == 3 * KD - 1))
                        n += 1
                mm.then_inc(s_mm, 1)

        @block.scalar
        def _(act):
            act.wait_ge(s_w, 32)
            act.copy(whi[:, :, :], wraw[:, :, :]).then_inc(s_whi, 1)
            for t in range(TILES):
                act.wait_ge(s_turn, t + 1)
                if t >= 2:
                    act.wait_ge(s_mm, t - 1)
                act.copy(ahi[:, t % 2, :, :], turn[t % 2][:, 0:D].rearrange("p (k q) -> p k q", k=KD)).then_inc(s_hi, 1)

        @block.vector
        def _(dve):
            dve.wait_ge(s_whi, 1)
            dve.tensor_tensor(wlo[:, :, :], wraw[:, :, :], whi[:, :, :].bitcast(F32),
                              ALU.subtract).then_inc(s_wlo, 1)

            def add(t):
                dve.wait_ge(s_mm, t + 1)
                dve.tensor_tensor(X[:, t, :], acc[t % 2][:, 0:D], X[:, t, :], ALU.add).then_inc(s_add, 1)

            for t in range(TILES):
                dve.wait_ge(s_hi, t + 1)
                dve.tensor_tensor(alo[:, t % 2, :, :], turn[t % 2][:, 0:D].rearrange("p (k q) -> p k q", k=KD),
                                  ahi[:, t % 2, :, :].bitcast(F32), ALU.subtract).then_inc(s_lo, 1)
                if t:
                    add(t - 1)
            add(TILES - 1)
            dve.wait_ge(s_add, TILES)


def constants():
    bf = np.dtype("bfloat16")
    r = np.arange(P)
    c = {
        "identf": np.eye(P, dtype=np.float32),
        "before": (r[:, None] < r[None, :]).astype(bf),
        "onesb": np.ones((P, P), bf),
        "iota": np.broadcast_to(np.arange(EXPERTS, dtype=np.float32), (P, TILES, EXPERTS)).copy(),
        "restart": np.broadcast_to((np.arange(TILES) > 0).astype(np.float32), (P, EXPERTS, TILES)).reshape(
            P, EXPERTS * TILES).copy(),
    }
    pos = np.arange(SEQ, dtype=np.float32)
    theta = (1.0 / np.float32(10000.0) ** (np.arange(HALF, dtype=np.float32) / HALF)).astype(np.float32)
    angle = np.outer(pos, theta).astype(np.float32)
    cos, sin = (np.tile(f(angle).astype(np.float32).T, (P // HALF, 1)) for f in (np.cos, np.sin))
    scale = np.float32(HD ** -0.5)
    c["rotary"] = np.stack([cos * scale, sin * scale, cos, sin], axis=1)
    c["identb"] = np.eye(P).astype(bf)
    c["future"] = np.where(r[None, :] > r[:, None], NEG, 0.0).astype(bf)
    slopes = (2.0 ** (-8.0 * np.arange(1, HEADS + 1, dtype=np.float32) / HEADS)).astype(np.float32)
    parts, rest = [], slopes
    for _ in range(3):
        parts.append(rest.astype(bf))
        rest = rest - parts[-1].astype(np.float32)
    q = np.zeros((SHIFT_ROWS + ALIBI_ROWS, BATCH, HEADS, SEQ), bf)
    q[SHIFT_ROWS:] = np.repeat(np.stack(parts), 2, axis=0)[:, None, :, None]
    c["query_rows"] = q.reshape(SHIFT_ROWS + ALIBI_ROWS, BATCH * HEADS, SEQ)
    k = np.ones((SHIFT_ROWS + ALIBI_ROWS, GROUPS, SEQ), bf)
    k[SHIFT_ROWS::2] = (pos // P * P).astype(bf)
    k[SHIFT_ROWS + 1::2] = (pos % P).astype(bf)
    c["key_rows"] = k
    return c


def program(nc, ins, consts, out):
    x = ins["L0_attn_x"].rearrange("b t d -> (b t) d")
    o = out.rearrange("b t d -> (b t) d")
    with ExitStack() as ctx:
        X = ctx.enter_context(nc.sbuf_tensor("X", [P, TILES, D], F32))
        Xd = nc.dram_tensor("slot_rows", [SLOTS, D], F32).ap()
        Y = nc.dram_tensor("expert_rows", [SLOTS + 1, D], F32).ap()
        moe = (ins["L0_ffn_Wg"], ins["L0_ffn_w1"], ins["L0_ffn_w2"], Xd, Y, consts)
        ffn(nc, X, x, *moe, None, "a")
        with ExitStack() as mid:
            v_all = mid.enter_context(nc.sbuf_tensor("v_all", [P, GROUPS, QT_TILES, 2 * HD], F32))
            attended = mid.enter_context(nc.sbuf_tensor("attended", [P, QT_TILES, GROUPS * GROUP * HD], F32))
            q_dram = nc.dram_tensor("q_parts", [PROWS, BATCH * HEADS, SEQ], BF16).ap()
            k_dram = nc.dram_tensor("k_parts", [PROWS, GROUPS, SEQ], BF16).ap()
            project(nc, X, ins["L0_attn_Wq"], ins["L0_attn_Wk"], ins["L0_attn_Wv"], consts, q_dram, k_dram, v_all)
            attend(nc, consts, q_dram, k_dram, v_all, attended)
            project_out(nc, X, ins["L0_attn_Wo"], attended, consts, o if MODE == "attn" else None)
        if MODE == "attn":
            return
        ffn(nc, X, None, *moe, o, "b")


MODE = "all"
_INS = ['L0_attn_x', 'L0_attn_Wq', 'L0_attn_Wk', 'L0_attn_Wv', 'L0_attn_Wo', 'L0_ffn_Wg', 'L0_ffn_w1', 'L0_ffn_w2']


def kernel(**inputs):
    import concourse.bacc as _bacc
    from concourse.bass_utils import run_bass_kernel_spmd as _run

    nc = _bacc.Bacc("TRN2", target_bir_lowering=False, num_devices=1)
    arrays, args, consts = {}, {}, {}
    for name in _INS:
        a = np.ascontiguousarray(inputs[name])
        if name in ("L0_attn_Wq", "L0_attn_Wk"):
            a = np.ascontiguousarray(a.reshape(D, -1, 2, HALF).transpose(0, 2, 1, 3).reshape(D, -1))
        arrays[f"in_{name}"] = a
        args[name] = nc.dram_tensor(f"in_{name}", a.shape, mybir.dt.from_np(a.dtype), kind="ExternalInput").ap()
    for name, a in constants().items():
        arrays[f"const_{name}"] = a
        consts[name] = nc.dram_tensor(f"const_{name}", a.shape, mybir.dt.from_np(a.dtype), kind="ExternalInput").ap()
    out = nc.dram_tensor("out_0", (BATCH, SEQ, D), F32, kind="ExternalOutput").ap()
    program(nc, args, consts, out)
    r = _run(nc, [arrays], core_ids=[0])
    return r.results[0]["out_0"]
```

```python
from contextlib import ExitStack

import numpy as np

import concourse.bass as bass
from concourse import mybir

F32 = mybir.dt.float32
F32R = mybir.dt.float32r
BF16 = mybir.dt.bfloat16
F16 = mybir.dt.float16
U32 = mybir.dt.uint32
ALU = mybir.AluOpType
ACT = mybir.ActivationFunctionType
AX = mybir.AxisListType

P = 128
BATCH, SEQ, D = 2, 1024, 256
TOKENS = BATCH * SEQ
TILES = TOKENS // P
KD = D // P
EXPERTS, TOPK, DFF = 8, 2, 1024
CAP = -(-5 * TOKENS * TOPK // (4 * EXPERTS))
ROWTILES = CAP // P
KF = DFF // P
HALFCAP = CAP // 2
EPS = 1e-5
BANK = 512
HEADS, KV_HEADS, HD = 16, 4, 16
HALF = HD // 2
GROUP = HEADS // KV_HEADS
NEG = -1e30
FACTS = 6
LNG = 4
LNT = TILES // LNG


def normalise(dve, step, X, stats, mv, veps, sd, rstd, nwt, nmr, s_var, s_sd, s_nmr, arrived):
    for g in range(LNG):
        a, b = g * LNT, (g + 1) * LNT
        arrived(g)
        for t in range(a, b):
            step(dve.bn_stats(stats[:, t, :], X[:, t, :]), t == b - 1)
        for t in range(a, b):
            step(dve.bn_aggr(mv[:, t, :], stats[:, t, :]), t == b - 1)
        dve.tensor_scalar(veps[:, a:b], mv[:, a:b, 1], EPS, None, ALU.add).then_inc(s_var, 1)
        dve.wait_ge(s_var, g + 1)
        step(dve.tensor_scalar(nwt[:, a:b], veps[:, a:b], -0.5, None, ALU.mult), False)
        dve.wait_ge(s_sd, g + 1)
        step(dve.reciprocal(rstd[:, a:b], sd[:, a:b]))
        step(dve.tensor_tensor(sd[:, a:b], rstd[:, a:b], rstd[:, a:b], ALU.mult))
        step(dve.tensor_tensor(sd[:, a:b], sd[:, a:b], nwt[:, a:b], ALU.mult))
        step(dve.scalar_tensor_tensor(rstd[:, a:b], sd[:, a:b], 1.5, rstd[:, a:b], ALU.add, ALU.mult))
        dve.scalar_tensor_tensor(nmr[:, a:b], mv[:, a:b, 0], -1.0, rstd[:, a:b],
                                 ALU.mult, ALU.mult).then_inc(s_nmr, 1)


def scale_rows(act, X, veps, sd, rstd, nmr, xn, s_var, s_sd, s_nmr, s_xn, behind=lambda g: None):
    def root(g):
        act.wait_ge(s_var, g + 1)
        act.activation(sd[:, g * LNT:(g + 1) * LNT], veps[:, g * LNT:(g + 1) * LNT], ACT.Sqrt).then_inc(s_sd, 1)

    root(0)
    for g in range(LNG):
        act.wait_ge(s_nmr, g + 1)
        for t in range(g * LNT, (g + 1) * LNT):
            act.activation(xn[:, t, :], X[:, t, :], ACT.Identity, bias=nmr[:, t:t + 1],
                           scale=rstd[:, t:t + 1]).then_inc(s_xn, 1)
        if g + 1 < LNG:
            root(g + 1)
        behind(g)


def ffn(nc, X, x_dram, Wg, w1, w2, xn_dram, acc, consts, out_dram, tag):
    first = x_dram is not None
    with ExitStack() as ctx:
        def sb(name, shape, dt):
            return ctx.enter_context(nc.sbuf_tensor(f"{name}_{tag}", shape, dt))

        def ps(name, shape, dt=F32):
            return ctx.enter_context(nc.psum_tensor(f"{name}_{tag}", shape, dt))

        def sem(name):
            return ctx.enter_context(nc.semaphore(f"{name}_{tag}"))

        ET = EXPERTS * TILES
        NX = 4
        identf = sb("identf", [P, P], F32)
        before = sb("before", [P, P], BF16)
        onesb = sb("onesb", [P, P], BF16)
        iota = sb("iota", [P, TILES, EXPERTS], F32)
        restart = sb("restart", [P, ET], F32)
        slot_iota = sb("slot_iota", [P, CAP], F16)
        spare = sb("spare", [P, ROWTILES], F32)
        wg = sb("wg", [P, KD, EXPERTS], F32)
        xn = sb("xn", [P, TILES, D], F32)
        stats = sb("stats", [P, TILES, 6], F32)
        mv = sb("mv", [P, TILES, 2], F32)
        veps = sb("veps", [P, TILES], F32)
        sd = sb("sd", [P, TILES], F32)
        rstd = sb("rstd", [P, TILES], F32)
        nwt = sb("nwt", [P, TILES], F32)
        nmr = sb("nmr", [P, TILES], F32)
        xt = sb("xt", [P, NX, D], F32)
        logits = sb("logits", [P, TILES, EXPERTS], F32)
        top = sb("top", [P, TILES, 8], F32)
        topi = sb("topi", [P, TILES, 8], U32)
        shifted = sb("shifted", [P, TILES, EXPERTS], F32)
        exps = sb("exps", [P, TILES, EXPERTS], F32)
        gap = sb("gap", [P, TILES], F32)
        egap = sb("egap", [P, TILES], F32)
        zsum = sb("zsum", [P, TILES], F32)
        gates = sb("gates", [P, TOPK, TILES], F32)
        expert = sb("expert", [P, TOPK, TILES], F32)
        onehot = sb("onehot", [P, TOPK, TILES, EXPERTS], F32)
        count = sb("count", [P, EXPERTS, TILES], F32)
        countb = sb("countb", [P, ET], BF16)
        upto = sb("upto", [P, ET], F32)
        priorb = sb("priorb", [P, ET], BF16)
        place = sb("place", [P, ET], F32)
        weighted = sb("weighted", [P, TOPK, TILES, EXPERTS], F32)
        weight = sb("weight", [P, ET], F32)
        wrest = sb("wrest", [P, ET], F32)
        facts = sb("facts", [P, EXPERTS, TILES, FACTS], BF16)
        takes = sb("takes", [P, TILES, CAP], BF16)
        learnt = sb("learnt", [P, ROWTILES, FACTS], F32)
        nidx = sb("nidx", [P, 3, ROWTILES], F32)
        row_in = sb("row_in", [P, ROWTILES], U32)
        nrow_out = sb("nrow_out", [P, ROWTILES], U32)
        nscale = sb("nscale", [P, ROWTILES], F32)
        row_out = sb("row_out", [P, ROWTILES], U32)
        rscale = sb("rscale", [P, ROWTILES], F32)
        w1raw = sb("w1raw", [P, KD, DFF], F32)
        w2raw = sb("w2raw", [P, KF, D], F32)
        w1hi = sb("w1hi", [P, KD, DFF], F32R)
        w1lo = sb("w1lo", [P, KD, DFF], F32R)
        w2hi = sb("w2hi", [P, KF, D], F32R)
        w2lo = sb("w2lo", [P, KF, D], F32R)
        xe = sb("xe", [P, ROWTILES, D], F32)
        xthi = sb("xthi", [P, KD * CAP], F32R)
        xtlo = sb("xtlo", [P, KD * CAP], F32R)
        hhi = sb("hhi", [P, KF, CAP], F32R)
        hlo = sb("hlo", [P, KF, CAP], F32R)
        ysb = sb("ysb", [P, ROWTILES, D], F32)

        up = [ps(f"up{i}", [P, BANK]) for i in range(4)]
        turn = ps("turn", [P, BANK])
        learn = ps("learn", [P, BANK])
        down = [ps(f"down{i}", [P, BANK]) for i in range(2)]

        lbank = [down[0], turn, learn, down[1]]

        s_const = sem("s_const")
        s_x = [sem(f"s_x{g}") for g in range(LNG)]
        s_acc = sem("s_acc")
        s_vec = sem("s_vec")
        s_var = sem("s_var")
        s_sd = sem("s_sd")
        s_nmr = sem("s_nmr")
        s_xn = sem("s_xn")
        s_xnout = sem("s_xnout")
        s_passed = sem("passed")
        s_rt = sem("s_rt")
        s_xt = sem("s_xt")
        s_gate = sem("s_gate")
        s_shift = sem("s_shift")
        s_exp = sem("s_exp")
        s_count = sem("s_count")
        s_pos = sem("s_pos")
        s_facts = sem("s_facts")
        takes_ok = sem("takes_ok")
        learn_ok = sem("learn_ok")
        learnt_ok = sem("learnt_ok")
        s_idx = sem("s_idx")
        rows_ok = sem("rows_ok")
        cur_ok = sem("cur_ok")
        w1_in = sem("w1_in")
        w2_in = sem("w2_in")
        xe_in = sem("xe_in")
        w1hi_ok = sem("w1hi_ok")
        w1lo_ok = sem("w1lo_ok")
        w2hi_ok = sem("w2hi_ok")
        w2lo_ok = sem("w2lo_ok")
        turned = sem("turned")
        xthi_ok = sem("xthi_ok")
        xtlo_ok = sem("xtlo_ok")
        up_ok = sem("up_ok")
        hhi_ok = sem("hhi_ok")
        hlo_ok = sem("hlo_ok")
        down_ok = sem("down_ok")
        y_ok = sem("y_ok")
        added = sem("added")
        s_out = sem("s_out")

        w1_v = w1.rearrange("e (k p) f -> e p k f", p=P)
        w2_v = w2.rearrange("e (k p) d -> e p k d", p=P)
        tokens = lambda a: a.rearrange("(t p) d -> p t d", p=P)
        NCONST = 9
        TURNS = [(0, 4), (4, 8), (8, 10)]
        NT = len(TURNS)
        NH = 2 * KF
        ACCS = 2
        LEARN_AFTER = {0: (0, 1), 1: (2, 3), 2: (4,)}
        LEARNT = 3

        def wait(eng, s, value):
            if not isinstance(value, int) or value > 0:
                eng.wait_ge(s, value)

        block = ctx.enter_context(nc.Block())

        @block.sync
        def _(sp):
            if first:
                for g in range(LNG):
                    sp.dma_start(X[:, g * LNT:(g + 1) * LNT, :],
                                 tokens(x_dram)[:, g * LNT:(g + 1) * LNT, :]).then_inc(s_x[g], 16)
            for dst, src in ((identf[:, :], consts["identf"]), (before[:, :], consts["before"]),
                             (onesb[:, :], consts["onesb"]), (iota[:, :, :], consts["iota"]),
                             (restart[:, :], consts["restart"]), (slot_iota[:, :], consts["slot_iota"]),
                             (spare[:, :], consts["spare"]),
                             (wg[:, :, :], Wg.rearrange("(k p) e -> p k e", p=P))):
                sp.dma_start(dst, src).then_inc(s_const, 16)
            sp.dma_start(facts[:, :, :, :], consts["facts"]).then_inc(s_const, 16)
            sp.dma_start(w1raw[:, :, :], w1_v[0]).then_inc(w1_in, 16)
            sp.dma_start(w2raw[:, :, :], w2_v[0]).then_inc(w2_in, 16)
            if first:
                sp.dma_start(acc[0:TOKENS, :], x_dram).then_inc(s_acc, 16)
                sp.dma_start(acc[TOKENS:TOKENS + CAP, :], x_dram[0:CAP, :]).then_inc(s_acc, 16)
            else:
                sp.dma_start(tokens(acc[0:TOKENS, :]), X[:, :, :]).then_inc(s_acc, 16)
                sp.dma_start(tokens(acc[TOKENS:TOKENS + CAP, :]), X[:, 0:ROWTILES, :]).then_inc(s_acc, 16)
            for g in range(LNG):
                sp.wait_ge(s_xn, LNT * (g + 1))
                sp.dma_start(tokens(xn_dram)[:, g * LNT:(g + 1) * LNT, :],
                             xn[:, g * LNT:(g + 1) * LNT, :]).then_inc(s_xnout, 16)
            with sp.Fori(1, EXPERTS) as e:
                sp.wait_ge(w1lo_ok, KD * e)
                sp.dma_start(w1raw[:, :, :], w1_v[e]).then_inc(w1_in, 16)
                sp.wait_ge(w2lo_ok, KF * e)
                sp.dma_start(w2raw[:, :, :], w2_v[e]).then_inc(w2_in, 16)
            sp.wait_ge(added, 16 * ROWTILES * EXPERTS)
            if out_dram is not None:
                sp.dma_start(out_dram, acc[0:TOKENS, :]).then_inc(s_out, 16)
                sp.wait_ge(s_out, 16)

        @block.gpsimd
        def _(pool):
            def gather(e):
                pool.wait_ge(rows_ok, e + 1)
                wait(pool, turned, NT * e)
                pool.sem_inc(s_passed, 1)
                for r in range(ROWTILES):
                    pool.indirect_dma_start(
                        out=xe[:, r, :], out_offset=None, in_=xn_dram[:, :],
                        in_offset=bass.IndirectOffsetOnAxis(ap=row_in[:, r:r + 1], axis=0)).then_inc(xe_in, 16)

            def add(e):
                pool.wait_ge(cur_ok, 2 * (e + 1))
                for r in range(ROWTILES):
                    pool.wait_ge(y_ok, ROWTILES * e + r + 1)
                    pool.sem_inc(s_passed, 1)
                    pool.indirect_dma_start(
                        out=acc[:, :], out_offset=bass.IndirectOffsetOnAxis(ap=row_out[:, r:r + 1], axis=0),
                        in_=ysb[:, r, :], in_offset=None, compute_op=ALU.add).then_inc(added, 16)

            pool.wait_ge(s_xnout, 16 * LNG)
            gather(0)
            gather(1)
            pool.wait_ge(s_acc, 16 * ACCS)
            with pool.Fori(1, EXPERTS - 1) as e:
                add(e - 1)
                gather(e + 1)
            add(EXPERTS - 2)
            add(EXPERTS - 1)

        @block.tensor
        def _(pe):
            def turn_tile(t):
                pe.wait_ge(s_xn, t + 1)
                if t >= NX:
                    pe.wait_ge(s_xt, t - NX + 1)
                for k in range(KD):
                    mm = pe.transpose(up[t % NX][:, k * P:(k + 1) * P],
                                      xn[:, t, k * P:(k + 1) * P], identf[:, :])
                mm.then_inc(s_rt, 1)

            def gate_tile(t):
                pe.wait_ge(s_xt, t + 1)
                for k in range(KD):
                    mm = pe.matmul(lbank[t // LNT][:, t * EXPERTS:(t + 1) * EXPERTS],
                                   xt[:, t % NX, k * P:(k + 1) * P],
                                   wg[:, k, :], start=(k == 0), stop=(k == KD - 1))
                mm.then_inc(s_gate, 1)

            pe.wait_ge(s_const, 16 * NCONST)
            AHEAD = 2
            for t in range(AHEAD):
                turn_tile(t)
            for t in range(TILES):
                if t + AHEAD < TILES:
                    turn_tile(t + AHEAD)
                gate_tile(t)
            pe.wait_ge(s_count, 2)
            pe.matmul(down[1][:, 0:ET], before[:, :], countb[:, :], start=True, stop=False)
            pe.matmul(down[1][:, 0:ET], onesb[:, :], priorb[:, :], start=False, stop=True).then_inc(s_pos, 1)

            def learn_rows(e, r):
                if r == 0:
                    pe.wait_ge(takes_ok, TILES * (e + 1))
                    wait(pe, learnt_ok, e)
                for t in range(TILES):
                    mm = pe.matmul(learn[:, r * FACTS:(r + 1) * FACTS], takes[:, t, r * P:(r + 1) * P],
                                   facts[:, e, t, :], start=(t == 0), stop=(t == TILES - 1))
                if r == ROWTILES - 1:
                    mm.then_inc(learn_ok, 1)

            def turn_rows(e, i):
                if i == 0:
                    pe.wait_ge(xe_in, 16 * ROWTILES * (e + 1))
                wait(pe, xtlo_ok, NT * e + i)
                for j in range(*TURNS[i]):
                    k, r = divmod(j, ROWTILES)
                    c = j - TURNS[i][0]
                    mm = pe.transpose(turn[:, c * P:(c + 1) * P], xe[:, r, k * P:(k + 1) * P], identf[:, :])
                mm.then_inc(turned, 1)

            def up_product(e, more):
                pe.wait_ge(xtlo_ok, NT * (e + 1))
                pe.wait_ge(w1lo_ok, KD * (e + 1))
                for f in range(KF):
                    for c in range(2):
                        i = 2 * f + c
                        wait(pe, hlo_ok, NH * e + i - 3)
                        o = up[i % 4][:, 0:HALFCAP]
                        n = 0
                        for k in range(KD):
                            for w, x in ((w1hi, xthi), (w1hi, xtlo), (w1lo, xthi)):
                                a = k * CAP + c * HALFCAP
                                mm = pe.matmul(o, w[:, k, f * P:(f + 1) * P], x[:, a:a + HALFCAP],
                                               start=(n == 0), stop=(n == 3 * KD - 1))
                                n += 1
                        mm.then_inc(up_ok, 1)
                    if more:
                        for r in LEARN_AFTER.get(f, ()):
                            learn_rows(e + 1, r)

            def down_tile(e, r):
                if r >= 2:
                    pe.wait_ge(y_ok, ROWTILES * e + r - 1)
                o = down[r % 2][:, 0:D]
                n = 0
                for f in range(KF):
                    if r == 0:
                        pe.wait_ge(hlo_ok, NH * e + 2 * (f + 1))
                        pe.wait_ge(w2lo_ok, KF * e + f + 1)
                    for h, w in ((hhi, w2hi), (hhi, w2lo), (hlo, w2hi)):
                        mm = pe.matmul(o, h[:, f, r * P:(r + 1) * P], w[:, f, :],
                                       start=(n == 0), stop=(n == 3 * KF - 1))
                        n += 1
                mm.then_inc(down_ok, 1)

            pe.wait_ge(s_facts, 1)
            for r in range(ROWTILES):
                learn_rows(0, r)
            for i in range(NT):
                turn_rows(0, i)
            up_product(0, True)

            def expert_step(e, more):
                for r in range(ROWTILES):
                    down_tile(e - 1, r)
                    if r < NT:
                        turn_rows(e, r)
                up_product(e, more)

            with pe.Fori(1, EXPERTS - 1) as e:
                expert_step(e, True)
            expert_step(EXPERTS - 1, False)
            for r in range(ROWTILES):
                down_tile(EXPERTS - 1, r)

        @block.scalar
        def _(act):
            def split_w1(e, k):
                if k == 0:
                    act.wait_ge(w1_in, 16 * (e + 1))
                    wait(act, up_ok, NH * e)
                act.copy(w1hi[:, k, :], w1raw[:, k, :]).then_inc(w1hi_ok, 1)

            def copy_turned(g):
                for t in range(g * LNT, (g + 1) * LNT):
                    act.wait_ge(s_rt, t + 1)
                    if t >= NX:
                        act.wait_ge(s_gate, t - NX + 1)
                    act.copy(xt[:, t % NX, :], up[t % NX][:, 0:D]).then_inc(s_xt, 1)

            scale_rows(act, X, veps, sd, rstd, nmr, xn, s_var, s_sd, s_nmr, s_xn, copy_turned)
            for k in range(KD):
                split_w1(0, k)
            act.wait_ge(s_shift, 2)
            act.activation(exps[:, :, :], shifted[:, :, :], ACT.Exp).then_inc(s_exp, 1)
            act.activation(egap[:, :], gap[:, :], ACT.Exp).then_inc(s_exp, 1)

            def split_w2(e, f):
                if f == 0:
                    act.wait_ge(w2_in, 16 * (e + 1))
                    wait(act, down_ok, ROWTILES * e)
                act.copy(w2hi[:, f, :], w2raw[:, f, :]).then_inc(w2hi_ok, 1)

            def split_rows(e, i):
                act.wait_ge(turned, NT * e + i + 1)
                if i == 0:
                    wait(act, up_ok, NH * e)
                a, b = TURNS[i][0] * P, TURNS[i][1] * P
                act.copy(xthi[:, a:b], turn[:, 0:b - a]).then_inc(xthi_ok, 1)

            def copy_learnt(e):
                act.wait_ge(learn_ok, e + 1)
                wait(act, rows_ok, e)
                act.copy(learnt[:, :, :], learn[:, 0:ROWTILES * FACTS].rearrange(
                    "p (r f) -> p r f", f=FACTS)).then_inc(learnt_ok, 1)

            def relu(e, f):
                for c in range(2):
                    i = 2 * f + c
                    act.wait_ge(up_ok, NH * e + i + 1)
                    if i == 0:
                        wait(act, down_ok, ROWTILES * e)
                    act.activation(hhi[:, f, c * HALFCAP:(c + 1) * HALFCAP], up[i % 4][:, 0:HALFCAP],
                                   ACT.Relu).then_inc(hhi_ok, 1)

            def copy_down(e, r):
                act.wait_ge(down_ok, ROWTILES * e + r + 1)
                if r == 0:
                    act.wait_ge(cur_ok, 2 * (e + 1))
                act.activation(ysb[:, r, :], down[r % 2][:, 0:D], ACT.Copy,
                               scale=rscale[:, r:r + 1]).then_inc(y_ok, 1)

            def up_part(e, more):
                for f in range(KF):
                    relu(e, f)
                    split_w2(e, f)
                    if f == LEARNT and more:
                        copy_learnt(e + 1)

            copy_learnt(0)
            for i in range(NT):
                split_rows(0, i)
            up_part(0, True)

            def expert_step(e, more):
                for r in range(ROWTILES):
                    if r < KD:
                        split_w1(e, r)
                    copy_down(e - 1, r)
                    if r < NT:
                        split_rows(e, r)
                up_part(e, more)

            with act.Fori(1, EXPERTS - 1) as e:
                expert_step(e, True)
            expert_step(EXPERTS - 1, False)
            for r in range(ROWTILES):
                copy_down(EXPERTS - 1, r)

        @block.vector
        def _(dve):
            steps = [0]

            def step(ins, wait=True):
                steps[0] += 1
                ins.then_inc(s_vec, 1)
                if wait:
                    dve.wait_ge(s_vec, steps[0])

            normalise(dve, step, X, stats, mv, veps, sd, rstd, nwt, nmr, s_var, s_sd, s_nmr,
                      lambda g: dve.wait_ge(s_x[g], 16) if first else None)
            dve.wait_ge(s_const, 16 * NCONST)
            for g in range(LNG):
                a, b = g * LNT, (g + 1) * LNT
                dve.wait_ge(s_gate, b)
                step(dve.tensor_copy(logits[:, a:b, :], lbank[g][:, a * EXPERTS:b * EXPERTS].rearrange(
                    "p (t e) -> p t e", e=EXPERTS)))
                for t in range(a, b):
                    step(dve.max(top[:, t, :], logits[:, t, :]), t == b - 1)
                for t in range(a, b):
                    step(dve.max_index(topi[:, t, :], top[:, t, :], logits[:, t, :]), t == b - 1)
                step(dve.tensor_copy(expert[:, :, a:b], topi[:, a:b, 0:TOPK].rearrange("p t k -> p k t")))
                for k in range(TOPK):
                    step(dve.tensor_tensor(onehot[:, k, a:b, :], iota[:, a:b, :],
                                           expert[:, k, a:b].rearrange("p (t o) -> p t o", o=1).to_broadcast(
                                               [P, LNT, EXPERTS]), ALU.is_equal), k == TOPK - 1)
                step(dve.tensor_tensor(count[:, :, a:b].rearrange("p e t -> p t e"), onehot[:, 0, a:b, :],
                                       onehot[:, 1, a:b, :], ALU.add))
            cflat = count[:, :, :].rearrange("p e t -> p (e t)")
            dve.tensor_copy(countb[:, :], cflat).then_inc(s_count, 1)
            step(dve.tensor_tensor_scan(upto[:, :], restart[:, :], cflat, 0.0, ALU.mult, ALU.add))
            dve.tensor_tensor(priorb[:, :], upto[:, :], cflat, ALU.subtract).then_inc(s_count, 1)
            dve.tensor_tensor(shifted[:, :, :], logits[:, :, :],
                              top[:, :, 0:1].to_broadcast([P, TILES, EXPERTS]), ALU.subtract).then_inc(s_shift, 1)
            dve.tensor_tensor(gap[:, :], top[:, :, 1], top[:, :, 0], ALU.subtract).then_inc(s_shift, 1)
            dve.wait_ge(s_pos, 1)
            step(dve.scalar_tensor_tensor(place[:, :], down[1][:, 0:ET], 1.0, cflat, ALU.add, ALU.mult))
            step(dve.tensor_scalar(place[:, :], place[:, :], -1.0, None, ALU.add))

            def rest_w1(e, k):
                dve.wait_ge(w1hi_ok, KD * e + k + 1)
                dve.tensor_tensor(w1lo[:, k, :], w1raw[:, k, :], w1hi[:, k, :].bitcast(F32),
                                  ALU.subtract).then_inc(w1lo_ok, 1)

            def make_takes(e, ts):
                for t in ts:
                    if t == 0:
                        wait(dve, learn_ok, e)
                    at = place[:, t + e * TILES:t + e * TILES + 1] if isinstance(e, int) else \
                        place[:, bass.ds(e * TILES + t, 1)]
                    dve.tensor_scalar(takes[:, t, :], slot_iota[:, :], at, None,
                                      ALU.is_equal).then_inc(takes_ok, 1)

            make_takes(0, range(TILES))
            dve.wait_ge(s_exp, 2)
            step(dve.tensor_reduce(zsum[:, :], exps[:, :, :], AX.X, ALU.add))
            step(dve.reciprocal(zsum[:, :], zsum[:, :]))
            step(dve.tensor_scalar(gates[:, 0, :], zsum[:, :], 0.5, None, ALU.mult))
            step(dve.tensor_tensor(gates[:, 1, :], gates[:, 0, :], egap[:, :], ALU.mult))
            for k in range(TOPK):
                step(dve.tensor_tensor(weighted[:, k, :, :], onehot[:, k, :, :],
                                       gates[:, k, :].rearrange("p (t o) -> p t o", o=1).to_broadcast(
                                           [P, TILES, EXPERTS]), ALU.mult), k == TOPK - 1)
            step(dve.tensor_tensor(weight[:, :].rearrange("p (e t) -> p t e", e=EXPERTS),
                                   weighted[:, 0, :, :], weighted[:, 1, :, :], ALU.add))
            col = lambda c: facts[:, :, :, c].rearrange("p e t -> p (e t)")
            step(dve.tensor_copy(col(3), weight[:, :]))
            step(dve.tensor_tensor(wrest[:, :], weight[:, :], col(3), ALU.subtract))
            step(dve.tensor_copy(col(4), wrest[:, :]))
            step(dve.tensor_tensor(col(5), wrest[:, :], col(4), ALU.subtract))
            dve.sem_inc(s_facts, 1)

            def rest_w2(e, f):
                dve.wait_ge(w2hi_ok, KF * e + f + 1)
                dve.tensor_tensor(w2lo[:, f, :], w2raw[:, f, :], w2hi[:, f, :].bitcast(F32),
                                  ALU.subtract).then_inc(w2lo_ok, 1)

            def rest_rows(e, i):
                dve.wait_ge(xthi_ok, NT * e + i + 1)
                a, b = TURNS[i][0] * P, TURNS[i][1] * P
                dve.tensor_tensor(xtlo[:, a:b], turn[:, 0:b - a], xthi[:, a:b].bitcast(F32),
                                  ALU.subtract).then_inc(xtlo_ok, 1)

            def rest_relu(e, f):
                for c in range(2):
                    i = 2 * f + c
                    dve.wait_ge(hhi_ok, NH * e + i + 1)
                    a = c * HALFCAP
                    dve.scalar_tensor_tensor(hlo[:, f, a:a + HALFCAP], up[i % 4][:, 0:HALFCAP], 0.0,
                                             hhi[:, f, a:a + HALFCAP].bitcast(F32),
                                             ALU.max, ALU.subtract).then_inc(hlo_ok, 1)

            def read_learnt(e):
                dve.wait_ge(learnt_ok, e + 1)
                dve.tensor_tensor(nidx[:, 0, :], learnt[:, :, 1], learnt[:, :, 2], ALU.add).then_inc(s_idx, 1)
                dve.tensor_tensor(nidx[:, 1, :], learnt[:, :, 3], learnt[:, :, 4], ALU.add).then_inc(s_idx, 1)
                dve.tensor_scalar(nidx[:, 2, :], learnt[:, :, 0], -1.0, 1.0, ALU.mult, ALU.add).then_inc(s_idx, 1)
                dve.wait_ge(s_idx, 4 * e + 3)
                wait(dve, xe_in, 16 * ROWTILES * e)
                dve.tensor_tensor(nidx[:, 2, :], nidx[:, 2, :], spare[:, :], ALU.mult).then_inc(s_idx, 1)
                dve.tensor_copy(row_in[:, :], nidx[:, 0, :])
                dve.tensor_tensor(nscale[:, :], nidx[:, 1, :], learnt[:, :, 5], ALU.add)
                dve.wait_ge(s_idx, 4 * e + 4)
                dve.tensor_tensor(nrow_out[:, :], nidx[:, 0, :], nidx[:, 2, :], ALU.add).then_inc(rows_ok, 1)

            def make_current(e):
                dve.wait_ge(rows_ok, e + 1)
                wait(dve, added, 16 * ROWTILES * e)
                dve.tensor_copy(row_out[:, :], nrow_out[:, :]).then_inc(cur_ok, 1)
                dve.tensor_copy(rscale[:, :], nscale[:, :]).then_inc(cur_ok, 1)

            def up_part(e, more):
                for f in range(KF):
                    rest_relu(e, f)
                    rest_w2(e, f)
                    if f == LEARNT:
                        make_current(e)
                        if more:
                            read_learnt(e + 1)

            read_learnt(0)
            for k in range(KD):
                rest_w1(0, k)
            make_takes(1, range(TILES))
            for i in range(NT):
                rest_rows(0, i)
            up_part(0, True)

            def expert_step(e, more):
                for r in range(NT):
                    if r < KD:
                        rest_w1(e, r)
                    if r and more:
                        make_takes(e + 1, range((r - 1) * TILES // 2, r * TILES // 2))
                    rest_rows(e, r)
                up_part(e, more)

            with dve.Fori(1, EXPERTS - 1) as e:
                expert_step(e, True)
            expert_step(EXPERTS - 1, False)


CHUNK = 512
CHUNKS = TOKENS // CHUNK
CT = CHUNK // P
GROUPS = BATCH * KV_HEADS
QT_TILES = SEQ // P
Q_PARTS = (0, 0, 1, 1, 0, 2)
K_PARTS = (0, 1, 0, 1, 2, 0)
PRODUCTS = len(Q_PARTS)
PROWS = 2 * PRODUCTS * HALF
SHIFT_ROWS, ALIBI_ROWS = 2, 6
KROWS = PROWS + SHIFT_ROWS + ALIBI_ROWS


def project(nc, X, x_dram, Wq, Wk, Wv, consts, q_dram, k_dram, v_all):
    with ExitStack() as ctx:
        def sb(name, shape, dt):
            return ctx.enter_context(nc.sbuf_tensor(name, shape, dt))

        def ps(name, shape, dt=F32):
            return ctx.enter_context(nc.psum_tensor(name, shape, dt))

        def sem(name):
            return ctx.enter_context(nc.semaphore(name))

        NQ, NK = HEADS * HD, KV_HEADS * HD
        QH, KH = NQ // 2, NK // 2
        NW = NQ + 2 * NK
        identf = sb("p_identf", [P, P], F32)
        tables = sb("p_tables", [P, 4, SEQ], F32)
        wraw = sb("p_wraw", [P, KD, NW], F32)
        whi = sb("p_whi", [P, KD, NW], F32R)
        wlo = sb("p_wlo", [P, KD, NW], F32R)
        xn = sb("p_xn", [P, TILES, D], F32)
        stats = sb("p_stats", [P, TILES, 6], F32)
        mv = sb("p_mv", [P, TILES, 2], F32)
        veps = sb("p_veps", [P, TILES], F32)
        sd = sb("p_sd", [P, TILES], F32)
        rstd = sb("p_rstd", [P, TILES], F32)
        nwt = sb("p_nwt", [P, TILES], F32)
        nmr = sb("p_nmr", [P, TILES], F32)
        xthi = sb("p_xthi", [P, KD, CHUNK], F32R)
        xtlo = sb("p_xtlo", [P, KD, CHUNK], F32R)
        terms = [sb(f"p_terms{i}", [P, 4, CHUNK], F32) for i in range(2)]
        rot = [sb(f"p_rot{i}", [P, 2, CHUNK], F32) for i in range(2)]
        rest = [sb(f"p_rest{i}", [P, 2, CHUNK], F32) for i in range(2)]
        parts = [sb(f"p_parts{i}", [P, 3, 2, CHUNK], BF16) for i in range(2)]

        turn = [ps(f"p_turn{i}", [P, BANK]) for i in range(KD)]
        halves = [[ps(f"p_half{i}{h}", [P, BANK]) for h in range(2)] for i in range(2)]
        vps = ps("p_v", [P, BANK])

        s_const = sem("p_const")
        s_w = sem("p_w")
        s_vec = sem("p_vec")
        s_var = sem("p_var")
        s_sd = sem("p_sd")
        s_nmr = sem("p_nmr")
        s_x = [sem(f"p_x{g}") for g in range(LNG)]
        s_xn = sem("p_xn")
        s_whi = sem("p_whi")
        s_wlo = sem("p_wlo")
        s_turn = sem("p_turned")
        s_hi = sem("p_xthi")
        s_lo = sem("p_xtlo")
        s_qk = sem("p_qk")
        s_v = sem("p_v")
        s_terms = sem("p_terms")
        s_rot = sem("p_rot")
        s_p0 = sem("p_part0")
        s_r1 = sem("p_rest1")
        s_p1 = sem("p_part1")
        s_p2 = sem("p_part2")
        s_vout = sem("p_vout")
        s_vone = sem("p_vone")
        s_store = [sem(f"p_store{i}") for i in range(2)]

        rows = (P, KH)
        nheads = (HEADS, KV_HEADS)
        scratch = (q_dram, k_dram)
        which = (Q_PARTS, K_PARTS)
        block = ctx.enter_context(nc.Block())

        @block.sync
        def _(sp):
            for g in range(LNG):
                sp.dma_start(X[:, g * LNT:(g + 1) * LNT, :], x_dram.rearrange("(t p) d -> p t d", p=P)[
                    :, g * LNT:(g + 1) * LNT, :]).then_inc(s_x[g], 16)
            sp.dma_start(identf[:, :], consts["identf"]).then_inc(s_const, 16)
            off = 0
            for w in (Wq, Wk, Wv):
                n = w.shape[1]
                sp.dma_start(wraw[:, :, off:off + n], w.rearrange("(k p) n -> p k n", p=P)).then_inc(s_w, 16)
                off += n
            sp.dma_start(tables[:, :, :], consts["rotary"]).then_inc(s_const, 16)
            for c in range(CHUNKS):
                b, t0 = c * CHUNK // SEQ, c * CHUNK % SEQ
                for i in range(2):
                    n = nheads[i]
                    sp.wait_ge(s_p0, 2 * c + i + 1)
                    sp.wait_ge(s_p1, 2 * c + i + 1)
                    sp.wait_ge(s_p2, 2 * c + i + 1)
                    for h in range(2):
                        for r, part in enumerate(which[i]):
                            row = (h * PRODUCTS + r) * HALF
                            dst = scratch[i][row:row + HALF, b * n:(b + 1) * n, t0:t0 + CHUNK].rearrange(
                                "j h t -> h j t")
                            sp.dma_start(dst, parts[i][0:rows[i], part, h, :]).then_inc(s_store[i], 16)
            for i in range(2):
                sp.wait_ge(s_store[i], 16 * 2 * PRODUCTS * CHUNKS)

        @block.gpsimd
        def _(pool):
            pool.memset(v_all[:, :, :, HD:HD + 1], 1.0).then_inc(s_vone, 1)
            pool.memset(v_all[:, :, :, HD + 1:2 * HD], 0.0).then_inc(s_vone, 1)
            for c in range(CHUNKS):
                for i in range(2):
                    m = rows[i]
                    pool.wait_ge(s_terms, 4 * (2 * c + i + 1))
                    pool.wait_ge(s_p0, 2 * c + i - 1) if c else None
                    pool.wait_ge(s_r1, 2 * c + i - 1) if c else None
                    pool.tensor_tensor(rot[i][0:m, 0, :], terms[i][0:m, 0, :], terms[i][0:m, 1, :],
                                       ALU.subtract).then_inc(s_rot, 1)
                    pool.tensor_tensor(rot[i][0:m, 1, :], terms[i][0:m, 2, :], terms[i][0:m, 3, :],
                                       ALU.add).then_inc(s_rot, 1)
            pool.wait_ge(s_vone, 2)

        @block.tensor
        def _(pe):
            pe.wait_ge(s_const, 32)

            def turn_chunk(c):
                pe.wait_ge(s_xn, CT * (c + 1))
                for k in range(KD):
                    if c:
                        pe.wait_ge(s_lo, KD * (c - 1) + k + 1)
                    for r in range(CT):
                        mm = pe.transpose(turn[k][:, r * P:(r + 1) * P],
                                          xn[:, c * CT + r, k * P:(k + 1) * P], identf[:, :])
                    mm.then_inc(s_turn, 1)

            turn_chunk(0)
            for c in range(CHUNKS):
                if c == 0:
                    pe.wait_ge(s_wlo, 1)
                pe.wait_ge(s_lo, KD * (c + 1))
                for i in range(2):
                    if c:
                        pe.wait_ge(s_terms, 4 * (2 * (c - 1) + i + 1))
                    for h in range(2):
                        m = rows[i]
                        a = i * NQ + h * m
                        n = 0
                        for k in range(KD):
                            for w, x in ((whi, xthi), (whi, xtlo), (wlo, xthi)):
                                mm = pe.matmul(halves[i][h][0:m, :], w[:, k, a:a + m], x[:, k, :],
                                               start=(n == 0), stop=(n == 3 * KD - 1))
                                n += 1
                    mm.then_inc(s_qk, 1)
                if c:
                    pe.wait_ge(s_vout, c)
                for r in range(CT):
                    n = 0
                    for k in range(KD):
                        for w, x in ((whi, xthi), (wlo, xthi), (whi, xtlo)):
                            mm = pe.matmul(vps[:, r * NK:(r + 1) * NK], x[:, k, r * P:(r + 1) * P],
                                           w[:, k, NQ + NK:NW], start=(n == 0), stop=(n == 3 * KD - 1))
                            n += 1
                mm.then_inc(s_v, 1)
                if c + 1 < CHUNKS:
                    turn_chunk(c + 1)

        @block.scalar
        def _(act):
            act.wait_ge(s_w, 48)
            act.copy(whi[:, :, :], wraw[:, :, :]).then_inc(s_whi, 1)
            scale_rows(act, X, veps, sd, rstd, nmr, xn, s_var, s_sd, s_nmr, s_xn)
            for c in range(CHUNKS):
                for k in range(KD):
                    act.wait_ge(s_turn, KD * c + k + 1)
                    if c:
                        act.wait_ge(s_v, c)
                    act.copy(xthi[:, k, :], turn[k][:, :]).then_inc(s_hi, 1)
                act.wait_ge(s_v, c + 1)
                b, t0 = c * CT // QT_TILES, c * CT % QT_TILES
                for r in range(CT):
                    cp = act.copy(v_all[:, b * KV_HEADS:(b + 1) * KV_HEADS, t0 + r, 0:HD],
                                  vps[:, r * NK:(r + 1) * NK].rearrange("p (g d) -> p g d", g=KV_HEADS))
                cp.then_inc(s_vout, 1)
                for i in range(2):
                    m = rows[i]
                    act.wait_ge(s_rot, 2 * (2 * c + i + 1))
                    if c:
                        act.wait_ge(s_store[i], 16 * 2 * PRODUCTS * c)
                    act.copy(parts[i][0:m, 0, :, :], rot[i][0:m, :, :]).then_inc(s_p0, 1)
                    act.wait_ge(s_r1, 2 * c + i + 1)
                    act.copy(parts[i][0:m, 1, :, :], rest[i][0:m, :, :]).then_inc(s_p1, 1)

        @block.vector
        def _(dve):
            steps = [0]

            def step(ins, wait=True):
                steps[0] += 1
                ins.then_inc(s_vec, 1)
                if wait:
                    dve.wait_ge(s_vec, steps[0])

            normalise(dve, step, X, stats, mv, veps, sd, rstd, nwt, nmr, s_var, s_sd, s_nmr,
                      lambda g: dve.wait_ge(s_x[g], 16))
            dve.wait_ge(s_whi, 1)
            dve.tensor_tensor(wlo[:, :, :], wraw[:, :, :], whi[:, :, :].bitcast(F32),
                              ALU.subtract).then_inc(s_wlo, 1)
            dve.wait_ge(s_const, 32)
            for c in range(CHUNKS):
                t0 = c * CHUNK % SEQ
                for k in range(KD):
                    dve.wait_ge(s_hi, KD * c + k + 1)
                    dve.tensor_tensor(xtlo[:, k, :], turn[k][:, :], xthi[:, k, :].bitcast(F32),
                                      ALU.subtract).then_inc(s_lo, 1)
                for i in range(2):
                    m = rows[i]
                    dve.wait_ge(s_qk, 2 * c + i + 1)
                    if c:
                        dve.wait_ge(s_rot, 2 * (2 * (c - 1) + i + 1))
                    cos = tables[0:m, 2 * i, t0:t0 + CHUNK]
                    sin = tables[0:m, 2 * i + 1, t0:t0 + CHUNK]
                    for n, (h, table) in enumerate(((0, cos), (1, sin), (0, sin), (1, cos))):
                        dve.tensor_tensor(terms[i][0:m, n, :], halves[i][h][0:m, :], table,
                                          ALU.mult).then_inc(s_terms, 1)
                for i in range(2):
                    m = rows[i]
                    dve.wait_ge(s_p0, 2 * c + i + 1)
                    dve.tensor_tensor(rest[i][0:m, :, :], rot[i][0:m, :, :], parts[i][0:m, 0, :, :],
                                      ALU.subtract).then_inc(s_r1, 1)
                    dve.wait_ge(s_p1, 2 * c + i + 1)
                    dve.tensor_tensor(parts[i][0:m, 2, :, :], rest[i][0:m, :, :], parts[i][0:m, 1, :, :],
                                      ALU.subtract).then_inc(s_p2, 1)


MAX_PIECES = [(i, c * BANK, min(BANK, (i + 1) * P - c * BANK))
              for i in range(QT_TILES) for c in range(2) if (i + 1) * P > c * BANK]
EXP_PIECES = [(j, max(j * P, c * BANK), BANK * (c + 1) - max(j * P, c * BANK))
              for j in range(QT_TILES) for c in range(2) if BANK * (c + 1) > j * P]
PIECES = len(MAX_PIECES)


def attend(nc, consts, q_dram, k_dram, v_all, attended):
    LAG, NS, NP = 2, 3, 4
    with ExitStack() as ctx:
        def sb(name, shape, dt):
            return ctx.enter_context(nc.sbuf_tensor(name, shape, dt))

        def ps(name, shape, dt=F32):
            return ctx.enter_context(nc.psum_tensor(name, shape, dt))

        def sem(name):
            return ctx.enter_context(nc.semaphore(name))

        identf = sb("a_identf", [P, P], F32)
        identb = sb("a_identb", [P, P], BF16)
        future = sb("a_future", [P, P], BF16)
        qt = sb("a_qt", [KROWS, BATCH * HEADS, SEQ], BF16)
        kt = sb("a_kt", [KROWS, GROUPS, SEQ], BF16)
        vg = sb("a_vg", [P, QT_TILES, 2 * HD], F32)
        probs = [sb(f"a_probs{i}", [P, BANK], F32) for i in range(NP)]
        piecemax = sb("a_piecemax", [P, GROUP, PIECES], F32)
        shift = sb("a_shift", [P, GROUP, QT_TILES], F32)
        shiftb = sb("a_shiftb", [P, P // (GROUP * QT_TILES), GROUP, QT_TILES], BF16)
        shiftT = sb("a_shiftT", [SHIFT_ROWS * GROUP * QT_TILES, P], BF16)
        osb = sb("a_osb", [P, SEQ], F32)
        rsum = sb("a_rsum", [P, QT_TILES, GROUP], F32)

        mscore = [ps(f"a_mscore{i}", [P, BANK]) for i in range(2)]
        score = [ps(f"a_score{i}", [P, BANK]) for i in range(NS)]
        oT = ps("a_oT", [P, 2 * BANK])
        misc = ps("a_misc", [P, BANK])

        s_const = sem("a_const")
        q_in = sem("a_q_in")
        mscored = sem("a_mscored")
        reduced = sem("a_reduced")
        s_blank = sem("a_blank")
        s_fin = sem("a_fin")
        shifts_ok = sem("a_shifts_ok")
        shiftT_ok = sem("a_shiftT_ok")
        shift_in = sem("a_shift_in")
        scored = sem("a_scored")
        expd = sem("a_expd")
        pv = sem("a_pv")
        vg_ok = sem("a_vg_ok")
        misc_shift = sem("a_misc_shift")
        misc_o = sem("a_misc_o")
        osb_ok = sem("a_osb_ok")
        s_rsum = sem("a_rsum")
        out_ok = sem("a_out_ok")

        PG = PIECES * GROUP
        NCONST = 5

        def wait(eng, s, value):
            if not isinstance(value, int) or value > 0:
                eng.wait_ge(s, value)

        block = ctx.enter_context(nc.Block())

        @block.sync
        def _(sp):
            sp.dma_start(identf[:, :], consts["identf"]).then_inc(s_const, 16)
            sp.dma_start(identb[:, :], consts["identb"]).then_inc(s_const, 16)
            sp.dma_start(future[:, :], consts["future"]).then_inc(s_const, 16)
            sp.dma_start(kt[PROWS:KROWS, :, :], consts["key_rows"]).then_inc(s_const, 16)
            sp.dma_start(qt[PROWS:KROWS, :, :], consts["query_rows"]).then_inc(s_const, 16)
            for b in range(BATCH):
                sp.dma_start(kt[0:PROWS, b * KV_HEADS:(b + 1) * KV_HEADS, :],
                             k_dram[:, b * KV_HEADS:(b + 1) * KV_HEADS, :]).then_inc(q_in, 16)
                sp.dma_start(qt[0:PROWS, b * HEADS:(b + 1) * HEADS, :],
                             q_dram[:, b * HEADS:(b + 1) * HEADS, :]).then_inc(q_in, 16)
                sp.wait_ge(q_in, 32 * (b + 1))
            with sp.Fori(0, GROUPS) as n:
                sp.wait_ge(shiftT_ok, n + 1)
                R = GROUP * QT_TILES
                for s in range(SHIFT_ROWS):
                    sp.dma_start(qt[PROWS + s:PROWS + s + 1, bass.ds(n * GROUP, GROUP), :].rearrange(
                        "o h (i q) -> o (h i) q", q=P), shiftT[s * R:(s + 1) * R, :]).then_inc(shift_in, 16)
            sp.wait_ge(shift_in, 16 * SHIFT_ROWS * GROUPS)

        @block.gpsimd
        def _(pool):
            def group(n):
                wait(pool, pv, PG * n)
                pool.tensor_copy(vg[:, :, :].rearrange("p j d -> p (j d)"),
                                 v_all[:, n, :, :].rearrange("p j d -> p (j d)")).then_inc(vg_ok, 1)

            group(0)
            with pool.Fori(1, GROUPS) as n:
                group(n)

        @block.tensor
        def _(pe):
            def max_piece(n, hh, t):
                i, k0, w = MAX_PIECES[t]
                last = k0 + w == (i + 1) * P
                wait(pe, reduced, PG * n + PIECES * hh + t - 1)
                o = mscore[t % 2][:, 0:w]
                mm = pe.matmul(o, qt[:, n * GROUP + hh, i * P:(i + 1) * P], kt[:, n, k0:k0 + w],
                               start=True, stop=True)
                if last:
                    mm = pe.matmul(mscore[t % 2][:, w - P:w], identb[:, :], future[:, :], start=False,
                                   stop=True, skip_group_check=True)
                mm.then_inc(mscored, 1)

            def exp_piece(n, hh, t):
                j, q0, w = EXP_PIECES[t]
                if hh == 0 and t == 0:
                    pe.wait_ge(shift_in, 16 * SHIFT_ROWS * (n + 1))
                wait(pe, expd, PG * n + PIECES * hh + t - NS + 1)
                mm = pe.matmul(score[t % NS][:, 0:w], kt[:, n, j * P:(j + 1) * P],
                               qt[:, n * GROUP + hh, q0:q0 + w], start=True, stop=True)
                if q0 == j * P:
                    mm = pe.matmul(score[t % NS][:, 0:P], future[:, :], identb[:, :], start=False,
                                   stop=True, skip_group_check=True)
                mm.then_inc(scored, 1)

            def v_piece(n, hh, t):
                j, q0, w = EXP_PIECES[t]
                if hh == 0 and t == 0:
                    pe.wait_ge(vg_ok, n + 1)
                    wait(pe, osb_ok, n)
                pe.wait_ge(expd, PG * n + PIECES * hh + t + 1)
                c = q0 // BANK
                pe.matmul(oT[2 * HD * hh:2 * HD * (hh + 1), q0:q0 + w], vg[:, j, :], probs[t % NP][:, 0:w],
                          start=(j == 0), stop=(j == (BANK * (c + 1)) // P - 1),
                          skip_group_check=True).then_inc(pv, 1)

            def turn_shifts(n):
                pe.wait_ge(shifts_ok, n + 1)
                wait(pe, out_ok, 2 * (n - 1))
                pe.transpose(misc[:, 0:P // 2].bitcast(BF16),
                             shiftb[:, :, :, :].rearrange("p s h i -> p (s h i)"),
                             identb[:, :]).then_inc(misc_shift, 1)

            def turn_out(n, c):
                pe.wait_ge(osb_ok, n + 1)
                if c == 0:
                    pe.wait_ge(shiftT_ok, n + 2 if not isinstance(n, int) or n + 1 < GROUPS else n + 1)
                else:
                    pe.wait_ge(out_ok, 2 * n + 1)
                for r in range(BANK // P):
                    mm = pe.transpose(misc[:, r * P:(r + 1) * P],
                                      osb[:, c * BANK + r * P:c * BANK + (r + 1) * P], identf[:, :])
                mm.then_inc(misc_o, 1)

            def group(n, more, before):
                for hh in range(GROUP):
                    for t in range(PIECES + LAG):
                        if t < PIECES:
                            exp_piece(n, hh, t)
                            if more:
                                max_piece(n + 1, hh, t)
                        if before and hh == 0 and t == 5:
                            turn_out(n - 1, 0)
                        if before and hh == 0 and t == 8:
                            turn_out(n - 1, 1)
                        if t >= LAG:
                            v_piece(n, hh, t - LAG)
                if more:
                    turn_shifts(n + 1)

            pe.wait_ge(s_const, 16 * NCONST)
            pe.wait_ge(q_in, 32 * BATCH)
            for hh in range(GROUP):
                for t in range(PIECES):
                    max_piece(0, hh, t)
            turn_shifts(0)
            group(0, True, False)
            with pe.Fori(1, GROUPS - 1) as n:
                group(n, True, True)
            group(GROUPS - 1, False, True)
            turn_out(GROUPS - 1, 0)
            turn_out(GROUPS - 1, 1)

        @block.scalar
        def _(act):
            def group(n):
                for hh in range(GROUP):
                    for t in range(PIECES):
                        w = EXP_PIECES[t][2]
                        act.wait_ge(scored, PG * n + PIECES * hh + t + 1)
                        wait(act, pv, PG * n + PIECES * hh + t - NP + 1)
                        act.activation(probs[t % NP][:, 0:w], score[t % NS][:, 0:w], ACT.Exp).then_inc(expd, 1)

            group(0)
            with act.Fori(1, GROUPS) as n:
                group(n)

        @block.vector
        def _(dve):
            def reduce_piece(n, hh, t):
                dve.wait_ge(mscored, PG * n + PIECES * hh + t + 1)
                if hh == 0 and t == 0:
                    wait(dve, s_fin, 4 * n)
                dve.tensor_reduce(piecemax[:, hh, t:t + 1], mscore[t % 2][:, 0:MAX_PIECES[t][2]], AX.X,
                                  ALU.max, negate=True).then_inc(reduced, 1)

            def finish_shifts(n):
                H = QT_TILES // 2
                dve.wait_ge(reduced, PG * (n + 1))
                two = piecemax[:, :, H:PIECES].rearrange("p h (i c) -> p h i c", c=2)
                dve.tensor_copy(shift[:, :, 0:H], piecemax[:, :, 0:H]).then_inc(s_fin, 1)
                dve.tensor_tensor(shift[:, :, H:QT_TILES], two[:, :, :, 0], two[:, :, :, 1],
                                  ALU.min).then_inc(s_fin, 1)
                dve.wait_ge(s_fin, 4 * n + 2)
                wait(dve, misc_shift, n)
                dve.tensor_copy(shiftb[:, 0, :, :], shift[:, :, :]).then_inc(s_fin, 1)
                dve.wait_ge(s_fin, 4 * n + 3)
                dve.tensor_tensor(shiftb[:, 1, :, :], shift[:, :, :], shiftb[:, 0, :, :],
                                  ALU.subtract).then_inc(s_fin, 1)
                dve.wait_ge(s_fin, 4 * n + 4)
                dve.sem_inc(shifts_ok, 1)

            def copy_shifts(n):
                dve.wait_ge(misc_shift, n + 1)
                wait(dve, shift_in, 16 * SHIFT_ROWS * n)
                dve.tensor_copy(shiftT[:, :], misc[:, 0:P // 2].bitcast(BF16)[
                    0:SHIFT_ROWS * GROUP * QT_TILES, 0:P]).then_inc(shiftT_ok, 1)

            def copy_sums(n):
                dve.wait_ge(pv, PG * (n + 1))
                wait(dve, misc_o, 2 * n)
                dve.tensor_copy(osb[:, :], oT[:, :]).then_inc(osb_ok, 1)

            def write_out(n, c):
                dve.wait_ge(misc_o, 2 * n + c + 1)
                H = BANK // P
                m = misc[:, :].rearrange("p (i h d) -> p i h d", i=H, h=GROUP)
                rs = rsum[:, c * H:(c + 1) * H, :]
                dve.reciprocal(rs, m[:, :, :, HD]).then_inc(s_rsum, 1)
                dve.wait_ge(s_rsum, 2 * n + c + 1)
                for r in range(H):
                    d = attended[:, c * H + r, bass.ds(n * GROUP * HD, GROUP * HD)]
                    last = dve.tensor_tensor(d.rearrange("p (h d) -> p h d", h=GROUP), m[:, r, :, 0:HD],
                                             rsum[:, c * H + r, :].rearrange("p (h o) -> p h o", o=1)
                                             .to_broadcast([P, GROUP, HD]), ALU.mult)
                last.then_inc(out_ok, 1)

            def group(n, more, before):
                for hh in range(GROUP):
                    for t in range(PIECES):
                        if before and hh == 0 and t == 6:
                            write_out(n - 1, 0)
                        if before and hh == 0 and t == 9:
                            write_out(n - 1, 1)
                        if more:
                            reduce_piece(n + 1, hh, t)
                if more:
                    finish_shifts(n + 1)
                    copy_shifts(n + 1)
                copy_sums(n)

            dve.memset(shiftb[:, SHIFT_ROWS:, :, :], 0.0).then_inc(s_blank, 1)
            dve.wait_ge(s_blank, 1)
            for hh in range(GROUP):
                for t in range(PIECES):
                    reduce_piece(0, hh, t)
            finish_shifts(0)
            copy_shifts(0)
            group(0, True, False)
            with dve.Fori(1, GROUPS - 1) as n:
                group(n, True, True)
            group(GROUPS - 1, False, True)
            write_out(GROUPS - 1, 0)
            write_out(GROUPS - 1, 1)
            dve.wait_ge(out_ok, 2 * GROUPS)


def project_out(nc, X, Wo, attended, consts, out_dram=None):
    with ExitStack() as ctx:
        def sb(name, shape, dt):
            return ctx.enter_context(nc.sbuf_tensor(name, shape, dt))

        def ps(name, shape, dt=F32):
            return ctx.enter_context(nc.psum_tensor(name, shape, dt))

        def sem(name):
            return ctx.enter_context(nc.semaphore(name))

        identf = sb("o_identf", [P, P], F32)
        wraw = sb("o_wraw", [P, KD, D], F32)
        whi = sb("o_whi", [P, KD, D], F32R)
        wlo = sb("o_wlo", [P, KD, D], F32R)
        ahi = sb("o_ahi", [P, 2, KD, P], F32R)
        alo = sb("o_alo", [P, 2, KD, P], F32R)
        turn = [ps(f"o_turn{i}", [P, BANK]) for i in range(2)]
        acc = [ps(f"o_acc{i}", [P, BANK]) for i in range(2)]
        s_w = sem("o_w")
        s_whi = sem("o_whi")
        s_wlo = sem("o_wlo")
        s_turn = sem("o_turned")
        s_hi = sem("o_hi")
        s_lo = sem("o_lo")
        s_mm = sem("o_mm")
        s_add = sem("o_add")
        s_out = sem("o_out")
        block = ctx.enter_context(nc.Block())

        @block.sync
        def _(sp):
            sp.dma_start(identf[:, :], consts["identf"]).then_inc(s_w, 16)
            sp.dma_start(wraw[:, :, :], Wo.rearrange("(k p) n -> p k n", p=P)).then_inc(s_w, 16)
            if out_dram is not None:
                sp.wait_ge(s_add, TILES)
                sp.dma_start(out_dram.rearrange("(t p) d -> p t d", p=P), X[:, :, :]).then_inc(s_out, 16)
                sp.wait_ge(s_out, 16)

        @block.tensor
        def _(pe):
            def turn_tile(t):
                b, i = t // QT_TILES, t % QT_TILES
                if t >= 2:
                    pe.wait_ge(s_lo, t - 1)
                for k in range(KD):
                    src = attended[:, i, b * D + k * P:b * D + (k + 1) * P]
                    mm = pe.transpose(turn[t % 2][:, k * P:(k + 1) * P], src, identf[:, :])
                mm.then_inc(s_turn, 1)

            pe.wait_ge(s_w, 32)
            turn_tile(0)
            pe.wait_ge(s_wlo, 1)
            for t in range(TILES):
                if t + 1 < TILES:
                    turn_tile(t + 1)
                pe.wait_ge(s_lo, t + 1)
                if t >= 2:
                    pe.wait_ge(s_add, t - 1)
                n = 0
                for k in range(KD):
                    for a, w in ((ahi, whi), (ahi, wlo), (alo, whi)):
                        mm = pe.matmul(acc[t % 2][:, 0:D], a[:, t % 2, k, :], w[:, k, :],
                                       start=(n == 0), stop=(n == 3 * KD - 1))
                        n += 1
                mm.then_inc(s_mm, 1)

        @block.scalar
        def _(act):
            act.wait_ge(s_w, 32)
            act.copy(whi[:, :, :], wraw[:, :, :]).then_inc(s_whi, 1)
            for t in range(TILES):
                act.wait_ge(s_turn, t + 1)
                if t >= 2:
                    act.wait_ge(s_mm, t - 1)
                act.copy(ahi[:, t % 2, :, :], turn[t % 2][:, 0:D].rearrange("p (k q) -> p k q", k=KD)).then_inc(s_hi, 1)

        @block.vector
        def _(dve):
            dve.wait_ge(s_whi, 1)
            dve.tensor_tensor(wlo[:, :, :], wraw[:, :, :], whi[:, :, :].bitcast(F32),
                              ALU.subtract).then_inc(s_wlo, 1)

            def add(t):
                dve.wait_ge(s_mm, t + 1)
                dve.tensor_tensor(X[:, t, :], acc[t % 2][:, 0:D], X[:, t, :], ALU.add).then_inc(s_add, 1)

            for t in range(TILES):
                dve.wait_ge(s_hi, t + 1)
                dve.tensor_tensor(alo[:, t % 2, :, :], turn[t % 2][:, 0:D].rearrange("p (k q) -> p k q", k=KD),
                                  ahi[:, t % 2, :, :].bitcast(F32), ALU.subtract).then_inc(s_lo, 1)
                if t:
                    add(t - 1)
            add(TILES - 1)
            dve.wait_ge(s_add, TILES)


def constants():
    bf = np.dtype("bfloat16")
    r = np.arange(P)
    c = {
        "identf": np.eye(P, dtype=np.float32),
        "before": (r[:, None] < r[None, :]).astype(bf),
        "onesb": np.ones((P, P), bf),
        "iota": np.broadcast_to(np.arange(EXPERTS, dtype=np.float32), (P, TILES, EXPERTS)).copy(),
        "restart": np.broadcast_to((np.arange(TILES) > 0).astype(np.float32), (P, EXPERTS, TILES)).reshape(
            P, EXPERTS * TILES).copy(),
    }
    c["slot_iota"] = np.broadcast_to(np.arange(CAP, dtype=np.float16), (P, CAP)).copy()
    c["spare"] = (TOKENS + np.arange(ROWTILES)[None, :] * P + r[:, None]).astype(np.float32)
    facts = np.zeros((P, EXPERTS, TILES, FACTS), bf)
    facts[:, :, :, 0] = 1
    facts[:, :, :, 1] = r[:, None, None]
    facts[:, :, :, 2] = (P * np.arange(TILES))[None, None, :]
    c["facts"] = facts
    pos = np.arange(SEQ, dtype=np.float32)
    theta = (1.0 / np.float32(10000.0) ** (np.arange(HALF, dtype=np.float32) / HALF)).astype(np.float32)
    angle = np.outer(pos, theta).astype(np.float32)
    cos, sin = (np.tile(f(angle).astype(np.float32).T, (P // HALF, 1)) for f in (np.cos, np.sin))
    scale = np.float32(HD ** -0.5)
    c["rotary"] = np.stack([cos * scale, sin * scale, cos, sin], axis=1)
    c["identb"] = np.eye(P).astype(bf)
    c["future"] = np.where(r[None, :] > r[:, None], NEG, 0.0).astype(bf)
    slopes = (2.0 ** (-8.0 * np.arange(1, HEADS + 1, dtype=np.float32) / HEADS)).astype(np.float32)
    parts, rest = [], slopes
    for _ in range(3):
        parts.append(rest.astype(bf))
        rest = rest - parts[-1].astype(np.float32)
    q = np.zeros((SHIFT_ROWS + ALIBI_ROWS, BATCH, HEADS, SEQ), bf)
    q[SHIFT_ROWS:] = np.repeat(np.stack(parts), 2, axis=0)[:, None, :, None]
    c["query_rows"] = q.reshape(SHIFT_ROWS + ALIBI_ROWS, BATCH * HEADS, SEQ)
    k = np.ones((SHIFT_ROWS + ALIBI_ROWS, GROUPS, SEQ), bf)
    k[SHIFT_ROWS::2] = (pos // P * P).astype(bf)
    k[SHIFT_ROWS + 1::2] = (pos % P).astype(bf)
    c["key_rows"] = k
    return c


def program(nc, ins, consts, out):
    x = ins["L0_attn_x"].rearrange("b t d -> (b t) d")
    o = out.rearrange("b t d -> (b t) d")
    with ExitStack() as ctx:
        X = ctx.enter_context(nc.sbuf_tensor("X", [P, TILES, D], F32))
        xn_dram = nc.dram_tensor("normalised", [TOKENS, D], F32).ap()
        acc = nc.dram_tensor("accumulated", [TOKENS + CAP, D], F32).ap()
        moe = (ins["L0_ffn_Wg"], ins["L0_ffn_w1"], ins["L0_ffn_w2"], xn_dram, acc, consts)
        ffn(nc, X, x, *moe, None, "a")
        with ExitStack() as mid:
            v_all = mid.enter_context(nc.sbuf_tensor("v_all", [P, GROUPS, QT_TILES, 2 * HD], F32))
            attended = mid.enter_context(nc.sbuf_tensor("attended", [P, QT_TILES, GROUPS * GROUP * HD], F32))
            q_dram = nc.dram_tensor("q_parts", [PROWS, BATCH * HEADS, SEQ], BF16).ap()
            k_dram = nc.dram_tensor("k_parts", [PROWS, GROUPS, SEQ], BF16).ap()
            project(nc, X, acc[0:TOKENS, :], ins["L0_attn_Wq"], ins["L0_attn_Wk"], ins["L0_attn_Wv"], consts, q_dram, k_dram, v_all)
            attend(nc, consts, q_dram, k_dram, v_all, attended)
            project_out(nc, X, ins["L0_attn_Wo"], attended, consts, o if MODE == "attn" else None)
        if MODE == "attn":
            return
        ffn(nc, X, None, *moe, o, "b")


MODE = "all"
_INS = ['L0_attn_x', 'L0_attn_Wq', 'L0_attn_Wk', 'L0_attn_Wv', 'L0_attn_Wo', 'L0_ffn_Wg', 'L0_ffn_w1', 'L0_ffn_w2']


def kernel(**inputs):
    import concourse.bacc as _bacc
    from concourse.bass_utils import run_bass_kernel_spmd as _run

    nc = _bacc.Bacc("TRN2", target_bir_lowering=False, num_devices=1)
    arrays, args, consts = {}, {}, {}
    for name in _INS:
        a = np.ascontiguousarray(inputs[name])
        if name in ("L0_attn_Wq", "L0_attn_Wk"):
            a = np.ascontiguousarray(a.reshape(D, -1, 2, HALF).transpose(0, 2, 1, 3).reshape(D, -1))
        arrays[f"in_{name}"] = a
        args[name] = nc.dram_tensor(f"in_{name}", a.shape, mybir.dt.from_np(a.dtype), kind="ExternalInput").ap()
    for name, a in constants().items():
        arrays[f"const_{name}"] = a
        consts[name] = nc.dram_tensor(f"const_{name}", a.shape, mybir.dt.from_np(a.dtype), kind="ExternalInput").ap()
    out = nc.dram_tensor("out_0", (BATCH, SEQ, D), F32, kind="ExternalOutput").ap()
    program(nc, args, consts, out)
    r = _run(nc, [arrays], core_ids=[0])
    return r.results[0]["out_0"]
```

```python
from contextlib import ExitStack

import numpy as np

import concourse.bass as bass
from concourse import mybir

F32 = mybir.dt.float32
F32R = mybir.dt.float32r
BF16 = mybir.dt.bfloat16
F16 = mybir.dt.float16
U32 = mybir.dt.uint32
ALU = mybir.AluOpType
ACT = mybir.ActivationFunctionType
AX = mybir.AxisListType

P = 128
BATCH, SEQ, D = 2, 1024, 256
TOKENS = BATCH * SEQ
TILES = TOKENS // P
KD = D // P
EXPERTS, TOPK, DFF = 8, 2, 1024
CAP = -(-5 * TOKENS * TOPK // (4 * EXPERTS))
ROWTILES = CAP // P
KF = DFF // P
HALFCAP = CAP // 2
EPS = 1e-5
BANK = 512
HEADS, KV_HEADS, HD = 16, 4, 16
HALF = HD // 2
GROUP = HEADS // KV_HEADS
NEG = -1e30
FACTS, ROWFACTS = 6, 3
LNG = 4
LNT = TILES // LNG


def normalise(dve, step, X, stats, mv, veps, sd, rstd, nwt, nmr, s_var, s_sd, s_nmr, g):
    a, b = g * LNT, (g + 1) * LNT
    for t in range(a, b):
        step(dve.bn_stats(stats[:, t, :], X[:, t, :]), t == b - 1)
    for t in range(a, b):
        step(dve.bn_aggr(mv[:, t, :], stats[:, t, :]), t == b - 1)
    dve.tensor_scalar(veps[:, a:b], mv[:, a:b, 1], EPS, None, ALU.add).then_inc(s_var, 1)
    dve.wait_ge(s_var, g + 1)
    step(dve.tensor_scalar(nwt[:, a:b], veps[:, a:b], -0.5, None, ALU.mult), False)
    dve.wait_ge(s_sd, g + 1)
    step(dve.reciprocal(rstd[:, a:b], sd[:, a:b]))
    step(dve.tensor_tensor(sd[:, a:b], rstd[:, a:b], rstd[:, a:b], ALU.mult))
    step(dve.tensor_tensor(sd[:, a:b], sd[:, a:b], nwt[:, a:b], ALU.mult))
    step(dve.scalar_tensor_tensor(rstd[:, a:b], sd[:, a:b], 1.5, rstd[:, a:b], ALU.add, ALU.mult))
    dve.scalar_tensor_tensor(nmr[:, a:b], mv[:, a:b, 0], -1.0, rstd[:, a:b],
                             ALU.mult, ALU.mult).then_inc(s_nmr, 1)


def root(act, veps, sd, s_var, s_sd, g):
    act.wait_ge(s_var, g + 1)
    act.activation(sd[:, g * LNT:(g + 1) * LNT], veps[:, g * LNT:(g + 1) * LNT], ACT.Sqrt).then_inc(s_sd, 1)


def scale_row_tile(act, X, rstd, nmr, xn, s_nmr, s_xn, t):
    if t % LNT == 0:
        act.wait_ge(s_nmr, t // LNT + 1)
    act.activation(xn[:, t, :], X[:, t, :], ACT.Identity, bias=nmr[:, t:t + 1],
                   scale=rstd[:, t:t + 1]).then_inc(s_xn, 1)


def scale_rows(act, X, rstd, nmr, xn, s_nmr, s_xn, g):
    for t in range(g * LNT, (g + 1) * LNT):
        scale_row_tile(act, X, rstd, nmr, xn, s_nmr, s_xn, t)


def ffn(nc, X, x_dram, Wg, w1, w2, xn_dram, acc, consts, out_dram, tag):
    first = x_dram is not None
    with ExitStack() as ctx:
        def sb(name, shape, dt):
            return ctx.enter_context(nc.sbuf_tensor(f"{name}_{tag}", shape, dt))

        def ps(name, shape, dt=F32):
            return ctx.enter_context(nc.psum_tensor(f"{name}_{tag}", shape, dt))

        def sem(name):
            return ctx.enter_context(nc.semaphore(f"{name}_{tag}"))

        ET = EXPERTS * TILES
        HT = TILES // 2
        NX = 4
        identf = sb("identf", [P, P], F32)
        before = sb("before", [P, P], BF16)
        onesb = sb("onesb", [P, P], BF16)
        iota = sb("iota", [P, TILES, EXPERTS], F32)
        restart = sb("restart", [P, ET], F32)
        slot_iota = sb("slot_iota", [P, CAP], F16)
        zeros = sb("zeros", [P, ROWTILES * FACTS], BF16)
        spare = sb("spare", [P, ROWTILES], F32)
        wg = sb("wg", [P, KD, EXPERTS], F32)
        xn = sb("xn", [P, TILES, D], F32)
        stats = sb("stats", [P, TILES, 6], F32)
        mv = sb("mv", [P, TILES, 2], F32)
        veps = sb("veps", [P, TILES], F32)
        sd = sb("sd", [P, TILES], F32)
        rstd = sb("rstd", [P, TILES], F32)
        nwt = sb("nwt", [P, TILES], F32)
        nmr = sb("nmr", [P, TILES], F32)
        xt = sb("xt", [P, NX, D], F32)
        logits = sb("logits", [P, TILES, EXPERTS], F32)
        top = sb("top", [P, TILES, 8], F32)
        topi = sb("topi", [P, TILES, 8], U32)
        shifted = sb("shifted", [P, TILES, EXPERTS], F32)
        exps = sb("exps", [P, TILES, EXPERTS], F32)
        gap = sb("gap", [P, TILES], F32)
        egap = sb("egap", [P, TILES], F32)
        zsum = sb("zsum", [P, TILES], F32)
        gates = sb("gates", [P, TOPK, TILES], F32)
        expert = sb("expert", [P, TOPK, TILES], F32)
        onehot = sb("onehot", [P, TOPK, TILES, EXPERTS], F32)
        count = sb("count", [P, EXPERTS, TILES], F32)
        countb = sb("countb", [P, ET], BF16)
        upto = sb("upto", [P, ET], F32)
        priorb = sb("priorb", [P, ET], BF16)
        place = sb("place", [P, ET], F32)
        weighted = sb("weighted", [P, TOPK, TILES, EXPERTS], F32)
        weight = sb("weight", [P, ET], F32)
        wrest = sb("wrest", [P, ET], F32)
        facts = sb("facts", [P, EXPERTS, TILES, FACTS], BF16)
        takes = sb("takes", [P, TILES, CAP], BF16)
        learnt = sb("learnt", [P, ROWTILES, FACTS], F32)
        nidx = sb("nidx", [P, 3, ROWTILES], F32)
        row_in = sb("row_in", [P, ROWTILES], U32)
        nrow_out = sb("nrow_out", [P, ROWTILES], U32)
        nscale = sb("nscale", [P, ROWTILES], F32)
        row_out = sb("row_out", [P, ROWTILES], U32)
        rscale = sb("rscale", [P, ROWTILES], F32)
        w1raw = sb("w1raw", [P, KD, DFF], F32)
        w2raw = sb("w2raw", [P, KF, D], F32)
        w1hi = sb("w1hi", [P, KD, DFF], F32R)
        w1lo = sb("w1lo", [P, KD, DFF], F32R)
        w2hi = sb("w2hi", [P, KF, D], F32R)
        w2lo = sb("w2lo", [P, KF, D], F32R)
        xe = sb("xe", [P, ROWTILES, D], F32)
        xthi = sb("xthi", [P, KD * CAP], F32R)
        xtlo = sb("xtlo", [P, KD * CAP], F32R)
        hhi = sb("hhi", [P, KF, CAP], F32R)
        hlo = sb("hlo", [P, KF, CAP], F32R)
        ysb = sb("ysb", [P, ROWTILES, D], F32)

        up = [ps(f"up{i}", [P, BANK]) for i in range(4)]
        turn = ps("turn", [P, BANK])
        learn = ps("learn", [P, BANK])
        down = [ps(f"down{i}", [P, BANK]) for i in range(2)]

        lbank = [down[0], turn, learn, down[1]]

        s_const = sem("s_const")
        s_gates_in = sem("s_gates_in")
        s_x = [sem(f"s_x{g}") for g in range(LNG)] if first else None
        s_acc = sem("s_acc")
        s_vec = sem("s_vec")
        s_var = sem("s_var")
        s_sd = sem("s_sd")
        s_nmr = sem("s_nmr")
        s_xn = sem("s_xn")
        s_xnout = sem("s_xnout")
        s_passed = sem("passed")
        s_rt = sem("s_rt")
        s_xt = sem("s_xt")
        s_gate = sem("s_gate")
        s_exp = sem("s_exp")
        s_count = sem("s_count")
        s_pos = sem("s_pos")
        s_facts = sem("s_facts")
        s_first = sem("s_first")
        s_firstout = sem("s_firstout")
        takes_ok = sem("takes_ok")
        learn_ok = sem("learn_ok")
        learnt_ok = sem("learnt_ok")
        s_idx = sem("s_idx")
        rows_ok = sem("rows_ok")
        cur_ok = sem("cur_ok")
        w1_in = sem("w1_in")
        w2_in = sem("w2_in")
        xe_in = [sem(f"xe_in{r}") for r in range(ROWTILES)]
        w1hi_ok = sem("w1hi_ok")
        w1lo_ok = sem("w1lo_ok")
        w2hi_ok = sem("w2hi_ok")
        w2lo_ok = sem("w2lo_ok")
        turned = sem("turned")
        xthi_ok = sem("xthi_ok")
        xtlo_ok = sem("xtlo_ok")
        up_ok = sem("up_ok")
        hhi_ok = sem("hhi_ok")
        hlo_ok = sem("hlo_ok")
        down_ok = sem("down_ok")
        y_ok = sem("y_ok")
        added = sem("added")
        s_out = sem("s_out") if out_dram is not None else None

        w1_v = w1.rearrange("e (k p) f -> e p k f", p=P)
        w2_v = w2.rearrange("e (k p) d -> e p k d", p=P)
        tokens = lambda a: a.rearrange("(t p) d -> p t d", p=P)
        NCONST = 8
        TURNS = [(r, min(r + 2, ROWTILES)) for r in range(0, ROWTILES, 2)]
        NT = len(TURNS)
        FIRST_BANKS = [up[3], turn, up[2]]

        def turned_view(bank, i):
            a, b = TURNS[i]
            return bank[:, 0:KD * (b - a) * P].rearrange("p (k c) -> p k c", k=KD)

        def part(x, i):
            a, b = TURNS[i]
            return x.rearrange("p (k c) -> p k c", k=KD)[:, :, a * P:b * P]

        NH = 2 * KF
        ACCS = 2
        LEARN_AFTER = {1: (0, 1), 2: (2, 3), 3: (4,)}
        LEARNT = 4

        def wait(eng, s, value):
            if not isinstance(value, int) or value > 0:
                eng.wait_ge(s, value)

        block = ctx.enter_context(nc.Block())

        @block.sync
        def _(sp):
            def load_x(g):
                sp.dma_start(X[:, g * LNT:(g + 1) * LNT, :],
                             tokens(x_dram)[:, g * LNT:(g + 1) * LNT, :]).then_inc(s_x[g], 16)

            if first:
                load_x(0)
            sp.dma_start(identf[:, :], consts["identf"]).then_inc(s_gates_in, 16)
            sp.dma_start(wg[:, :, :], Wg.rearrange("(k p) e -> p k e", p=P)).then_inc(s_gates_in, 16)
            if first:
                for g in range(1, LNG):
                    load_x(g)
            for dst, src in ((before[:, :], consts["before"]), (onesb[:, :], consts["onesb"]),
                             (iota[:, :, :], consts["iota"]), (restart[:, :], consts["restart"]),
                             (slot_iota[:, :], consts["slot_iota"]), (spare[:, :], consts["spare"]),
                             (zeros[:, :], consts["zeros"])):
                sp.dma_start(dst, src).then_inc(s_const, 16)
            sp.dma_start(facts[:, :, :, :], consts["facts"]).then_inc(s_const, 16)
            sp.dma_start(w1raw[:, :, :], w1_v[0]).then_inc(w1_in, 16)
            sp.dma_start(w2raw[:, :, :], w2_v[0]).then_inc(w2_in, 16)
            if first:
                sp.dma_start(acc[0:TOKENS, :], x_dram).then_inc(s_acc, 16)
                sp.dma_start(acc[TOKENS:TOKENS + CAP, :], x_dram[0:CAP, :]).then_inc(s_acc, 16)
            else:
                sp.dma_start(tokens(acc[0:TOKENS, :]), X[:, :, :]).then_inc(s_acc, 16)
                sp.dma_start(tokens(acc[TOKENS:TOKENS + CAP, :]), X[:, 0:ROWTILES, :]).then_inc(s_acc, 16)
            for g in range(LNG):
                sp.wait_ge(s_xn, LNT * (g + 1))
                sp.dma_start(tokens(xn_dram)[:, g * LNT:(g + 1) * LNT, :],
                             xn[:, g * LNT:(g + 1) * LNT, :]).then_inc(s_xnout, 16)
            with sp.Fori(1, EXPERTS) as e:
                sp.wait_ge(w1lo_ok, KD * e)
                sp.dma_start(w1raw[:, :, :], w1_v[e]).then_inc(w1_in, 16)
                sp.wait_ge(w2lo_ok, KF * e)
                sp.dma_start(w2raw[:, :, :], w2_v[e]).then_inc(w2_in, 16)
            sp.wait_ge(added, 16 * ROWTILES * EXPERTS)
            if out_dram is not None:
                sp.dma_start(out_dram, acc[0:TOKENS, :]).then_inc(s_out, 16)
                sp.wait_ge(s_out, 16)

        @block.gpsimd
        def _(pool):
            def gather(e):
                pool.wait_ge(rows_ok, e + 1)
                wait(pool, turned, NT * e)
                pool.sem_inc(s_passed, 1)
                for r in range(ROWTILES):
                    pool.indirect_dma_start(
                        out=xe[:, r, :], out_offset=None, in_=xn_dram[:, :],
                        in_offset=bass.IndirectOffsetOnAxis(ap=row_in[:, r:r + 1], axis=0)).then_inc(xe_in[r], 16)

            def add(e):
                pool.wait_ge(cur_ok, 2 * (e + 1))
                for r in range(ROWTILES):
                    pool.wait_ge(y_ok, ROWTILES * e + r + 1)
                    pool.sem_inc(s_passed, 1)
                    pool.indirect_dma_start(
                        out=acc[:, :], out_offset=bass.IndirectOffsetOnAxis(ap=row_out[:, r:r + 1], axis=0),
                        in_=ysb[:, r, :], in_offset=None, compute_op=ALU.add).then_inc(added, 16)

            pool.wait_ge(s_xnout, 16 * LNG)
            gather(0)
            gather(1)
            pool.wait_ge(s_acc, 16 * ACCS)
            with pool.Fori(1, EXPERTS - 1) as e:
                add(e - 1)
                gather(e + 1)
            add(EXPERTS - 2)
            add(EXPERTS - 1)

        @block.tensor
        def _(pe):
            def turn_tile(t):
                pe.wait_ge(s_xn, t + 1)
                if t >= NX:
                    pe.wait_ge(s_xt, t - NX + 1)
                for k in range(KD):
                    mm = pe.transpose(up[t % NX][:, k * P:(k + 1) * P],
                                      xn[:, t, k * P:(k + 1) * P], identf[:, :])
                mm.then_inc(s_rt, 1)

            def gate_tile(t):
                pe.wait_ge(s_xt, t + 1)
                for k in range(KD):
                    mm = pe.matmul(lbank[t // LNT][:, t * EXPERTS:(t + 1) * EXPERTS],
                                   xt[:, t % NX, k * P:(k + 1) * P],
                                   wg[:, k, :], start=(k == 0), stop=(k == KD - 1))
                mm.then_inc(s_gate, 1)

            pe.wait_ge(s_gates_in, 32)
            AHEAD = 2
            for t in range(AHEAD):
                turn_tile(t)
            for t in range(TILES):
                if t + AHEAD < TILES:
                    turn_tile(t + AHEAD)
                gate_tile(t)
            pe.wait_ge(s_const, 16 * NCONST)
            pe.wait_ge(s_count, 2)
            pe.matmul(down[1][:, 0:ET], before[:, :], countb[:, :], start=True, stop=False)
            pe.matmul(down[1][:, 0:ET], onesb[:, :], priorb[:, :], start=False, stop=True).then_inc(s_pos, 1)

            def learn_first():
                pe.matmul(learn[:, 0:ROWTILES * FACTS], before[:, :], zeros[:, :], start=True, stop=False,
                          skip_group_check=True)
                for t in range(TILES):
                    pe.wait_ge(takes_ok, t + 1)
                    for r in range(ROWTILES):
                        mm = pe.matmul(learn[:, r * FACTS:r * FACTS + ROWFACTS], takes[:, t, r * P:(r + 1) * P],
                                       facts[:, 0, t, 0:ROWFACTS], start=False, stop=(t == TILES - 1),
                                       skip_group_check=True)
                mm.then_inc(s_first, 1)
                pe.wait_ge(s_facts, 1)
                pe.wait_ge(s_firstout, 1)
                for r in range(ROWTILES):
                    for t in range(TILES):
                        mm = pe.matmul(learn[:, r * FACTS + ROWFACTS:(r + 1) * FACTS],
                                       takes[:, t, r * P:(r + 1) * P], facts[:, 0, t, ROWFACTS:FACTS],
                                       start=(t == 0), stop=(t == TILES - 1))
                mm.then_inc(learn_ok, 1)

            def learn_rows(e, r):
                if r == 0:
                    pe.wait_ge(takes_ok, TILES * (e + 1))
                    wait(pe, learnt_ok, e)
                for t in range(TILES):
                    mm = pe.matmul(learn[:, r * FACTS:(r + 1) * FACTS], takes[:, t, r * P:(r + 1) * P],
                                   facts[:, e, t, :], start=(t == 0), stop=(t == TILES - 1))
                if r == ROWTILES - 1:
                    mm.then_inc(learn_ok, 1)

            def turn_rows(e, i, bank=turn):
                for r in range(*TURNS[i]):
                    pe.wait_ge(xe_in[r], 16 * (e + 1))
                if bank is turn:
                    wait(pe, xtlo_ok, NT * e + i)
                for r in range(*TURNS[i]):
                    for k in range(KD):
                        c = (k * (TURNS[i][1] - TURNS[i][0]) + r - TURNS[i][0]) * P
                        mm = pe.transpose(bank[:, c:c + P], xe[:, r, k * P:(k + 1) * P], identf[:, :])
                mm.then_inc(turned, 1)

            def up_product(e, more):
                pe.wait_ge(xtlo_ok, NT * (e + 1))
                pe.wait_ge(w1lo_ok, KD * (e + 1))
                for f in range(KF):
                    for c in range(2):
                        i = 2 * f + c
                        wait(pe, hlo_ok, NH * e + i - 3)
                        o = up[i % 4][:, 0:HALFCAP]
                        n = 0
                        for k in range(KD):
                            for w, x in ((w1hi, xthi), (w1hi, xtlo), (w1lo, xthi)):
                                a = k * CAP + c * HALFCAP
                                mm = pe.matmul(o, w[:, k, f * P:(f + 1) * P], x[:, a:a + HALFCAP],
                                               start=(n == 0), stop=(n == 3 * KD - 1))
                                n += 1
                        mm.then_inc(up_ok, 1)
                    if more:
                        for r in LEARN_AFTER.get(f, ()):
                            learn_rows(e + 1, r)

            def down_tile(e, r):
                if r >= 2:
                    pe.wait_ge(y_ok, ROWTILES * e + r - 1)
                o = down[r % 2][:, 0:D]
                n = 0
                for f in range(KF):
                    if r == 0:
                        pe.wait_ge(hlo_ok, NH * e + 2 * (f + 1))
                        pe.wait_ge(w2lo_ok, KF * e + f + 1)
                    for h, w in ((hhi, w2hi), (hhi, w2lo), (hlo, w2hi)):
                        mm = pe.matmul(o, h[:, f, r * P:(r + 1) * P], w[:, f, :],
                                       start=(n == 0), stop=(n == 3 * KF - 1))
                        n += 1
                mm.then_inc(down_ok, 1)

            learn_first()
            for i in range(NT):
                turn_rows(0, i, FIRST_BANKS[i])
            up_product(0, True)

            def expert_step(e, more):
                for r in range(ROWTILES):
                    down_tile(e - 1, r)
                    if r < NT:
                        turn_rows(e, r)
                up_product(e, more)

            with pe.Fori(1, EXPERTS - 1) as e:
                expert_step(e, True)
            expert_step(EXPERTS - 1, False)
            for r in range(ROWTILES):
                down_tile(EXPERTS - 1, r)

        @block.scalar
        def _(act):
            def split_w1(e, k):
                if k == 0:
                    act.wait_ge(w1_in, 16 * (e + 1))
                    wait(act, up_ok, NH * e)
                act.copy(w1hi[:, k, :], w1raw[:, k, :]).then_inc(w1hi_ok, 1)

            def copy_turned(t):
                act.wait_ge(s_rt, t + 1)
                if t >= NX:
                    act.wait_ge(s_gate, t - NX + 1)
                act.copy(xt[:, t % NX, :], up[t % NX][:, 0:D]).then_inc(s_xt, 1)

            root(act, veps, sd, s_var, s_sd, 0)
            scale_rows(act, X, rstd, nmr, xn, s_nmr, s_xn, 0)
            root(act, veps, sd, s_var, s_sd, 1)
            for t in range(TILES):
                copy_turned(t)
                ahead = t + LNT - 1
                if LNT <= ahead < TILES and t % LNT:
                    scale_row_tile(act, X, rstd, nmr, xn, s_nmr, s_xn, ahead)
                if t % LNT == LNT - 1 and t + 1 < TILES:
                    scale_row_tile(act, X, rstd, nmr, xn, s_nmr, s_xn, ahead + 1)
                    if ahead + 2 < TILES:
                        root(act, veps, sd, s_var, s_sd, (ahead + 2) // LNT)
                if t % LNT == LNT - 1 and t // LNT - 1 in range(KD):
                    split_w1(0, t // LNT - 1)
            act.wait_ge(s_count, 4)
            act.activation(exps[:, :, :], shifted[:, :, :], ACT.Exp).then_inc(s_exp, 1)
            act.activation(egap[:, :], gap[:, :], ACT.Exp).then_inc(s_exp, 1)

            def split_w2(e, f):
                if f == 0:
                    act.wait_ge(w2_in, 16 * (e + 1))
                    wait(act, down_ok, ROWTILES * e)
                act.copy(w2hi[:, f, :], w2raw[:, f, :]).then_inc(w2hi_ok, 1)

            def split_rows(e, i, bank=turn):
                act.wait_ge(turned, NT * e + i + 1)
                if i == 0:
                    wait(act, up_ok, NH * e)
                act.copy(part(xthi[:, :], i), turned_view(bank, i)).then_inc(xthi_ok, 1)

            def copy_learnt(e):
                act.wait_ge(learn_ok, e + 1)
                wait(act, rows_ok, e)
                a = ROWFACTS if isinstance(e, int) and e == 0 else 0
                act.copy(learnt[:, :, a:], learn[:, 0:ROWTILES * FACTS].rearrange(
                    "p (r f) -> p r f", f=FACTS)[:, :, a:]).then_inc(learnt_ok, 1)

            def relu(e, f):
                for c in range(2):
                    i = 2 * f + c
                    act.wait_ge(up_ok, NH * e + i + 1)
                    if i == 0:
                        wait(act, down_ok, ROWTILES * e)
                    act.activation(hhi[:, f, c * HALFCAP:(c + 1) * HALFCAP], up[i % 4][:, 0:HALFCAP],
                                   ACT.Relu).then_inc(hhi_ok, 1)

            def copy_down(e, r):
                act.wait_ge(down_ok, ROWTILES * e + r + 1)
                if r == 0:
                    act.wait_ge(cur_ok, 2 * (e + 1))
                act.activation(ysb[:, r, :], down[r % 2][:, 0:D], ACT.Copy,
                               scale=rscale[:, r:r + 1]).then_inc(y_ok, 1)

            def up_part(e, more):
                for f in range(KF):
                    relu(e, f)
                    split_w2(e, f)
                    if f == LEARNT and more:
                        copy_learnt(e + 1)

            act.wait_ge(s_first, 1)
            act.copy(learnt[:, :, 0:ROWFACTS], learn[:, 0:ROWTILES * FACTS].rearrange(
                "p (r f) -> p r f", f=FACTS)[:, :, 0:ROWFACTS]).then_inc(s_firstout, 1)
            copy_learnt(0)
            for i in range(NT):
                split_rows(0, i, FIRST_BANKS[i])
            up_part(0, True)

            def expert_step(e, more):
                for r in range(ROWTILES):
                    if r < KD:
                        split_w1(e, r)
                    copy_down(e - 1, r)
                    if r < NT:
                        split_rows(e, r)
                up_part(e, more)

            with act.Fori(1, EXPERTS - 1) as e:
                expert_step(e, True)
            expert_step(EXPERTS - 1, False)
            for r in range(ROWTILES):
                copy_down(EXPERTS - 1, r)

        @block.vector
        def _(dve):
            steps = [0]

            def step(ins, wait=True):
                steps[0] += 1
                ins.then_inc(s_vec, 1)
                if wait:
                    dve.wait_ge(s_vec, steps[0])

            for g in range(LNG):
                if first:
                    dve.wait_ge(s_x[g], 16)
                normalise(dve, step, X, stats, mv, veps, sd, rstd, nwt, nmr, s_var, s_sd, s_nmr, g)
            def rest_w1(e, k):
                dve.wait_ge(w1hi_ok, KD * e + k + 1)
                dve.tensor_tensor(w1lo[:, k, :], w1raw[:, k, :], w1hi[:, k, :].bitcast(F32),
                                  ALU.subtract).then_inc(w1lo_ok, 1)

            dve.wait_ge(s_const, 16 * NCONST)
            for half in range(2):
                a, b = half * HT, (half + 1) * HT
                for g in range(a // LNT, b // LNT):
                    c, d = g * LNT, (g + 1) * LNT
                    dve.wait_ge(s_gate, d)
                    step(dve.tensor_copy(logits[:, c:d, :], lbank[g][:, c * EXPERTS:d * EXPERTS].rearrange(
                        "p (t e) -> p t e", e=EXPERTS)), d == b)
                for t in range(a, b):
                    step(dve.max(top[:, t, :], logits[:, t, :]), t == b - 1)
                for t in range(a, b):
                    step(dve.max_index(topi[:, t, :], top[:, t, :], logits[:, t, :]), t == b - 1)
                step(dve.tensor_copy(expert[:, :, a:b], topi[:, a:b, 0:TOPK].rearrange("p t k -> p k t")))
                for k in range(TOPK):
                    step(dve.tensor_tensor(onehot[:, k, a:b, :], iota[:, a:b, :],
                                           expert[:, k, a:b].rearrange("p (t o) -> p t o", o=1).to_broadcast(
                                               [P, HT, EXPERTS]), ALU.is_equal), k == TOPK - 1)
                step(dve.tensor_tensor(count[:, :, a:b].rearrange("p e t -> p t e"), onehot[:, 0, a:b, :],
                                       onehot[:, 1, a:b, :], ALU.add))
                if half == 0:
                    for k in range(KD):
                        rest_w1(0, k)
            cflat = count[:, :, :].rearrange("p e t -> p (e t)")
            dve.tensor_copy(countb[:, :], cflat).then_inc(s_count, 1)
            step(dve.tensor_tensor_scan(upto[:, :], restart[:, :], cflat, 0.0, ALU.mult, ALU.add))
            dve.tensor_tensor(priorb[:, :], upto[:, :], cflat, ALU.subtract).then_inc(s_count, 1)
            dve.tensor_tensor(shifted[:, :, :], logits[:, :, :],
                              top[:, :, 0:1].to_broadcast([P, TILES, EXPERTS]), ALU.subtract).then_inc(s_count, 1)
            dve.tensor_tensor(gap[:, :], top[:, :, 1], top[:, :, 0], ALU.subtract).then_inc(s_count, 1)
            dve.wait_ge(s_pos, 1)
            step(dve.scalar_tensor_tensor(place[:, :], down[1][:, 0:ET], 1.0, cflat, ALU.add, ALU.mult))
            step(dve.tensor_scalar(place[:, :], place[:, :], -1.0, None, ALU.add))

            def make_takes(e, ts):
                for t in ts:
                    if t == 0:
                        wait(dve, learn_ok, e)
                    at = place[:, t + e * TILES:t + e * TILES + 1] if isinstance(e, int) else \
                        place[:, bass.ds(e * TILES + t, 1)]
                    dve.tensor_scalar(takes[:, t, :], slot_iota[:, :], at, None,
                                      ALU.is_equal).then_inc(takes_ok, 1)

            def find_rows(e):
                dve.tensor_tensor(nidx[:, 0, :], learnt[:, :, 1], learnt[:, :, 2], ALU.add).then_inc(s_idx, 1)
                dve.tensor_scalar(nidx[:, 2, :], learnt[:, :, 0], -1.0, 1.0, ALU.mult, ALU.add).then_inc(s_idx, 1)
                done = 2 if isinstance(e, int) and e == 0 else 5 * e + 3
                dve.wait_ge(s_idx, done)
                for r in range(ROWTILES):
                    wait(dve, xe_in[r], 16 * e)
                dve.tensor_tensor(nidx[:, 2, :], nidx[:, 2, :], spare[:, :], ALU.mult).then_inc(s_idx, 1)
                dve.tensor_copy(row_in[:, :], nidx[:, 0, :])
                if not isinstance(e, int) or e:
                    add_weights(e)
                dve.wait_ge(s_idx, done + 1)
                dve.tensor_tensor(nrow_out[:, :], nidx[:, 0, :], nidx[:, 2, :], ALU.add).then_inc(rows_ok, 1)

            def add_weights(e):
                dve.tensor_tensor(nscale[:, :], nidx[:, 1, :], learnt[:, :, 5], ALU.add).then_inc(s_idx, 1)

            def pair_weights():
                dve.tensor_tensor(nidx[:, 1, :], learnt[:, :, 3], learnt[:, :, 4], ALU.add).then_inc(s_idx, 1)

            def read_learnt(e):
                dve.wait_ge(learnt_ok, e + 1)
                pair_weights()
                find_rows(e)

            make_takes(0, range(TILES))
            dve.wait_ge(s_firstout, 1)
            find_rows(0)
            dve.wait_ge(s_exp, 2)
            step(dve.tensor_reduce(zsum[:, :], exps[:, :, :], AX.X, ALU.add))
            step(dve.reciprocal(zsum[:, :], zsum[:, :]))
            step(dve.tensor_scalar(gates[:, 0, :], zsum[:, :], 0.5, None, ALU.mult))
            step(dve.tensor_tensor(gates[:, 1, :], gates[:, 0, :], egap[:, :], ALU.mult))
            for k in range(TOPK):
                step(dve.tensor_tensor(weighted[:, k, :, :], onehot[:, k, :, :],
                                       gates[:, k, :].rearrange("p (t o) -> p t o", o=1).to_broadcast(
                                           [P, TILES, EXPERTS]), ALU.mult), k == TOPK - 1)
            step(dve.tensor_tensor(weight[:, :].rearrange("p (e t) -> p t e", e=EXPERTS),
                                   weighted[:, 0, :, :], weighted[:, 1, :, :], ALU.add))
            col = lambda c: facts[:, :, :, c].rearrange("p e t -> p (e t)")
            step(dve.tensor_copy(col(3), weight[:, :]))
            step(dve.tensor_tensor(wrest[:, :], weight[:, :], col(3), ALU.subtract))
            step(dve.tensor_copy(col(4), wrest[:, :]))
            step(dve.tensor_tensor(col(5), wrest[:, :], col(4), ALU.subtract))
            dve.sem_inc(s_facts, 1)

            def rest_w2(e, f):
                dve.wait_ge(w2hi_ok, KF * e + f + 1)
                dve.tensor_tensor(w2lo[:, f, :], w2raw[:, f, :], w2hi[:, f, :].bitcast(F32),
                                  ALU.subtract).then_inc(w2lo_ok, 1)

            def rest_rows(e, i, bank=turn):
                dve.wait_ge(xthi_ok, NT * e + i + 1)
                dve.tensor_tensor(part(xtlo[:, :], i), turned_view(bank, i), part(xthi[:, :].bitcast(F32), i),
                                  ALU.subtract).then_inc(xtlo_ok, 1)

            def rest_relu(e, f):
                for c in range(2):
                    i = 2 * f + c
                    dve.wait_ge(hhi_ok, NH * e + i + 1)
                    a = c * HALFCAP
                    dve.scalar_tensor_tensor(hlo[:, f, a:a + HALFCAP], up[i % 4][:, 0:HALFCAP], 0.0,
                                             hhi[:, f, a:a + HALFCAP].bitcast(F32),
                                             ALU.max, ALU.subtract).then_inc(hlo_ok, 1)

            def make_current(e):
                dve.wait_ge(rows_ok, e + 1)
                dve.wait_ge(s_idx, 5 * (e + 1))
                wait(dve, added, 16 * ROWTILES * e)
                dve.tensor_copy(row_out[:, :], nrow_out[:, :]).then_inc(cur_ok, 1)
                dve.tensor_copy(rscale[:, :], nscale[:, :]).then_inc(cur_ok, 1)

            def up_part(e, more):
                for f in range(KF):
                    rest_relu(e, f)
                    rest_w2(e, f)
                    if f == LEARNT:
                        make_current(e)
                        if more:
                            read_learnt(e + 1)

            dve.wait_ge(learnt_ok, 1)
            pair_weights()
            dve.wait_ge(s_idx, 4)
            add_weights(0)
            for i in range(NT):
                if i < 2:
                    make_takes(1, range(i * TILES // NT, (i + 1) * TILES // NT))
                rest_rows(0, i, FIRST_BANKS[i])
            make_takes(1, range(2 * TILES // NT, TILES))
            up_part(0, True)

            def expert_step(e, more):
                for r in range(NT):
                    if r < KD:
                        rest_w1(e, r)
                    if r and more:
                        make_takes(e + 1, range((r - 1) * TILES // 2, r * TILES // 2))
                    rest_rows(e, r)
                up_part(e, more)

            with dve.Fori(1, EXPERTS - 1) as e:
                expert_step(e, True)
            expert_step(EXPERTS - 1, False)


CHUNK = 512
CHUNKS = TOKENS // CHUNK
CT = CHUNK // P
GROUPS = BATCH * KV_HEADS
QT_TILES = SEQ // P
PARTS = 3
MEETS = [PARTS - s for s in range(PARTS)]
PROWS = sum(MEETS) * HD
SHIFT_ROWS, ALIBI_ROWS = 2, 6
KROWS = PROWS + SHIFT_ROWS + ALIBI_ROWS


def project(nc, X, x_dram, Wq, Wk, Wv, consts, held, q_dram, k_dram, qt, kt, v_all):
    assert CT == LNT
    with ExitStack() as ctx:
        def sb(name, shape, dt):
            return ctx.enter_context(nc.sbuf_tensor(name, shape, dt))

        def ps(name, shape, dt=F32):
            return ctx.enter_context(nc.psum_tensor(name, shape, dt))

        def sem(name):
            return ctx.enter_context(nc.semaphore(name))

        NQ, NK = HEADS * HD, KV_HEADS * HD
        QH, KH = NQ // 2, NK // 2
        KSWAP = NQ + KH
        V0 = NQ + NK + KH
        NW = V0 + NK
        identf, identb, future = held
        tables = sb("p_tables", [P, 4, SEQ], F32)
        wraw = sb("p_wraw", [P, KD, NW], F32)
        whi = sb("p_whi", [P, KD, NW], F32R)
        wlo = sb("p_wlo", [P, KD, NW], F32R)
        stats = sb("p_stats", [P, TILES, 6], F32)
        mv = sb("p_mv", [P, TILES, 2], F32)
        veps = sb("p_veps", [P, TILES], F32)
        sd = sb("p_sd", [P, TILES], F32)
        rstd = sb("p_rstd", [P, TILES], F32)
        nwt = sb("p_nwt", [P, TILES], F32)
        nmr = sb("p_nmr", [P, TILES], F32)
        xthi = [sb(f"p_xthi{i}", [P, KD, CHUNK], F32R) for i in range(2)]
        xtlo = [sb(f"p_xtlo{i}", [P, KD, CHUNK], F32R) for i in range(2)]
        HALVES = (2, 1)
        terms = [sb(f"p_terms{i}", [P, 2 * n, CHUNK], F32) for i, n in enumerate(HALVES)]
        rot = [[sb(f"p_rot{i}{c}", [P, n, CHUNK], F32) for c in range(2)] for i, n in enumerate(HALVES)]
        parts = [[sb(f"p_parts{i}{c}", [P, PARTS, n, CHUNK], BF16) for c in range(2)]
                 for i, n in enumerate(HALVES)]

        turn = [ps(f"p_turn{i}", [P, BANK]) for i in range(KD)]
        halves = [[ps(f"p_half{i}{h}", [P, BANK]) for h in range(2)] for i in range(2)]
        vps = ps("p_v", [P, BANK])

        s_const = sem("p_const")
        s_ident = sem("p_ident")
        s_w = sem("p_w")
        s_vec = sem("p_vec")
        s_var = sem("p_var")
        s_sd = sem("p_sd")
        s_nmr = sem("p_nmr")
        s_x = [sem(f"p_x{g}") for g in range(LNG)]
        s_xn = sem("p_xn")
        s_whi = sem("p_whi")
        s_wlo = sem("p_wlo")
        s_turn = sem("p_turned")
        s_hi = sem("p_xthi")
        s_lo = sem("p_xtlo")
        s_qk = sem("p_qk")
        s_v = sem("p_v")
        s_terms = sem("p_terms")
        s_rot = sem("p_rot")
        s_p0 = sem("p_part0")
        s_r1 = sem("p_rest1")
        s_p1 = sem("p_part1")
        s_p2 = [sem(f"p_part2{i}") for i in range(2)]
        s_vout = sem("p_vout")
        s_store = [[sem(f"p_store{i}{c}") for c in range(2)] for i in range(2)]
        s_load = sem("p_load")

        rows = (QH, NK)
        TERMS, ROTS = (4, 2), (2, 1)

        def after(counts, c, i):
            return c * sum(counts) + sum(counts[:i + 1])

        scratch = (q_dram, k_dram)
        def leave_second(eng, c, i):
            m = rows[i]
            eng.wait_ge(s_p1, 2 * c + i + 1)
            eng.tensor_tensor(parts[i][c % 2][0:m, 2, :, :], rot[i][c % 2][0:m, :, :],
                              parts[i][c % 2][0:m, 1, :, :], ALU.subtract).then_inc(s_p2[i], 1)

        block = ctx.enter_context(nc.Block())

        @block.sync
        def _(sp):
            def load_x(g):
                sp.dma_start(X[:, g * LNT:(g + 1) * LNT, :], x_dram.rearrange("(t p) d -> p t d", p=P)[
                    :, g * LNT:(g + 1) * LNT, :]).then_inc(s_x[g], 16)

            load_x(0)
            sp.dma_start(identf[:, :], consts["identf"]).then_inc(s_ident, 16)
            load_x(1)
            for w, cols, at in ((Wq, slice(0, NQ), 0), (Wk, slice(0, NK), NQ), (Wk, slice(0, KH), NQ + NK),
                                (Wv, slice(0, NK), V0)):
                sp.dma_start(wraw[:, :, at:at + cols.stop],
                             w.rearrange("(k p) n -> p k n", p=P)[:, :, cols]).then_inc(s_w, 16)
            sp.dma_start(tables[:, :, :], consts["rotary"]).then_inc(s_const, 16)
            for g in range(2, LNG):
                load_x(g)
            sp.dma_start(identb[:, :], consts["identb"]).then_inc(s_load, 16)
            sp.dma_start(future[:, :], consts["future"]).then_inc(s_load, 16)
            sp.dma_start(kt[PROWS:KROWS, :, :], consts["key_rows"]).then_inc(s_load, 16)
            sp.dma_start(qt[PROWS:KROWS, :, :], consts["query_rows"]).then_inc(s_load, 16)
            for c in range(CHUNKS):
                b, t0 = c * CHUNK // SEQ, c * CHUNK % SEQ
                for i in range(2):
                    sp.wait_ge(s_p0, 2 * c + i + 1)
                    sp.wait_ge(s_p1, 2 * c + i + 1)
                    sp.wait_ge(s_p2[i], c + 1)
                    dst = scratch[i][b, :, :, :, :, t0:t0 + CHUNK]
                    if i == 0:
                        dst = dst.rearrange("m e j h t -> (j h) (m e) t")
                        src = parts[i][c % 2][:, :, :, :].rearrange("p m e t -> p (m e) t")
                    else:
                        dst = dst.rearrange("m e j h t -> (e j h) m t")
                        src = parts[i][c % 2][0:NK, :, 0, :]
                    sp.dma_start(dst, src).then_inc(s_store[i][c % 2], 16)
                if (c + 1) * CHUNK == SEQ:
                    for i in range(2):
                        for n in range(2):
                            sp.wait_ge(s_store[i][n], 16 * (c + 1) // 2)
                    load_parts(sp, q_dram, k_dram, qt, kt, 0, 1, s_load)
            for i in range(2):
                for n in range(2):
                    sp.wait_ge(s_store[i][n], 16 * CHUNKS // 2)
            sp.wait_ge(s_load, 16 * (4 + PARTS + sum(MEETS)))

        @block.gpsimd
        def _(pool):
            for c in range(CHUNKS):
                for i in range(2):
                    m = rows[i]
                    pool.wait_ge(s_terms, after(TERMS, c, i))
                    if c >= 2:
                        pool.wait_ge(s_p1, 2 * (c - 2) + i + 1)
                        pool.wait_ge(s_p2[i], c - 1)
                    for n, op in enumerate((ALU.subtract, ALU.add)[i:]):
                        pool.tensor_tensor(rot[i][c % 2][0:m, n, :], terms[i][0:m, 2 * n, :],
                                           terms[i][0:m, 2 * n + 1, :], op).then_inc(s_rot, 1)
                if c:
                    leave_second(pool, c - 1, 0)
            leave_second(pool, CHUNKS - 1, 0)

        @block.tensor
        def _(pe):
            pe.wait_ge(s_ident, 16)

            def turn_chunk(c):
                pe.wait_ge(s_xn, CT * (c + 1))
                for k in range(KD):
                    if c:
                        pe.wait_ge(s_lo, KD * (c - 1) + k + 1)
                    for r in range(CT):
                        mm = pe.transpose(turn[k][:, r * P:(r + 1) * P],
                                          X[:, c * CT + r, k * P:(k + 1) * P], identf[:, :])
                    mm.then_inc(s_turn, 1)

            turn_chunk(0)
            for c in range(CHUNKS):
                if c == 0:
                    pe.wait_ge(s_wlo, 2)
                pe.wait_ge(s_lo, KD * (c + 1))
                xh, xl = xthi[c % 2], xtlo[c % 2]
                for i in range(2):
                    if i == 1 and c + 1 < CHUNKS:
                        turn_chunk(c + 1)
                    if c:
                        pe.wait_ge(s_terms, after(TERMS, c - 1, i))
                    for h in range(2):
                        m = rows[i]
                        a = (0, QH)[h] if i == 0 else (NQ, KSWAP)[h]
                        n = 0
                        for k in range(KD):
                            for w, x in ((whi, xh), (whi, xl), (wlo, xh)):
                                mm = pe.matmul(halves[i][h][0:m, :], w[:, k, a:a + m], x[:, k, :],
                                               start=(n == 0), stop=(n == 3 * KD - 1))
                                n += 1
                    mm.then_inc(s_qk, 1)
                if c:
                    pe.wait_ge(s_vout, c)
                for r in range(CT):
                    n = 0
                    for k in range(KD):
                        for w, x in ((whi, xh), (wlo, xh), (whi, xl)):
                            mm = pe.matmul(vps[:, r * NK:(r + 1) * NK], x[:, k, r * P:(r + 1) * P],
                                           w[:, k, V0:NW], start=(n == 0), stop=(n == 3 * KD - 1))
                            n += 1
                mm.then_inc(s_v, 1)

        @block.scalar
        def _(act):
            root(act, veps, sd, s_var, s_sd, 0)
            scale_rows(act, X, rstd, nmr, X, s_nmr, s_xn, 0)
            act.wait_ge(s_w, 64)
            act.activation(whi[:, :, 0:NQ], wraw[:, :, 0:NQ], ACT.Copy, scale=HD ** -0.5).then_inc(s_whi, 1)
            act.copy(whi[:, :, NQ:NW], wraw[:, :, NQ:NW]).then_inc(s_whi, 1)

            def split_chunk(c):
                for k in range(KD):
                    act.wait_ge(s_turn, KD * c + k + 1)
                    if c >= 2:
                        act.wait_ge(s_v, c - 1)
                    act.copy(xthi[c % 2][:, k, :], turn[k][:, :]).then_inc(s_hi, 1)

            def part(c, i, n):
                m = rows[i]
                if n == 0:
                    act.wait_ge(s_rot, after(ROTS, c, i))
                    if c >= 2:
                        act.wait_ge(s_store[i][c % 2], 16 * (c // 2))
                else:
                    act.wait_ge(s_r1, 2 * c + i + 1)
                act.copy(parts[i][c % 2][0:m, n, :, :], rot[i][c % 2][0:m, :, :]).then_inc((s_p0, s_p1)[n], 1)

            def copy_v(c):
                act.wait_ge(s_v, c + 1)
                b, t0 = c * CT // QT_TILES, c * CT % QT_TILES
                for r in range(CT):
                    cp = act.copy(v_all[:, b * KV_HEADS:(b + 1) * KV_HEADS, t0 + r, 0:HD],
                                  vps[:, r * NK:(r + 1) * NK].rearrange("p (g d) -> p g d", g=KV_HEADS))
                cp.then_inc(s_vout, 1)

            split_chunk(0)
            root(act, veps, sd, s_var, s_sd, 1)
            scale_rows(act, X, rstd, nmr, X, s_nmr, s_xn, 1)
            for c in range(CHUNKS + 1):
                if c:
                    part(c - 1, 0, 0)
                if c + 1 < CHUNKS:
                    split_chunk(c + 1)
                if c:
                    part(c - 1, 0, 1)
                    part(c - 1, 1, 0)
                if c + 2 < CHUNKS:
                    root(act, veps, sd, s_var, s_sd, c + 2)
                    scale_rows(act, X, rstd, nmr, X, s_nmr, s_xn, c + 2)
                if c:
                    part(c - 1, 1, 1)
                if c < CHUNKS:
                    copy_v(c)

        @block.vector
        def _(dve):
            steps = [0]

            def step(ins, wait=True):
                steps[0] += 1
                ins.then_inc(s_vec, 1)
                if wait:
                    dve.wait_ge(s_vec, steps[0])

            def normalise_group(g):
                dve.wait_ge(s_x[g], 16)
                normalise(dve, step, X, stats, mv, veps, sd, rstd, nwt, nmr, s_var, s_sd, s_nmr, g)

            normalise_group(0)
            dve.wait_ge(s_whi, 2)
            dve.scalar_tensor_tensor(wlo[:, :, 0:NQ], wraw[:, :, 0:NQ], HD ** -0.5,
                                     whi[:, :, 0:NQ].bitcast(F32), ALU.mult, ALU.subtract).then_inc(s_wlo, 1)
            dve.tensor_tensor(wlo[:, :, NQ:NW], wraw[:, :, NQ:NW], whi[:, :, NQ:NW].bitcast(F32),
                              ALU.subtract).then_inc(s_wlo, 1)

            def rest_chunk(c):
                for k in range(KD):
                    dve.wait_ge(s_hi, KD * c + k + 1)
                    dve.tensor_tensor(xtlo[c % 2][:, k, :], turn[k][:, :], xthi[c % 2][:, k, :].bitcast(F32),
                                      ALU.subtract).then_inc(s_lo, 1)

            rest_chunk(0)
            normalise_group(1)
            dve.wait_ge(s_const, 16)

            def terms_of(c, i):
                t0 = c * CHUNK % SEQ
                cos, sin = (tables[0:rows[i], 2 * i + n, t0:t0 + CHUNK] for n in range(2))
                factors = (((0, cos), (1, sin), (0, sin), (1, cos)), ((0, cos), (1, sin)))[i]
                dve.wait_ge(s_qk, 2 * c + i + 1)
                if c:
                    dve.wait_ge(s_rot, after(ROTS, c - 1, i))
                for n, (h, table) in enumerate(factors):
                    dve.tensor_tensor(terms[i][0:rows[i], n, :], halves[i][h][0:rows[i], :], table,
                                      ALU.mult).then_inc(s_terms, 1)

            def leave_first(c, i):
                m = rows[i]
                dve.wait_ge(s_p0, 2 * c + i + 1)
                dve.tensor_tensor(rot[i][c % 2][0:m, :, :], rot[i][c % 2][0:m, :, :], parts[i][c % 2][0:m, 0, :, :],
                                  ALU.subtract).then_inc(s_r1, 1)

            for c in range(CHUNKS + 1):
                if c < CHUNKS:
                    terms_of(c, 0)
                if c:
                    leave_first(c - 1, 0)
                if c + 1 < CHUNKS:
                    rest_chunk(c + 1)
                if c < CHUNKS:
                    terms_of(c, 1)
                if c:
                    leave_first(c - 1, 1)
                if c + 2 < CHUNKS:
                    normalise_group(c + 2)
                if c:
                    leave_second(dve, c - 1, 1)


def load_parts(sp, q_dram, k_dram, qt, kt, first, last, loaded):
    b = first // KV_HEADS
    groups = slice(first % KV_HEADS, (last - 1) % KV_HEADS + 1)
    heads = slice(groups.start * GROUP, groups.stop * GROUP)
    row = 0
    for part, meets in enumerate(MEETS):
        n = meets * HD
        sp.dma_start(kt[row:row + n, first:last, :],
                     k_dram[b, 0:meets, :, :, groups].rearrange("m e j h t -> (m e j) h t")).then_inc(loaded, 16)
        for m in range(meets):
            sp.dma_start(qt[row + m * HD:row + (m + 1) * HD, first * GROUP:last * GROUP, :],
                         q_dram[b, part, :, :, heads].rearrange("e j h t -> (e j) h t")).then_inc(loaded, 16)
        row += n


MAX_PIECES = [(i, c * BANK, min(BANK, (i + 1) * P - c * BANK))
              for i in range(QT_TILES) for c in range(2) if (i + 1) * P > c * BANK]
EXP_PIECES = [(j, max(j * P, c * BANK), BANK * (c + 1) - max(j * P, c * BANK))
              for j in range(QT_TILES) for c in range(2) if BANK * (c + 1) > j * P]
PIECES = len(MAX_PIECES)


MAX_ORDER = (4, 5, 8, 1, 9, 11, 10, 0, 3, 6, 7, 2)
STEPS = GROUP * PIECES


def attend(nc, X, x_dram, held, q_dram, k_dram, qt, kt, v_all, attended, Wo, wraw):
    NM, NS = 3, 2
    with ExitStack() as ctx:
        def sb(name, shape, dt):
            return ctx.enter_context(nc.sbuf_tensor(name, shape, dt))

        def ps(name, shape, dt=F32):
            return ctx.enter_context(nc.psum_tensor(name, shape, dt))

        def sem(name):
            return ctx.enter_context(nc.semaphore(name))

        identf, identb, future = held
        vg = sb("a_vg", [P, QT_TILES, 2 * HD], F32)
        probs = [[sb(f"a_probs{i}{h}", [P, BANK], F32) for h in range(GROUP)] for i in range(2)]
        piecemax = sb("a_piecemax", [P, GROUP, PIECES], F32)
        shift = sb("a_shift", [P, GROUP, QT_TILES], F32)
        shiftb = sb("a_shiftb", [P, P // (GROUP * QT_TILES), GROUP, QT_TILES], BF16)
        shiftT = sb("a_shiftT", [SHIFT_ROWS * GROUP * QT_TILES, P], BF16)
        osb = sb("a_osb", [P, 2 * BANK], F32)
        rsum = sb("a_rsum", [P, BANK // P, GROUP], F32)

        mscore = [ps(f"a_mscore{i}", [P, BANK]) for i in range(NM)]
        score = [ps(f"a_score{i}", [P, BANK]) for i in range(NS)]
        oT = ps("a_oT", [P, 2 * BANK])
        misc = ps("a_misc", [P, BANK])

        q_in = sem("a_q_in")
        group_in = sem("a_group_in")
        x_in = sem("a_x_in")
        mscored = sem("a_mscored")
        reduced = sem("a_reduced")
        s_blank = sem("a_blank")
        s_fin = sem("a_fin")
        shifts_ok = sem("a_shifts_ok")
        shiftT_ok = sem("a_shiftT_ok")
        shift_in = sem("a_shift_in")
        scored = sem("a_scored")
        expd = sem("a_expd")
        pv = sem("a_pv")
        v_blank = sem("a_v_blank")
        v_low = sem("a_v_low")
        v_high = sem("a_v_high")
        misc_shift = sem("a_misc_shift")
        misc_o = sem("a_misc_o")
        osb_ok = sem("a_osb_ok")
        s_rsum = sem("a_rsum")
        out_ok = sem("a_out_ok")

        LAST = [max(t for t in range(PIECES) if EXP_PIECES[t][1] // BANK == c) for c in range(2)]
        COPY = [t + 2 for t in LAST]
        TURN = [t + 3 for t in LAST]
        MAX_STEP = STEPS - 11
        SHIFT_STEP = MAX_STEP + 4
        OVERHEAD, SPAN = 64, 400
        cost = [MAX_PIECES[MAX_ORDER[m // GROUP]][2] + OVERHEAD for m in range(STEPS)]
        span = [EXP_PIECES[s // GROUP][2] + SPAN for s in range(STEPS)]

        def found_by(s):
            share = sum(cost) * (1 + (sum(span[:s + 1]) - sum(span[:MAX_STEP + 1])) / sum(span))
            m = 0
            while sum(cost[:min(m, STEPS)]) + sum(cost[:max(m - STEPS, 0)]) < share - 1e-6 * sum(cost):
                m += 1
            return m

        AHEAD = found_by(-1)
        FOUND = [found_by(s) for s in range(STEPS)]

        def maxima(s, more):
            for m in range(FOUND[s - 1] if s else AHEAD, FOUND[s]):
                ahead, m = 1 + m // STEPS, m % STEPS
                if ahead <= more:
                    yield ahead, m

        def wait(eng, s, value):
            if not isinstance(value, int) or value > 0:
                eng.wait_ge(s, value)

        block = ctx.enter_context(nc.Block())

        @block.sync
        def _(sp):
            LOADS = PARTS + sum(MEETS)

            def shifts(n):
                sp.wait_ge(shiftT_ok, n + 1)
                R = GROUP * QT_TILES
                for s in range(SHIFT_ROWS):
                    sp.dma_start(qt[PROWS + s:PROWS + s + 1, bass.ds(n * GROUP, GROUP), :].rearrange(
                        "o h (i q) -> o (h i) q", q=P), shiftT[s * R:(s + 1) * R, :]).then_inc(shift_in, 16)

            sp.sem_inc(group_in, 1)
            load_parts(sp, q_dram, k_dram, qt, kt, 1, KV_HEADS, q_in)
            sp.wait_ge(q_in, 16 * LOADS)
            sp.sem_inc(group_in, KV_HEADS - 1)
            shifts(0)
            for b in range(1, BATCH):
                load_parts(sp, q_dram, k_dram, qt, kt, b * KV_HEADS, (b + 1) * KV_HEADS, q_in)
                if b == 1:
                    sp.dma_start(X[:, :, :], x_dram.rearrange("(t p) d -> p t d", p=P)).then_inc(x_in, 16)
                    sp.dma_start(wraw[:, :, :], Wo.rearrange("(k p) n -> p k n", p=P)).then_inc(x_in, 16)
                with sp.Fori((b - 1) * KV_HEADS + 1, b * KV_HEADS - 1) as n:
                    shifts(n)
                sp.wait_ge(q_in, 16 * LOADS * (b + 1))
                sp.sem_inc(group_in, KV_HEADS)
                shifts(b * KV_HEADS - 1)
                shifts(b * KV_HEADS)
            with sp.Fori((BATCH - 1) * KV_HEADS + 1, GROUPS) as n:
                shifts(n)
            sp.wait_ge(x_in, 32)
            sp.wait_ge(shift_in, 16 * SHIFT_ROWS * GROUPS)

        @block.gpsimd
        def _(pool):
            H = QT_TILES // 2

            def set_v(n):
                for half, done, behind in ((0, v_low, 2 * H), (1, v_high, PIECES)):
                    wait(pool, pv, PIECES * (n - 1) + behind)
                    js = slice(half * H, (half + 1) * H)
                    pool.tensor_copy(vg[:, js, 0:HD], v_all[:, n, js, :]).then_inc(done, 1)

            pool.memset(vg[:, :, :], 0.0).then_inc(v_blank, 1)
            pool.wait_ge(v_blank, 1)
            pool.memset(vg[:, :, HD:HD + 1], 1.0).then_inc(v_blank, 1)
            pool.wait_ge(v_blank, 2)
            set_v(0)
            with pool.Fori(1, GROUPS) as n:
                set_v(n)

        @block.tensor
        def _(pe):
            def max_piece(n, m):
                t, hh = MAX_ORDER[m // GROUP], m % GROUP
                i, k0, w = MAX_PIECES[t]
                if m == 0:
                    pe.wait_ge(group_in, n + 1)
                last = k0 + w == (i + 1) * P
                wait(pe, reduced, STEPS * n + m - NM + 1)
                mm = pe.matmul(mscore[m % NM][:, 0:w], qt[:, n * GROUP + hh, i * P:(i + 1) * P],
                               kt[:, n, k0:k0 + w], start=True, stop=True)
                if last:
                    mm = pe.matmul(mscore[m % NM][:, w - P:w], identb[:, :], future[:, :], start=False,
                                   stop=True, skip_group_check=True)
                mm.then_inc(mscored, 1)

            def exp_piece(n, s):
                t, hh = divmod(s, GROUP)
                j, q0, w = EXP_PIECES[t]
                if s == 0:
                    pe.wait_ge(shift_in, 16 * SHIFT_ROWS * (n + 1))
                wait(pe, expd, STEPS * n + s - NS + 1)
                mm = pe.matmul(score[s % NS][:, 0:w], kt[:, n, j * P:(j + 1) * P],
                               qt[:, n * GROUP + hh, q0:q0 + w], start=True, stop=True)
                if q0 == j * P:
                    mm = pe.matmul(score[s % NS][:, 0:P], future[:, :], identb[:, :], start=False,
                                   stop=True, skip_group_check=True)
                mm.then_inc(scored, 1)

            def v_round(n, t):
                j, q0, w = EXP_PIECES[t]
                c = q0 // BANK
                if t == 0:
                    pe.wait_ge(v_low, n + 1)
                if t == 2 * (QT_TILES // 2):
                    pe.wait_ge(v_high, n + 1)
                if j == 0:
                    wait(pe, osb_ok, 2 * n + c - 1)
                pe.wait_ge(expd, STEPS * n + GROUP * (t + 1))
                for hh in range(GROUP):
                    mm = pe.matmul(oT[2 * HD * hh:2 * HD * (hh + 1), q0:q0 + w], vg[:, j, :],
                                   probs[t % 2][hh][:, 0:w], start=(j == 0),
                                   stop=(j == (BANK * (c + 1)) // P - 1), skip_group_check=True)
                mm.then_inc(pv, 1)

            def turn_shifts(n):
                pe.wait_ge(shifts_ok, n + 1)
                wait(pe, out_ok, 2 * (n - 1) + 1)
                pe.transpose(misc[:, 0:P // 2].bitcast(BF16),
                             shiftb[:, :, :, :].rearrange("p s h i -> p (s h i)"),
                             identb[:, :]).then_inc(misc_shift, 1)

            def turn_out(n, c, last=False):
                pe.wait_ge(osb_ok, 2 * n + c + 1)
                wait(pe, out_ok, 2 * n + c)
                if c == 1 and not last:
                    pe.wait_ge(shiftT_ok, n + 2)
                for r in range(BANK // P):
                    mm = pe.transpose(misc[:, r * P:(r + 1) * P],
                                      osb[:, c * BANK + r * P:c * BANK + (r + 1) * P], identf[:, :])
                mm.then_inc(misc_o, 1)

            def group(n, more, before):
                for t in range(PIECES):
                    for s in range(GROUP * t, GROUP * (t + 1)):
                        exp_piece(n, s)
                        for ahead, m in maxima(s, more):
                            max_piece(n + ahead, m)
                        if more and s == SHIFT_STEP:
                            turn_shifts(n + 1)
                    if t:
                        v_round(n, t - 1)
                    elif before:
                        v_round(n - 1, PIECES - 1)
                    for c in range(2):
                        if t == TURN[c]:
                            turn_out(n, c)
                        elif t + PIECES == TURN[c] and before:
                            turn_out(n - 1, c)

            for m in range(STEPS):
                max_piece(0, m)
            turn_shifts(0)
            for m in range(AHEAD):
                max_piece(1, m)
            group(0, 2, False)
            with pe.Fori(1, GROUPS - 2) as n:
                group(n, 2, True)
            group(GROUPS - 2, 1, True)
            group(GROUPS - 1, 0, True)
            v_round(GROUPS - 1, PIECES - 1)
            turn_out(GROUPS - 1, 1, last=True)

        @block.scalar
        def _(act):
            def copy_sums(n, c):
                act.wait_ge(pv, PIECES * n + LAST[c] + 1)
                wait(act, misc_o, 2 * n + c - 1)
                act.copy(osb[:, c * BANK:(c + 1) * BANK], oT[:, c * BANK:(c + 1) * BANK]).then_inc(osb_ok, 1)

            def group(n, before):
                for t in range(PIECES):
                    for c in range(2):
                        if t == COPY[c]:
                            copy_sums(n, c)
                        elif t + PIECES == COPY[c] and before:
                            copy_sums(n - 1, c)
                    w = EXP_PIECES[t][2]
                    for hh in range(GROUP):
                        s = GROUP * t + hh
                        act.wait_ge(scored, STEPS * n + s + 1)
                        if hh == 0:
                            wait(act, pv, PIECES * n + t - 1)
                        act.activation(probs[t % 2][hh][:, 0:w], score[s % NS][:, 0:w], ACT.Exp).then_inc(expd, 1)

            group(0, False)
            with act.Fori(1, GROUPS) as n:
                group(n, True)
            copy_sums(GROUPS - 1, 1)

        @block.vector
        def _(dve):
            def reduce_piece(n, m):
                t, hh = MAX_ORDER[m // GROUP], m % GROUP
                dve.wait_ge(mscored, STEPS * n + m + 1)
                if m == 0:
                    wait(dve, s_fin, 4 * n)
                dve.tensor_reduce(piecemax[:, hh, t:t + 1], mscore[m % NM][:, 0:MAX_PIECES[t][2]], AX.X,
                                  ALU.max, negate=True).then_inc(reduced, 1)

            def finish_shifts(n):
                H = QT_TILES // 2
                dve.wait_ge(reduced, STEPS * (n + 1))
                two = piecemax[:, :, H:PIECES].rearrange("p h (i c) -> p h i c", c=2)
                dve.tensor_copy(shift[:, :, 0:H], piecemax[:, :, 0:H]).then_inc(s_fin, 1)
                dve.tensor_tensor(shift[:, :, H:QT_TILES], two[:, :, :, 0], two[:, :, :, 1],
                                  ALU.min).then_inc(s_fin, 1)
                dve.wait_ge(s_fin, 4 * n + 2)
                wait(dve, misc_shift, n)
                dve.tensor_copy(shiftb[:, 0, :, :], shift[:, :, :]).then_inc(s_fin, 1)
                dve.wait_ge(s_fin, 4 * n + 3)
                dve.tensor_tensor(shiftb[:, 1, :, :], shift[:, :, :], shiftb[:, 0, :, :],
                                  ALU.subtract).then_inc(s_fin, 1)
                dve.wait_ge(s_fin, 4 * n + 4)
                dve.sem_inc(shifts_ok, 1)

            def copy_shifts(n):
                dve.wait_ge(misc_shift, n + 1)
                wait(dve, shift_in, 16 * SHIFT_ROWS * n)
                dve.tensor_copy(shiftT[:, :], misc[:, 0:P // 2].bitcast(BF16)[
                    0:SHIFT_ROWS * GROUP * QT_TILES, 0:P]).then_inc(shiftT_ok, 1)

            def write_out(n, c):
                dve.wait_ge(misc_o, 2 * n + c + 1)
                H = BANK // P
                m = misc[:, :].rearrange("p (i h d) -> p i h d", i=H, h=GROUP)
                dve.reciprocal(rsum[:, :, :], m[:, :, :, HD]).then_inc(s_rsum, 1)
                dve.wait_ge(s_rsum, 2 * n + c + 1)
                d = attended[:, c * H:(c + 1) * H, bass.ds(n * GROUP * HD, GROUP * HD)]
                dve.tensor_tensor(d.rearrange("p i (h d) -> p i h d", h=GROUP), m[:, :, :, 0:HD],
                                  rsum[:, :, :].rearrange("p i (h o) -> p i h o", o=1)
                                  .to_broadcast([P, H, GROUP, HD]), ALU.mult).then_inc(out_ok, 1)

            def group(n, more, before):
                for t in range(PIECES):
                    for s in range(GROUP * t, GROUP * (t + 1)):
                        for ahead, m in maxima(s, more):
                            reduce_piece(n + ahead, m)
                            if m == STEPS - 1:
                                finish_shifts(n + 1)
                        if more and s == SHIFT_STEP:
                            copy_shifts(n + 1)
                    for c in range(2):
                        if t == TURN[c]:
                            write_out(n, c)
                        elif t + PIECES == TURN[c] and before:
                            write_out(n - 1, c)

            dve.memset(shiftb[:, SHIFT_ROWS:, :, :], 0.0).then_inc(s_blank, 1)
            dve.wait_ge(s_blank, 1)
            for m in range(STEPS):
                reduce_piece(0, m)
            finish_shifts(0)
            copy_shifts(0)
            for m in range(AHEAD):
                reduce_piece(1, m)
            group(0, 2, False)
            with dve.Fori(1, GROUPS - 2) as n:
                group(n, 2, True)
            group(GROUPS - 2, 1, True)
            group(GROUPS - 1, 0, True)
            write_out(GROUPS - 1, 1)
            dve.wait_ge(out_ok, 2 * GROUPS)


def project_out(nc, X, wraw, attended, identf):
    with ExitStack() as ctx:
        def sb(name, shape, dt):
            return ctx.enter_context(nc.sbuf_tensor(name, shape, dt))

        def ps(name, shape, dt=F32):
            return ctx.enter_context(nc.psum_tensor(name, shape, dt))

        def sem(name):
            return ctx.enter_context(nc.semaphore(name))

        whi = sb("o_whi", [P, KD, D], F32R)
        wlo = sb("o_wlo", [P, KD, D], F32R)
        ahi = sb("o_ahi", [P, 2, KD, P], F32R)
        alo = sb("o_alo", [P, 2, KD, P], F32R)
        turn = [ps(f"o_turn{i}", [P, BANK]) for i in range(2)]
        acc = [ps(f"o_acc{i}", [P, BANK]) for i in range(2)]
        s_whi = sem("o_whi")
        s_wlo = sem("o_wlo")
        s_turn = sem("o_turned")
        s_hi = sem("o_hi")
        s_lo = sem("o_lo")
        s_mm = sem("o_mm")
        s_add = sem("o_add")
        block = ctx.enter_context(nc.Block())

        @block.tensor
        def _(pe):
            def turn_tile(t):
                b, i = t // QT_TILES, t % QT_TILES
                if t >= 2:
                    pe.wait_ge(s_lo, t - 1)
                for k in range(KD):
                    src = attended[:, i, b * D + k * P:b * D + (k + 1) * P]
                    mm = pe.transpose(turn[t % 2][:, k * P:(k + 1) * P], src, identf[:, :])
                mm.then_inc(s_turn, 1)

            turn_tile(0)
            pe.wait_ge(s_wlo, 1)
            for t in range(TILES):
                if t + 1 < TILES:
                    turn_tile(t + 1)
                pe.wait_ge(s_lo, t + 1)
                if t >= 2:
                    pe.wait_ge(s_add, t - 1)
                n = 0
                for k in range(KD):
                    for a, w in ((ahi, whi), (ahi, wlo), (alo, whi)):
                        mm = pe.matmul(acc[t % 2][:, 0:D], a[:, t % 2, k, :], w[:, k, :],
                                       start=(n == 0), stop=(n == 3 * KD - 1))
                        n += 1
                mm.then_inc(s_mm, 1)

        @block.scalar
        def _(act):
            act.copy(whi[:, :, :], wraw[:, :, :]).then_inc(s_whi, 1)
            for t in range(TILES):
                act.wait_ge(s_turn, t + 1)
                if t >= 2:
                    act.wait_ge(s_mm, t - 1)
                act.copy(ahi[:, t % 2, :, :], turn[t % 2][:, 0:D].rearrange("p (k q) -> p k q", k=KD)).then_inc(s_hi, 1)

        @block.vector
        def _(dve):
            dve.wait_ge(s_whi, 1)
            dve.tensor_tensor(wlo[:, :, :], wraw[:, :, :], whi[:, :, :].bitcast(F32),
                              ALU.subtract).then_inc(s_wlo, 1)

            def add(t):
                dve.wait_ge(s_mm, t + 1)
                dve.tensor_tensor(X[:, t, :], acc[t % 2][:, 0:D], X[:, t, :], ALU.add).then_inc(s_add, 1)

            for t in range(TILES):
                dve.wait_ge(s_hi, t + 1)
                dve.tensor_tensor(alo[:, t % 2, :, :], turn[t % 2][:, 0:D].rearrange("p (k q) -> p k q", k=KD),
                                  ahi[:, t % 2, :, :].bitcast(F32), ALU.subtract).then_inc(s_lo, 1)
                if t:
                    add(t - 1)
            add(TILES - 1)
            dve.wait_ge(s_add, TILES)


def constants():
    bf = np.dtype("bfloat16")
    r = np.arange(P)
    c = {
        "identf": np.eye(P, dtype=np.float32),
        "before": (r[:, None] < r[None, :]).astype(bf),
        "onesb": np.ones((P, P), bf),
        "iota": np.broadcast_to(np.arange(EXPERTS, dtype=np.float32), (P, TILES, EXPERTS)).copy(),
        "restart": np.broadcast_to((np.arange(TILES) > 0).astype(np.float32), (P, EXPERTS, TILES)).reshape(
            P, EXPERTS * TILES).copy(),
    }
    c["slot_iota"] = np.broadcast_to(np.arange(CAP, dtype=np.float16), (P, CAP)).copy()
    c["zeros"] = np.zeros((P, ROWTILES * FACTS), bf)
    c["spare"] = (TOKENS + np.arange(ROWTILES)[None, :] * P + r[:, None]).astype(np.float32)
    facts = np.zeros((P, EXPERTS, TILES, FACTS), bf)
    facts[:, :, :, 0] = 1
    facts[:, :, :, 1] = r[:, None, None]
    facts[:, :, :, 2] = (P * np.arange(TILES))[None, None, :]
    c["facts"] = facts
    pos = np.arange(SEQ, dtype=np.float32)
    theta = (1.0 / np.float32(10000.0) ** (np.arange(HALF, dtype=np.float32) / HALF)).astype(np.float32)
    angle = np.outer(pos, theta).astype(np.float32)
    rotary = []
    for heads in (HEADS, KV_HEADS):
        for f in (np.cos, np.sin):
            t = np.repeat(f(angle).astype(np.float32).T, heads, axis=0)
            rotary.append(np.tile(t, (P // t.shape[0], 1)))
    rotary[3][0:KV_HEADS * HALF] *= -1
    c["rotary"] = np.stack(rotary, axis=1)
    c["identb"] = np.eye(P).astype(bf)
    c["future"] = np.where(r[None, :] > r[:, None], NEG, 0.0).astype(bf)
    slopes = (2.0 ** (-8.0 * np.arange(1, HEADS + 1, dtype=np.float32) / HEADS)).astype(np.float32)
    parts, rest = [], slopes
    for _ in range(3):
        parts.append(rest.astype(bf))
        rest = rest - parts[-1].astype(np.float32)
    q = np.zeros((SHIFT_ROWS + ALIBI_ROWS, BATCH, HEADS, SEQ), bf)
    q[SHIFT_ROWS:] = np.repeat(np.stack(parts), 2, axis=0)[:, None, :, None]
    c["query_rows"] = q.reshape(SHIFT_ROWS + ALIBI_ROWS, BATCH * HEADS, SEQ)
    k = np.ones((SHIFT_ROWS + ALIBI_ROWS, GROUPS, SEQ), bf)
    k[SHIFT_ROWS::2] = (pos // P * P).astype(bf)
    k[SHIFT_ROWS + 1::2] = (pos % P).astype(bf)
    c["key_rows"] = k
    return c


def program(nc, ins, consts, out):
    x = ins["L0_attn_x"].rearrange("b t d -> (b t) d")
    o = out.rearrange("b t d -> (b t) d")
    with ExitStack() as ctx:
        X = ctx.enter_context(nc.sbuf_tensor("X", [P, TILES, D], F32))
        xn_dram = nc.dram_tensor("normalised", [TOKENS, D], F32).ap()
        acc = nc.dram_tensor("accumulated", [TOKENS + CAP, D], F32).ap()
        moe = (ins["L0_ffn_Wg"], ins["L0_ffn_w1"], ins["L0_ffn_w2"], xn_dram, acc, consts)
        ffn(nc, X, x, *moe, None, "a")
        with ExitStack() as mid:
            v_all = mid.enter_context(nc.sbuf_tensor("v_all", [P, GROUPS, QT_TILES, HD], F32))
            attended = mid.enter_context(nc.sbuf_tensor("attended", [P, QT_TILES, GROUPS * GROUP * HD], F32))
            qt = mid.enter_context(nc.sbuf_tensor("qt", [KROWS, BATCH * HEADS, SEQ], BF16))
            kt = mid.enter_context(nc.sbuf_tensor("kt", [KROWS, GROUPS, SEQ], BF16))
            wo = mid.enter_context(nc.sbuf_tensor("wo", [P, KD, D], F32))
            held = (mid.enter_context(nc.sbuf_tensor("a_identf", [P, P], F32)),
                    mid.enter_context(nc.sbuf_tensor("a_identb", [P, P], BF16)),
                    mid.enter_context(nc.sbuf_tensor("a_future", [P, P], BF16)))
            q_dram = nc.dram_tensor("q_parts", [BATCH, PARTS, 2, HALF, HEADS, SEQ], BF16).ap()
            k_dram = nc.dram_tensor("k_parts", [BATCH, PARTS, 2, HALF, KV_HEADS, SEQ], BF16).ap()
            project(nc, X, acc[0:TOKENS, :], ins["L0_attn_Wq"], ins["L0_attn_Wk"], ins["L0_attn_Wv"], consts,
                    held, q_dram, k_dram, qt, kt, v_all)
            attend(nc, X, acc[0:TOKENS, :], held, q_dram, k_dram, qt, kt, v_all, attended,
                   ins["L0_attn_Wo"], wo)
            project_out(nc, X, wo, attended, held[0])
        ffn(nc, X, None, *moe, o, "b")

_INS = ['L0_attn_x', 'L0_attn_Wq', 'L0_attn_Wk', 'L0_attn_Wv', 'L0_attn_Wo', 'L0_ffn_Wg', 'L0_ffn_w1', 'L0_ffn_w2']


def kernel(**inputs):
    import concourse.bacc as _bacc
    from concourse.bass_utils import run_bass_kernel_spmd as _run

    nc = _bacc.Bacc("TRN2", target_bir_lowering=False, num_devices=1)
    arrays, args, consts = {}, {}, {}
    for name in _INS:
        a = np.ascontiguousarray(inputs[name])
        if name in ("L0_attn_Wq", "L0_attn_Wk"):
            a = np.ascontiguousarray(a.reshape(D, -1, 2, HALF).transpose(0, 2, 3, 1).reshape(D, -1))
        arrays[f"in_{name}"] = a
        args[name] = nc.dram_tensor(f"in_{name}", a.shape, mybir.dt.from_np(a.dtype), kind="ExternalInput").ap()
    for name, a in constants().items():
        arrays[f"const_{name}"] = a
        consts[name] = nc.dram_tensor(f"const_{name}", a.shape, mybir.dt.from_np(a.dtype), kind="ExternalInput").ap()
    out = nc.dram_tensor("out_0", (BATCH, SEQ, D), F32, kind="ExternalOutput").ap()
    program(nc, args, consts, out)
    r = _run(nc, [arrays], core_ids=[0])
    return r.results[0]["out_0"]
```
